# Optimizing a Trainium2 kernel written in Bass

```python
import numpy as np
import jax
import jax.numpy as jnp

def _softmax(x, axis=-1):
    return jax.nn.softmax(x, axis=axis)

def _gelu(x):
    return jax.nn.gelu(x, approximate=True)

def _silu(x):
    return jax.nn.silu(x)

def _sigmoid(x):
    return jax.nn.sigmoid(x)

def _layernorm(x, axis=-1, eps=1e-05):
    m = jnp.mean(x, axis=axis, keepdims=True)
    v = jnp.var(x, axis=axis, keepdims=True)
    return (x - m) / jnp.sqrt(v + eps)

def _scatter_add(tgt, idx, src, axis=0):
    return tgt.at[idx].add(src)

def _segment_sum(src, seg, n):
    return jax.ops.segment_sum(src, seg, n)
kernel_name = 'mk_xattn_ffn_d2_seqx_r8_189a6b'

def setup_inputs(seed: int=0):
    np.random.seed(seed)
    _w = jnp.asarray

    def _rec_inputs():
        import jax
        import jax.numpy as jnp
        _rk = jax.random.key(seed)
        x = -0.0002928 + 1 * jax.random.normal(jax.random.fold_in(_rk, 1), (16, 128, 256), jnp.float32)
        _lenS = 128 - jax.random.randint(jax.random.fold_in(_rk, 7), (16,), 0, max(1, 128 // 4) + 1, jnp.int32)
        _lenS2 = 128 - jax.random.randint(jax.random.fold_in(_rk, 8), (16,), 0, max(1, 128 // 4) + 1, jnp.int32)
        _ctx_512P = jax.random.normal(jax.random.fold_in(_rk, 11), (16, 16, 64), jnp.float32)
        _ctx_512c = jax.random.dirichlet(jax.random.fold_in(_rk, 511), 0.3 * jnp.ones((16,), jnp.float32), (16, 128))
        _ctx_512t = jnp.einsum('bsk,bkd->bsd', _ctx_512c, _ctx_512P)
        _ctx_512t = _ctx_512t * jax.lax.rsqrt(jnp.mean(jnp.square(_ctx_512t)) + 1e-12) * 0.953939
        ctx_512 = 0.000227908 + 0.99994 * (_ctx_512t + 0.3 * jax.random.normal(jax.random.fold_in(_rk, 611), (16, 128, 64), jnp.float32))
        return (x, ctx_512)
    x, ctx_512 = _rec_inputs()

    def _L0_xattn_setup():
        import jax, jax.numpy as jnp
        import numpy as np
        B, S, L = (2, 128, 128)
        DIM_Q, H, K, D_C, D_CQ, R = (256, 16, 128, 64, 192, 64)

        def _rope_tables(seq_len, dim, dtype):
            inv_freq = 1.0 / 10000.0 ** (jnp.arange(0, dim, 2, dtype=dtype) / dim)
            t = jnp.arange(seq_len, dtype=dtype)
            freqs = t[:, None] * inv_freq[None, :]
            sin = jnp.repeat(jnp.sin(freqs), 2, axis=-1)
            cos = jnp.repeat(jnp.cos(freqs), 2, axis=-1)
            return (sin, cos)

        def _rotate_half(x):
            h = x.shape[-1] // 2
            return jnp.concatenate([-x[..., h:], x[..., :h]], axis=-1)
        key = jax.random.key(seed)
        ks = jax.random.split(key, 8)
        s_in = 1.0 / np.sqrt(DIM_Q)
        s_k = 1.0 / np.sqrt(K)
        s_cq = 1.0 / np.sqrt(D_CQ)
        s_c = 1.0 / np.sqrt(D_C)
        return {'hidden_q': jax.random.normal(ks[0], (B, S, DIM_Q), jnp.float32), 'kv_c': jax.random.normal(ks[1], (B, L, D_C), jnp.float32), 'Wq': jax.random.normal(ks[2], (H * K, DIM_Q), jnp.float32) * s_in, 'w_kc_q': jax.random.normal(ks[3], (H, K, D_CQ), jnp.float32) * s_k, 'w_kc_kv': jax.random.normal(ks[4], (H, K, D_C), jnp.float32) * s_k, 'W_qr': jax.random.normal(ks[5], (H, D_CQ, R), jnp.float32) * s_cq / np.sqrt(R), 'W_kr': jax.random.normal(ks[6], (H, D_C, R), jnp.float32) * s_c, 'Wo': jax.random.normal(ks[7], (DIM_Q, H * K), jnp.float32) * s_k}
    _L0_xattn_all = _L0_xattn_setup()
    _L0_xattn_in = {k: v for k, v in _L0_xattn_all.items() if k in ('Wq', 'w_kc_q', 'w_kc_kv', 'W_qr', 'W_kr', 'Wo')}
    del _L0_xattn_all

    def _L0_ffn_setup():
        import jax, jax.numpy as jnp
        import numpy as np
        E = 64
        K = 8
        H = 256
        I = 96
        CAP = 64

        def _moe(hidden_states, gate_w, wg, wu, wd):
            B, S, Hd = hidden_states.shape
            x = hidden_states.reshape(-1, Hd)
            T = x.shape[0]
            logits = x @ gate_w.T
            probs = jax.nn.softmax(logits.astype(jnp.float32), axis=-1)
            w, sel = jax.lax.top_k(probs, K)
            w = w / jnp.sum(w, axis=-1, keepdims=True)
            w = w.astype(x.dtype)
            eid = sel.reshape(-1)
            tok = jnp.repeat(jnp.arange(T), K)
            oh = jax.nn.one_hot(eid, E, dtype=jnp.int32)
            pos = jnp.sum(jnp.cumsum(oh, axis=0) * oh, axis=-1) - 1
            valid = pos < CAP
            slot = jnp.where(valid, pos, CAP)
            xin = jnp.zeros((E, CAP + 1, Hd), x.dtype).at[eid, slot].set(x[tok])
            inp = xin[:, :CAP]
            h = jax.nn.silu(jnp.einsum('ech,ehi->eci', inp, wg)) * jnp.einsum('ech,ehi->eci', inp, wu)
            out = jnp.einsum('eci,eih->ech', h, wd)
            out_pad = jnp.concatenate([out, jnp.zeros((E, 1, Hd), out.dtype)], axis=1)
            g = out_pad[eid, slot] * (w.reshape(-1) * valid.astype(w.dtype))[:, None]
            y = jnp.zeros((T, Hd), x.dtype).at[tok].add(g)
            return y.reshape(B, S, Hd)
        key = jax.random.key(seed)
        k1, k2, k3, k4, k5 = jax.random.split(key, 5)
        hidden_states = jax.random.normal(k1, (1, 256, H), dtype=jnp.float32)
        gate_w = jax.random.normal(k2, (E, H), dtype=jnp.float32) * 0.02
        wg = jax.random.normal(k3, (E, H, I), dtype=jnp.float32) * 0.02
        wu = jax.random.normal(k4, (E, H, I), dtype=jnp.float32) * 0.02
        wd = jax.random.normal(k5, (E, I, H), dtype=jnp.float32) * 0.02
        return {'hidden_states': hidden_states, 'gate_w': gate_w, 'wg': wg, 'wu': wu, 'wd': wd}
    _L0_ffn_all = _L0_ffn_setup()
    _L0_ffn_in = {k: v for k, v in _L0_ffn_all.items() if k in ('gate_w', 'wg', 'wu', 'wd')}
    del _L0_ffn_all

    def _L1_xattn_setup():
        import jax, jax.numpy as jnp
        import numpy as np
        import math
        NUM_Q_HEADS = 32
        NUM_KV_HEADS = 8
        key = jax.random.key(seed)
        k1, k2, k3 = jax.random.split(key, 3)
        B, S, E = (2, 256, 256)
        kv_E = NUM_KV_HEADS * (E // NUM_Q_HEADS)
        q = jax.random.normal(k1, (B, S, E), dtype=jnp.float32)
        k = jax.random.normal(k2, (B, S, kv_E), dtype=jnp.float32)
        v = jax.random.normal(k3, (B, S, kv_E), dtype=jnp.float32)
        return {'q': q, 'k': k, 'v': v}
    _L1_xattn_all = _L1_xattn_setup()
    _L1_xattn_in = {k: v for k, v in _L1_xattn_all.items() if k in ()}
    del _L1_xattn_all

    def _L1_ffn_setup():
        import jax, jax.numpy as jnp
        import numpy as np
        EPS = 1e-05

        def weight_quant(w):
            scale = 1.0 / jnp.clip(jnp.mean(jnp.abs(w)), EPS, None)
            return jnp.clip(jnp.round(w * scale), -1.0, 1.0) / scale

        def act_quant(x):
            scale = 127.0 / jnp.clip(jnp.max(jnp.abs(x), axis=-1, keepdims=True), EPS, None)
            return jnp.clip(jnp.round(x * scale), -128.0, 127.0) / scale

        def bitlinear(x, w):
            return jnp.einsum('bsd,od->bso', act_quant(x), weight_quant(w))
        key = jax.random.key(seed)
        k1, k2, k3, k4 = jax.random.split(key, 4)
        B, S, D = (4, 256, 256)
        I = int(np.ceil(D * np.pi / 64) * 64)
        x = jax.random.normal(k1, (B, S, D), dtype=jnp.float32)
        w_gate = jax.random.normal(k2, (I, D), dtype=jnp.float32) * 0.02
        w_up = jax.random.normal(k3, (I, D), dtype=jnp.float32) * 0.02
        w_down = jax.random.normal(k4, (D, I), dtype=jnp.float32) * 0.02
        return {'x': x, 'w_gate': w_gate, 'w_up': w_up, 'w_down': w_down}
    _L1_ffn_all = _L1_ffn_setup()
    _L1_ffn_in = {k: v for k, v in _L1_ffn_all.items() if k in ('w_gate', 'w_up', 'w_down')}
    del _L1_ffn_all
    return {'x': x, 'ctx_512': ctx_512, 'L0_xattn_Wq': _L0_xattn_in['Wq'], 'L0_xattn_w_kc_q': _L0_xattn_in['w_kc_q'], 'L0_xattn_w_kc_kv': _L0_xattn_in['w_kc_kv'], 'L0_xattn_W_qr': _L0_xattn_in['W_qr'], 'L0_xattn_W_kr': _L0_xattn_in['W_kr'], 'L0_xattn_Wo': _L0_xattn_in['Wo'], 'L0_ffn_gate_w': _L0_ffn_in['gate_w'], 'L0_ffn_wg': _L0_ffn_in['wg'], 'L0_ffn_wu': _L0_ffn_in['wu'], 'L0_ffn_wd': _L0_ffn_in['wd'], 'L1_ffn_w_gate': _L1_ffn_in['w_gate'], 'L1_ffn_w_up': _L1_ffn_in['w_up'], 'L1_ffn_w_down': _L1_ffn_in['w_down']}

def reference(x, ctx_512, L0_xattn_Wq, L0_xattn_w_kc_q, L0_xattn_w_kc_kv, L0_xattn_W_qr, L0_xattn_W_kr, L0_xattn_Wo, L0_ffn_gate_w, L0_ffn_wg, L0_ffn_wu, L0_ffn_wd, L1_ffn_w_gate, L1_ffn_w_up, L1_ffn_w_down):
    import jax
    import jax.numpy as jnp

    def _L0_xattn_ref(hidden_q, kv_c, Wq, w_kc_q, w_kc_kv, W_qr, W_kr, Wo):
        import jax, jax.numpy as jnp
        import numpy as np
        B, S, L = (2, 128, 128)
        DIM_Q, H, K, D_C, D_CQ, R = (256, 16, 128, 64, 192, 64)

        def _rope_tables(seq_len, dim, dtype):
            inv_freq = 1.0 / 10000.0 ** (jnp.arange(0, dim, 2, dtype=dtype) / dim)
            t = jnp.arange(seq_len, dtype=dtype)
            freqs = t[:, None] * inv_freq[None, :]
            sin = jnp.repeat(jnp.sin(freqs), 2, axis=-1)
            cos = jnp.repeat(jnp.cos(freqs), 2, axis=-1)
            return (sin, cos)

        def _rotate_half(x):
            h = x.shape[-1] // 2
            return jnp.concatenate([-x[..., h:], x[..., :h]], axis=-1)
        b, s, _ = hidden_q.shape
        l = kv_c.shape[1]
        q_hk = (hidden_q @ Wq.T).reshape(b, s, H, K)
        q_big = jnp.einsum('bshk,hkq->bshq', q_hk, w_kc_q)
        sin, cos = _rope_tables(l, D_C, kv_c.dtype)
        kv_rope = kv_c * cos[None] + _rotate_half(kv_c) * sin[None]
        q_r = jnp.einsum('bshq,hqr->bhsr', q_big, W_qr)
        k_r = jnp.einsum('bld,hdr->bhlr', kv_rope, W_kr)
        scores = jnp.einsum('bhsr,bhlr->bhsl', q_r, k_r)
        attn = jax.nn.softmax(scores, axis=-1)
        ctx_c = jnp.einsum('bhsl,bld->bhsd', attn, kv_rope)
        ctx_lat = jnp.einsum('bhsd,hkd->bshk', ctx_c, w_kc_kv)
        out = ctx_lat.reshape(b, s, H * K) @ Wo.T
        return out

    def _L0_ffn_ref(hidden_states, gate_w, wg, wu, wd):
        import jax, jax.numpy as jnp
        import numpy as np
        E = 64
        K = 8
        H = 256
        I = 96
        CAP = 64

        def _moe(hidden_states, gate_w, wg, wu, wd):
            B, S, Hd = hidden_states.shape
            x = hidden_states.reshape(-1, Hd)
            T = x.shape[0]
            logits = x @ gate_w.T
            probs = jax.nn.softmax(logits.astype(jnp.float32), axis=-1)
            w, sel = jax.lax.top_k(probs, K)
            w = w / jnp.sum(w, axis=-1, keepdims=True)
            w = w.astype(x.dtype)
            eid = sel.reshape(-1)
            tok = jnp.repeat(jnp.arange(T), K)
            oh = jax.nn.one_hot(eid, E, dtype=jnp.int32)
            pos = jnp.sum(jnp.cumsum(oh, axis=0) * oh, axis=-1) - 1
            valid = pos < CAP
            slot = jnp.where(valid, pos, CAP)
            xin = jnp.zeros((E, CAP + 1, Hd), x.dtype).at[eid, slot].set(x[tok])
            inp = xin[:, :CAP]
            h = jax.nn.silu(jnp.einsum('ech,ehi->eci', inp, wg)) * jnp.einsum('ech,ehi->eci', inp, wu)
            out = jnp.einsum('eci,eih->ech', h, wd)
            out_pad = jnp.concatenate([out, jnp.zeros((E, 1, Hd), out.dtype)], axis=1)
            g = out_pad[eid, slot] * (w.reshape(-1) * valid.astype(w.dtype))[:, None]
            y = jnp.zeros((T, Hd), x.dtype).at[tok].add(g)
            return y.reshape(B, S, Hd)
        return _moe(hidden_states, gate_w, wg, wu, wd)

    def _L1_xattn_ref(q, k, v):
        import jax, jax.numpy as jnp
        import numpy as np
        import math
        NUM_Q_HEADS = 32
        NUM_KV_HEADS = 8
        B, S, E = q.shape
        H, KV = (NUM_Q_HEADS, NUM_KV_HEADS)
        D = E // H
        G = H // KV
        scale = math.sqrt(D)
        qh = q.reshape(B, S, KV, G, D).transpose(0, 2, 3, 1, 4)
        kh = k.reshape(B, S, KV, D).transpose(0, 2, 1, 3)
        vh = v.reshape(B, S, KV, D).transpose(0, 2, 1, 3)
        scores = jnp.einsum('bkgsd,bktd->bkgst', qh, kh) / scale
        weights = jax.nn.softmax(scores, axis=-1)
        out = jnp.einsum('bkgst,bktd->bkgsd', weights, vh)
        return out.transpose(0, 3, 1, 2, 4).reshape(B, S, E)

    def _L1_ffn_ref(x, w_gate, w_up, w_down):
        import jax, jax.numpy as jnp
        import numpy as np
        EPS = 1e-05

        def weight_quant(w):
            scale = 1.0 / jnp.clip(jnp.mean(jnp.abs(w)), EPS, None)
            return jnp.clip(jnp.round(w * scale), -1.0, 1.0) / scale

        def act_quant(x):
            scale = 127.0 / jnp.clip(jnp.max(jnp.abs(x), axis=-1, keepdims=True), EPS, None)
            return jnp.clip(jnp.round(x * scale), -128.0, 127.0) / scale

        def bitlinear(x, w):
            return jnp.einsum('bsd,od->bso', act_quant(x), weight_quant(w))
        gate = jax.nn.silu(bitlinear(x, w_gate))
        up = bitlinear(x, w_up)
        return bitlinear(gate * up, w_down)
    x = x + _L0_xattn_ref(_layernorm(x, axis=-1), ctx_512, L0_xattn_Wq, L0_xattn_w_kc_q, L0_xattn_w_kc_kv, L0_xattn_W_qr, L0_xattn_W_kr, L0_xattn_Wo)
    x = x + _L0_ffn_ref(_layernorm(x, axis=-1), L0_ffn_gate_w, L0_ffn_wg, L0_ffn_wu, L0_ffn_wd)
    x = x + _L1_xattn_ref(_layernorm(x, axis=-1), ctx_512, ctx_512)
    x = x + _L1_ffn_ref(_layernorm(x, axis=-1), L1_ffn_w_gate, L1_ffn_w_up, L1_ffn_w_down)
    return x

_drawn_inputs = setup_inputs


def setup_inputs(seed=0):
    import zlib

    import numpy as np

    out = dict(_drawn_inputs(seed))
    spreads = {}
    factors = {'L0_ffn_gate_w': 8.0,
     'L0_ffn_wg': 8.0,
     'L0_ffn_wu': 8.0,
     'L0_ffn_wd': 8.0,
     'L1_ffn_w_gate': 8.0,
     'L1_ffn_w_up': 8.0,
     'L1_ffn_w_down': 8.0}
    for name, (base, spread) in spreads.items():
        noise = np.random.default_rng([zlib.crc32(name.encode()), seed]).standard_normal(out[name].shape)
        drawn = base * np.exp(spread * noise) if base else spread * noise
        out[name] = jnp.asarray(drawn.astype(out[name].dtype))
    for name, factor in factors.items():
        out[name] = (out[name] * factor).astype(out[name].dtype)
    return out
```

```python
import numpy as np
import concourse.bass as bass
from concourse import mybir
from contextlib import ExitStack

fp32 = mybir.dt.float32
bf16 = mybir.dt.bfloat16
i32 = mybir.dt.int32
ALU = mybir.AluOpType
ACT = mybir.ActivationFunctionType
AX = mybir.AxisListType

B, S, D, DC = 16, 128, 256, 64
H0, K0, CQ, R0 = 16, 128, 192, 64
NP0 = H0 // 2
E, TOPK, FE, CAP = 64, 8, 96, 64
NPE = E // 2
H1, KV, DH = 32, 8, 8
G1 = H1 // KV
F1 = 832
FT = 7
EPS = 1e-5
SCALE1 = DH ** -0.5
MAGIC = 1.5 * 2.0 ** 23
KC = CQ // 2
RING = 8
XW = D + E
C_ID, C_UP, C_ECODE, C_COS, C_SIN, C_I3, C_PAR, C_END = 0, 128, 256, 320, 384, 448, 480, 544


class Chain:

    def __init__(self, eng, sem):
        self.eng, self.sem, self.base, self.n = eng, sem, 0, 0

    def link(self, ins):
        ins.then_inc(self.sem, 1)
        self.n += 1
        self.eng.wait_ge(self.sem, self.base + self.n)

    def enter(self, i, per):
        self.before, self.per = self.base + self.n, per
        self.base, self.n = i * per + self.before, 0

    def leave(self, times):
        assert self.n == self.per, f"a turn of the loop links {self.n}, not {self.per}"
        self.base, self.n = self.before + times * self.per, 0


def build(nc, x, ctx, fold_a, fold_b, gate_t, wgu, wd, w1, w2, consts, out, stage):
    es = ExitStack()
    with es:
        def sb(name, shape, dt=fp32):
            return es.enter_context(nc.sbuf_tensor(name, shape, dt))

        def sem(name):
            return es.enter_context(nc.semaphore(name))

        X = sb("X", [128, B, D])
        CT = sb("CT", [128, B, DC])
        KR = sb("KR", [128, B, DC])
        CO = sb("CO", [128, C_END])
        identf = CO[:, C_ID:C_ID + 128]
        identb = sb("identb", [128, 128], bf16)
        epsneg = sb("epsneg", [128, 1])
        NV = sb("NV", [128, 2 * NP0 * (128 + 128)])
        N = NV[:, 0:2 * NP0 * 128].rearrange("p (c h n) -> p c h n", c=2, h=NP0)
        V = NV[:, 2 * NP0 * 128:].rearrange("p (h n) -> p h n", h=NP0)
        st = sb("st", [128, 2, 6])
        mv = sb("mv", [128, 2, 2])
        veps = sb("veps", [128, 2, 1])
        rstd = sb("rstd", [128, 2, 1])
        xn = sb("xn", [128, 2, D])
        xnT = sb("xnT", [128, 2, 2, 128])
        FA = sb("FA", [128, 2, 1152])
        FB = sb("FB", [128, 2, 768])
        KB = sb("KB", [128, 2, 128])
        A1 = sb("A1", [KC, 2, 2, 128])
        A2 = sb("A2", [128, 2, 2, 64])
        KD = sb("KD", [128, 2, 2, DC])
        VD = sb("VD", [128, 2, DC])
        BD = sb("BD", [128, 2, 2, 128])
        qT = sb("qT", [128, 2, NP0, 128])
        nmx = sb("nmx", [128, 2, H0])
        den = sb("den", [128, 2, H0])
        rden = sb("rden", [128, 2, H0])
        P = sb("P", [128, 2, H0, 128])
        PT = sb("PT", [128, 4, 512])
        cT = sb("cT", [128, 2, 512])

        GT = sb("GT", [128, 2, E])
        upb = sb("upb", [128, 128], bf16)
        onesb = sb("onesb", [128, 128], bf16)
        XR = sb("XR", [128, 2, XW])
        LG = sb("LG", [128, 2, E])
        top = sb("top", [128, 2, 8])
        rest = sb("rest", [128, 2, E])
        sel = sb("sel", [128, 2, E], bf16)
        seen = sb("seen", [128, 2, E], bf16)
        ex = sb("ex", [128, 2, E])
        lsum = sb("lsum", [128, 2, 2])
        ntop = sb("ntop", [128, 2, 1])
        fits = sb("fits", [128, 2, E])
        code = sb("code", [128, 2, E])
        code8 = sb("code8", [128, 2, 8])
        none8 = sb("none8", [128, 2, 8])
        IDX = sb("IDX", [128, B, 8], i32)
        wide = P[:, :, :, :].rearrange("p u h l -> p (u h l)")
        REV = wide[0:E, 0:B * S]
        SELT = wide[0:E, B * S:2 * B * S]
        TL = sb("TL", [E, 2, CAP])
        GI = sb("GI", [128, NPE], i32)
        gidx = sb("gidx", [128, 2, 1], i32)
        XG = sb("XG", [128, 2, XW])
        XGT = sb("XGT", [128, 2, 2, 128])
        WGU = sb("WGU", [128, RING, 2, 2, 2 * FE])
        WD = sb("WD", [FE, RING, 2, D])
        TH = sb("TH", [128, 2, FE])
        HH = sb("HH", [128, 2, FE])
        HT = sb("HT", [FE, 2, 128])
        wslot = sb("wslot", [128, 2, 1])
        OS = sb("OS", [128, 2, D])
        cidx = sb("cidx", [128, 2, 8], i32)
        YG = NV[:, :].rearrange("p (u k d) -> p u k d", u=2, k=TOPK)
        YS = sb("YS", [128, 2, D])
        routed = nc.dram_tensor("routed", (B * S, XW), fp32, kind="Internal").ap()
        moe = nc.dram_tensor("moe", (E * CAP + 1, D), fp32, kind="Internal").ap()

        CB = [sb(f"CB{k}", [128, B, DC], bf16) for k in range(3)]
        CRST = cT[:, :, :].rearrange("p q n -> p (q n)").rearrange("p (b c) -> p b c", b=B)
        KZ = sb("KZ", [128, 2, 4, 2, 6, DH], bf16)
        V1 = sb("V1", [128, 2, KV, 32])
        xq = sb("xq", [128, 2, D])
        Q6 = sb("Q6", [128, G1, KV, 6, DH], bf16)
        QT = sb("QT", [96, 16, 128], bf16)
        KT = sb("KT", [96, KV, 128], bf16)
        nm = sb("nm", [128, H1])
        M3 = sb("M3", [128, 3, H1], bf16)
        MT = sb("MT", [96, 128], bf16)
        I3b = sb("I3b", [96, H1], bf16)
        PE1 = P[:, :, :, :].rearrange("p u h l -> p (u h l)").rearrange("p (k n) -> p k n", k=KV)
        OT = PT[:, 0:2, :]
        RD = sb("RD", [128, 2, G1, 4])
        OA = sb("OA", [128, D])

        ring = WGU[:, :, :, :, :].rearrange("p r e c n -> p (r e c n)")
        W1F = ring[:, 0:4 * F1]
        W2F = ring[:, 4 * F1:4 * F1 + FT * D]
        W1 = FA[:, :, :].rearrange("p u n -> p (u n)")[:, 0:2 * F1].bitcast(bf16).rearrange(
            "p (c w n) -> p c w n", c=2, w=2)
        W2 = FB[:, :, :].rearrange("p u n -> p (u n)")[:, 0:FT * D // 2].bitcast(bf16).rearrange(
            "p (t n) -> p t n", t=FT)
        qflat = qT[:, :, :, :].rearrange("p u h s -> p (u h s)")
        ones = sb("ones", [128, 128])
        magic = sb("magic", [128, 1])
        wsum = sb("wsum", [128, 3, 2])
        wmean = sb("wmean", [128, 3])
        wscale = sb("wscale", [128, 3])
        wdeq = sb("wdeq", [128, 3])
        XF = qflat[:, 2 * F1:2 * F1 + D]
        XQ = sb("XQ", [128, D], bf16)
        XQT = sb("XQT", [128, 2, 128], bf16)
        tok = sb("tok", [128, 8])
        TG = qflat[:, 0:F1]
        HG = qflat[:, F1:2 * F1]
        HQ = sb("HQ", [128, F1], bf16)
        HQT = sb("HQT", [128, FT, 128], bf16)

        PS = es.enter_context(nc.psum_tensor("PS", [128, 8, 512], fp32))
        bank = [PS[:, i, :] for i in range(8)]

        ld_const = sem("ld_const"); ld_x = sem("ld_x"); ld_ctx = sem("ld_ctx")
        ld_fa = [sem("ld_fa0"), sem("ld_fa1")]; ld_fb = [sem("ld_fb0"), sem("ld_fb1")]
        dve_own = sem("dve_own"); act_own = sem("act_own"); pool_own = sem("pool_own")
        held = sem("held")
        rope_done = sem("rope_done"); setup_done = sem("setup_done")
        fold_block = sem("fold_block"); fold_a1 = sem("fold_a1"); fold_a1_out = sem("fold_a1_out")
        fold_a2 = sem("fold_a2"); fold_a2_out = sem("fold_a2_out"); fold_nv = sem("fold_nv")
        fold_n_out = sem("fold_n_out"); fold_v_out = sem("fold_v_out")
        var_ready = sem("var_ready"); rstd_ready = sem("rstd_ready")
        xn_ready = sem("xn_ready"); xnT_psum = sem("xnT_psum"); xnT_ready = sem("xnT_ready")
        kd_ready = sem("kd_ready"); vd_ready = sem("vd_ready"); kdT_psum = sem("kdT_psum"); bd_ready = sem("bd_ready")
        q_psum = sem("q_psum"); qT_ready = sem("qT_ready")
        score_psum = sem("score_psum"); max_ready = sem("max_ready"); exp_ready = sem("exp_ready")
        prob_ready = sem("prob_ready"); pT_psum = sem("pT_psum"); pT_ready = sem("pT_ready")
        ctx_psum = sem("ctx_psum"); ctxT_ready = sem("ctxT_ready"); att_psum = sem("att_psum")
        x1_ready = sem("x1_ready")
        ld_gate = sem("ld_gate"); ld_w = [sem(f"ld_w{r}") for r in range(RING)]
        rt_psum = sem("rt_psum"); rt_ready = sem("rt_ready"); logit_psum = sem("logit_psum")
        top_ready = sem("top_ready"); ex_ready = sem("ex_ready"); sel_ready = sem("sel_ready")
        place_psum = sem("place_psum"); place_read = sem("place_read")
        row_ready = sem("row_ready"); row_stored = [sem("row_stored0"), sem("row_stored1")]
        rev_ready = sem("rev_ready"); list_ready = sem("list_ready"); slot_psum = sem("slot_psum")
        gi_ready = sem("gi_ready"); gathered = [sem("gathered0"), sem("gathered1")]
        xg_psum = sem("xg_psum"); xg_ready = sem("xg_ready"); gu_psum = sem("gu_psum")
        tanh_ready = sem("tanh_ready"); h_ready = sem("h_ready"); hT_psum = sem("hT_psum")
        hT_ready = sem("hT_ready"); down_psum = sem("down_psum"); os_ready = sem("os_ready")
        os_stored = [sem("os_stored0"), sem("os_stored1")]; zero_ready = sem("zero_ready")
        zero_stored = sem("zero_stored"); idx_ready = sem("idx_ready")
        parts_ready = sem("parts_ready"); kz_ready = sem("kz_ready"); v1_ready = sem("v1_ready")
        xq_ready = sem("xq_ready"); xr_ready = sem("xr_ready"); q6_copied = sem("q6_copied")
        ld_w12 = sem("ld_w12"); w2_cleared = sem("w2_cleared"); wsum_ready = sem("wsum_ready")
        wsum_psum = sem("wsum_psum"); wscale_ready = sem("wscale_ready"); wround_ready = sem("wround_ready")
        w_ready = sem("w_ready"); xqf_ready = sem("xqf_ready"); xqT_psum = sem("xqT_psum")
        xqT_ready = sem("xqT_ready"); gu1_psum = sem("gu1_psum"); gate_scale = sem("gate_scale")
        tg_ready = sem("tg_ready"); hq_ready = sem("hq_ready"); hqT_psum = sem("hqT_psum")
        hqT_ready = sem("hqT_ready"); down1_psum = sem("down1_psum"); y_ready = sem("y_ready")
        q6_ready = sem("q6_ready"); qt_psum = sem("qt_psum"); qt_ready = sem("qt_ready")
        kt_psum = sem("kt_psum"); kt_ready = sem("kt_ready"); a_psum = sem("a_psum"); a_read = sem("a_read")
        m3_ready = sem("m3_ready"); mt_psum = sem("mt_psum"); mt_ready = sem("mt_ready")
        b_psum = sem("b_psum"); e_ready = sem("e_ready"); pv_psum = sem("pv_psum"); ot_ready = sem("ot_ready")
        o_psum = sem("o_psum"); x3_ready = sem("x3_ready")
        yg_in = [sem("yg_in0"), sem("yg_in1")]; x2_ready = sem("x2_ready")
        stored = sem("stored")
        block = es.enter_context(nc.Block())

        def heads(row):
            return row.rearrange("p (k g d) -> p g k d", k=KV, g=G1)

        def hold(eng):
            eng.sem_inc(held, 1)

        @block.sync
        def _(sp):
            sp.dma_start(CO[:, :], consts).then_inc(ld_const, 16)
            sp.dma_start(CT[:, :, :], ctx.rearrange("b s c -> s b c")).then_inc(ld_ctx, 16)
            sp.dma_start(GT[:, :, :], gate_t).then_inc(ld_gate, 16)
            for p in range(2):
                sp.dma_start(FA[:, p, :], fold_a[p]).then_inc(ld_fa[p], 16)
                sp.dma_start(FB[:, p, :], fold_b[p]).then_inc(ld_fb[p], 16)
            sp.dma_start(X[:, :, :], x.rearrange("b s d -> s b d")).then_inc(ld_x, 16)
            with sp.Fori(0, NP0 // 2 - 1) as i:
                for u in range(2):
                    sp.wait_ge(fold_nv, i * 2 + u + 1)
                    sp.dma_start(FA[:, u, :], fold_a[i * 2 + u + 2]).then_inc(ld_fa[u], 16)
                    sp.dma_start(FB[:, u, :], fold_b[i * 2 + u + 2]).then_inc(ld_fb[u], 16)
            for r in range(RING):
                sp.dma_start(WGU[:, r, :, :, :], wgu[r]).then_inc(ld_w[r], 16)
                sp.dma_start(WD[:, r, :, :], wd[r]).then_inc(ld_w[r], 16)
            with sp.Fori(0, B // 2) as i:
                for u in range(2):
                    sp.wait_ge(row_ready, i * 2 + u + 1)
                    sp.dma_start(routed[bass.ds((i * 2 + u) * S, S), :], XR[:, u, :]).then_inc(row_stored[u], 16)
            sp.wait_ge(zero_ready, 1)
            sp.dma_start(moe[E * CAP:E * CAP + 1, :], YS[0:1, 0, :]).then_inc(zero_stored, 16)

            def store_slots(i, v):
                j = i * RING + v
                sp.wait_ge(os_ready, j + 1)
                sp.dma_start(moe[bass.ds(j * 128, 128), :], OS[:, v % 2, :]).then_inc(os_stored[v % 2], 16)

            with sp.Fori(0, NPE // RING - 1) as i:
                for v in range(RING):
                    store_slots(i, v)
                    sp.dma_start(WGU[:, v, :, :, :], wgu[(i + 1) * RING + v]).then_inc(ld_w[v], 16)
                    sp.dma_start(WD[:, v, :, :], wd[(i + 1) * RING + v]).then_inc(ld_w[v], 16)
            for v in range(RING):
                store_slots(NPE // RING - 1, v)
            sp.wait_ge(os_ready, NPE)
            sp.wait_ge(w2_cleared, 1)
            sp.dma_start(W1F, w1.rearrange("p c n -> p (c n)")).then_inc(ld_w12, 16)
            for t in range(FT):
                rows = min(128, F1 - t * 128)
                sp.dma_start(W2F[0:rows, t * D:t * D + D], w2[t * 128:t * 128 + rows, :]).then_inc(ld_w12, 16)
            with sp.Fori(0, B) as b:
                sp.wait_ge(y_ready, b + 1)
                sp.dma_start(out[b], X[:, b, :]).then_inc(stored, 16)
            sp.wait_ge(stored, 16 * B)

        @block.tensor
        def _(pe):
            mm = nc.tensor.matmul

            def fold(i, u):
                p = i * 2 + u
                pe.wait_ge(ld_fa[u], i * 16 + 16)
                pe.wait_ge(fold_block, p + 1)
                for c in range(2):
                    last = mm(bank[u][0:KC, c * 128:c * 128 + 128],
                              FB[:, u, 512 + c * KC:512 + c * KC + KC], KB[:, u, :], start=True, stop=True)
                last.then_inc(fold_a1, 1)
                pe.wait_ge(fold_a1_out, p + 1)
                for h in range(2):
                    for c in range(2):
                        last = mm(bank[2 + u][:, h * 64:h * 64 + 64],
                                  FB[0:KC, u, (c * 2 + h) * 128:(c * 2 + h) * 128 + 128],
                                  A1[:, u, c, h * 64:h * 64 + 64], start=(c == 0), stop=(c == 1))
                last.then_inc(fold_a2, 1)
                for h in range(2):
                    mm(bank[6 + u][64 * h:64 * h + 64, 0:D], FA[:, u, 512 + h * 64:512 + h * 64 + 64],
                       FA[:, u, 640 + h * 256:640 + h * 256 + 256], start=True, stop=True)
                pe.wait_ge(fold_a2_out, p + 1)
                for c in range(2):
                    for h in range(2):
                        last = mm(bank[4 + u][:, c * 128 + h * 64:c * 128 + h * 64 + 64],
                                  FA[:, u, h * 256 + c * 128:h * 256 + c * 128 + 128], A2[:, u, h, :],
                                  start=True, stop=True)
                last.then_inc(fold_nv, 1)

            pe.wait_ge(setup_done, 1)
            for u in range(2):
                fold(0, u)
            with pe.Fori(1, NP0 // 2) as i:
                for u in range(2):
                    pe.wait_ge(fold_n_out, i * 2 + u - 1)
                    pe.wait_ge(fold_v_out, i * 2 + u - 1)
                    fold(i, u)

            def query(b, u):
                pe.wait_ge(xn_ready, b + 1)
                for c in range(2):
                    last = nc.tensor.transpose(bank[6][:, c * 128:c * 128 + 128], xn[:, u, c * 128:c * 128 + 128],
                                               identf)
                last.then_inc(xnT_psum, 1)
                pe.wait_ge(kd_ready, b + 1)
                nc.tensor.transpose(bank[7][:, 256:384], KD[:, u, :, :].rearrange("p a d -> p (a d)"),
                                    identf).then_inc(kdT_psum, 1)
                pe.wait_ge(xnT_ready, b + 1)
                for q in range(2):
                    for p in range(4):
                        for c in range(2):
                            last = mm(bank[4 + q][:, p * 128:p * 128 + 128], N[:, c, q * 4 + p, :], xnT[:, u, c, :],
                                      start=(c == 0), stop=(c == 1))
                    last.then_inc(q_psum, 1)

            def scores(b, u):
                pe.wait_ge(qT_ready, b * 2 + 2)
                pe.wait_ge(bd_ready, b + 1)
                for q in range(2):
                    for p in range(4):
                        last = mm(bank[q * 2 + p // 2][:, (p % 2) * 256:(p % 2) * 256 + 256], qT[:, u, q * 4 + p, :],
                                  BD[:, u, :, :].rearrange("p a l -> p (a l)"), start=True, stop=True)
                    last.then_inc(score_psum, 1)

            def attend(b, u):
                for q in range(2):
                    pe.wait_ge(prob_ready, b * 2 + q + 1)
                    for par in range(2):
                        if q == 1:
                            pe.wait_ge(pT_ready, b * 4 + par + 1)
                        for p in range(4):
                            last = nc.tensor.transpose(bank[4 + par][:, p * 128:p * 128 + 128],
                                                       P[:, u, (q * 4 + p) * 2 + par, :], identf)
                        last.then_inc(pT_psum, 1)
                pe.wait_ge(vd_ready, b + 1)
                for q in range(2):
                    if q == 1:
                        pe.wait_ge(ctxT_ready, b * 2 + 1)
                    for par in range(2):
                        pe.wait_ge(pT_ready, b * 4 + q * 2 + par + 1)
                        last = mm(bank[6][64 * par:64 * par + 64, :], VD[:, u, :], PT[:, q * 2 + par, :],
                                  start=True, stop=True)
                    last.then_inc(ctx_psum, 1)
                for q in range(2):
                    pe.wait_ge(ctxT_ready, b * 2 + q + 1)
                    for p in range(4):
                        last = mm(bank[7][:, 0:D], cT[:, q, p * 128:p * 128 + 128], V[:, q * 4 + p, :],
                                  start=(q + p == 0), stop=(q * 4 + p == NP0 - 1))
                last.then_inc(att_psum, 1)

            def body(b, u, nxt, cur, prv, added=True):
                if nxt:
                    if prv and added:
                        pe.wait_ge(x1_ready, b - 1)
                    query(b + 1, 1 - u)
                if prv:
                    if nxt:
                        pe.wait_ge(qT_ready, b * 2 + 4)
                        pe.wait_ge(bd_ready, b + 2)
                    attend(b - 1, 1 - u)
                if nxt:
                    if cur:
                        pe.wait_ge(exp_ready, b * 2 + 2)
                    scores(b + 1, 1 - u)

            pe.wait_ge(fold_n_out, NP0)
            pe.wait_ge(fold_v_out, NP0)
            body(-1, 1, True, False, False)
            body(0, 0, True, True, False)
            body(1, 1, True, True, True, added=False)
            body(2, 0, True, True, True)
            with pe.Fori(1, B // 2 - 1) as i:
                for v in range(2):
                    body(i * 2 + v + 1, 1 - v, True, True, True)
            body(B - 1, 1, False, True, True)
            body(B, 0, False, False, True)

            pe.wait_ge(ld_gate, 16)
            pe.wait_ge(x1_ready, B)

            def route_logits(b, u):
                pe.wait_ge(xn_ready, B + b + 1)
                for c in range(2):
                    last = nc.tensor.transpose(bank[6][:, c * 128:c * 128 + 128], XR[:, u, c * 128:c * 128 + 128],
                                               identf)
                last.then_inc(xnT_psum, 1)
                pe.wait_ge(xnT_ready, B + b + 1)
                for c in range(2):
                    last = mm(bank[u][:, 0:E], xnT[:, u, c, :], GT[:, c, :], start=(c == 0), stop=(c == 1))
                last.then_inc(logit_psum, 1)

            def route_places(b, u, first):
                pe.wait_ge(sel_ready, b + 1)
                mm(bank[2 + u][:, 0:E], upb[:, :], sel[:, u, :], start=True, stop=False)
                mm(bank[2 + u][:, 0:E], onesb[:, :], seen[:, u, :], start=False, stop=True)
                mm(bank[4 + u][0:E, 0:128], sel[:, u, :], identb[:, :], start=True, stop=True).then_inc(place_psum, 1)

            route_logits(0, 0)
            with pe.Fori(0, B // 2 - 1) as i:
                for v in range(2):
                    route_logits(i * 2 + v + 1, 1 - v)
                    route_places(i * 2 + v, v, False)
            route_logits(B - 1, 1)
            route_places(B - 2, 0, False)
            route_places(B - 1, 1, False)

            pe.wait_ge(list_ready, 1)
            for par in range(2):
                last = mm(bank[0][64 * par:64 * par + CAP, 0:NPE], TL[:, 1, :],
                          CO[0:E, C_PAR + par * NPE:C_PAR + par * NPE + NPE], start=True, stop=True)
            last.then_inc(slot_psum, 1)
            pe.wait_ge(gi_ready, 1)

            def expert_rows(i, v):
                j, u = i * RING + v, v % 2
                pe.wait_ge(gathered[u], i * (RING // 2 * 16) + v // 2 * 16 + 16)
                for c in range(2):
                    last = nc.tensor.transpose(bank[u][:, c * 128:c * 128 + 128], XG[:, u, c * 128:c * 128 + 128],
                                               identf)
                last.then_inc(xg_psum, 1)

            def expert_up(i, v):
                j, u = i * RING + v, v % 2
                pe.wait_ge(xg_ready, j + 1)
                pe.wait_ge(ld_w[v], i * 32 + 32)
                for c in range(2):
                    for e in range(2):
                        last = mm(bank[2 + u][64 * e:64 * e + 64, 0:2 * FE], XGT[:, u, c, 64 * e:64 * e + 64],
                                  WGU[:, v, e, c, :], start=(c == 0), stop=(c == 1))
                last.then_inc(gu_psum, 1)

            def expert_turn(i, v):
                j, u = i * RING + v, v % 2
                pe.wait_ge(h_ready, j + 1)
                nc.tensor.transpose(bank[4 + u][0:FE, 0:128], HH[:, u, :], identf).then_inc(hT_psum, 1)

            def expert_down(i, v):
                j, u = i * RING + v, v % 2
                pe.wait_ge(hT_ready, j + 1)
                if not (isinstance(i, int) and j < 2):
                    pe.wait_ge(os_ready, j - 1)
                for e in range(2):
                    last = mm(bank[6 + u][64 * e:64 * e + 64, 0:D], HT[:, u, 64 * e:64 * e + 64], WD[:, v, e, :],
                              start=True, stop=True)
                last.then_inc(down_psum, 1)

            def expert_body(i, v, nxt):
                n = (i, v + 1) if v + 1 < RING else (i + 1, 0)
                if nxt:
                    expert_rows(*n)
                expert_turn(i, v)
                if nxt:
                    expert_up(*n)
                expert_down(i, v)

            expert_rows(0, 0)
            expert_up(0, 0)
            for v in range(RING):
                expert_body(0, v, True)
            with pe.Fori(1, NPE // RING - 1) as i:
                for v in range(RING):
                    expert_body(i, v, True)
            for v in range(RING):
                expert_body(NPE // RING - 1, v, v + 1 < RING)

            def turn_queries(b):
                pe.wait_ge(q6_ready, b + 1)
                pe.wait_ge(q6_copied, b + 1)
                for g in range(G1):
                    for j in range(4):
                        last = nc.tensor.transpose(bank[4 + g // 2].bitcast(bf16)[0:96, (g % 2 * 4 + j) * 128:(g % 2 * 4 + j) * 128 + 128],
                                                   Q6[:, g, 2 * j:2 * j + 2, :, :].rearrange("p k t d -> p (k t d)"),
                                                   identb[:, :])
                    if g % 2:
                        last.then_inc(qt_psum, 1)
                pe.wait_ge(kz_ready, b + 1)
                for kv in range(KV):
                    last = nc.tensor.transpose(bank[6].bitcast(bf16)[0:96, kv * 128:kv * 128 + 128],
                                               KZ[:, kv % 2, kv // 2, :, :, :].rearrange("p k t d -> p (k t d)"),
                                               identb[:, :])
                last.then_inc(kt_psum, 1)

            def rows_scores(b, first):
                pe.wait_ge(qt_ready, b * 2 + 2)
                pe.wait_ge(kt_ready, b + 1)
                if not first:
                    pe.wait_ge(e_ready, b * 8)
                for g in range(G1):
                    if g >= 2:
                        pe.wait_ge(a_read, b * 4 + g - 1)
                    for j in range(4):
                        last = mm(bank[g % 2 * 2 + j // 2][:, j % 2 * 256:j % 2 * 256 + 256], QT[:, g * 4 + j, :],
                                  KT[:, 2 * j:2 * j + 2, :].rearrange("p k t -> p (k t)"), start=True, stop=True)
                    last.then_inc(a_psum, 1)

            def columns_scores(b):
                pe.wait_ge(m3_ready, b + 1)
                nc.tensor.transpose(bank[7].bitcast(bf16)[0:96, 0:128], M3[:, :, :].rearrange("p a h -> p (a h)"),
                                    identb[:, :]).then_inc(mt_psum, 1)
                pe.wait_ge(mt_ready, b + 1)
                qt = QT[:, :, :].rearrange("p (g j) s -> p j g s", g=G1)
                for kv in range(KV):
                    if kv < 4:
                        pe.wait_ge(a_read, b * 4 + 4)
                    else:
                        pe.wait_ge(e_ready, b * 8 + kv - 3)
                    mm(bank[kv % 4], KT[:, kv, :], qt[:, kv // 2, :, :], start=True, stop=False)
                    for g in range(G1):
                        last = mm(bank[kv % 4][:, g * 128:g * 128 + 128],
                                  I3b[:, g * KV + kv:g * KV + kv + 1].to_broadcast([96, 128]), MT[:, :],
                                  start=False, stop=(g == G1 - 1))
                    last.then_inc(b_psum, 1)

            def values(b, u, nxt):
                pe.wait_ge(v1_ready, b + 1)
                if nxt:
                    pe.wait_ge(qt_ready, b * 2 + 4)
                    pe.wait_ge(kt_ready, b + 2)
                for kv in range(KV):
                    pe.wait_ge(e_ready, b * 8 + kv + 1)
                    last = mm(bank[4 + kv // 4][32 * (kv % 4):32 * (kv % 4) + 32, :], V1[:, u, kv, :],
                              PE1[:, kv, :], start=True, stop=True)
                    if kv % 4 == 3:
                        last.then_inc(pv_psum, 1)
                for half in range(2):
                    pe.wait_ge(ot_ready, b * 2 + half + 1)
                    for g in range(G1):
                        last = nc.tensor.transpose(bank[6 + half][:, g * 128:g * 128 + 128],
                                                   OT[:, half, g * 128:g * 128 + 128], identf)
                    last.then_inc(o_psum, 1)

            def tile(b, u, first, nxt):
                rows_scores(b, first)
                columns_scores(b)
                if nxt:
                    turn_queries(b + 1)
                values(b, u, nxt)

            turn_queries(0)
            tile(0, 0, True, True)
            tile(1, 1, False, True)
            with pe.Fori(1, B // 2 - 1) as i:
                for u in range(2):
                    tile(i * 2 + u, u, False, True)
            tile(B - 2, 0, False, True)
            tile(B - 1, 1, False, False)

            pe.wait_ge(wsum_ready, 1)
            pe.wait_ge(x3_ready, B)
            mm(bank[7][:, 0:6], ones[:, :], wsum[:, :, :].rearrange("p w c -> p (w c)"),
               start=True, stop=True).then_inc(wsum_psum, 1)
            pe.wait_ge(w_ready, 1)

            def feed(b, first):
                pe.wait_ge(xqf_ready, b + 1)
                for c in range(2):
                    last = nc.tensor.transpose(bank[6].bitcast(bf16)[:, c * 128:c * 128 + 128],
                                               XQ[:, c * 128:c * 128 + 128], identb[:, :])
                last.then_inc(xqT_psum, 1)
                pe.wait_ge(xqT_ready, b + 1)
                for half in range(4):
                    for c in range(2):
                        last = mm(bank[half][:, 0:F1 // 2], XQT[:, c, :],
                                  W1[:, c, half // 2, half % 2 * (F1 // 2):half % 2 * (F1 // 2) + F1 // 2],
                                  start=(c == 0), stop=(c == 1))
                last.then_inc(gu1_psum, 1)
                pe.wait_ge(hq_ready, b + 1)
                for t in range(FT):
                    rows = min(128, F1 - t * 128)
                    last = nc.tensor.transpose(bank[4].bitcast(bf16)[0:rows, t * 128:t * 128 + 128],
                                               HQ[:, t * 128:t * 128 + rows], identb[:, :])
                last.then_inc(hqT_psum, 1)
                pe.wait_ge(hqT_ready, b + 1)
                for t in range(FT):
                    rows = min(128, F1 - t * 128)
                    last = mm(bank[5][:, 0:D], HQT[0:rows, t, :], W2[0:rows, t, :], start=(t == 0), stop=(t == FT - 1))
                last.then_inc(down1_psum, 1)

            with pe.Fori(0, B) as b:
                feed(b, False)

        @block.vector
        def _(dve):
            ch = Chain(dve, dve_own)
            link = ch.link
            dve.wait_ge(ld_const, 16)
            nc.vector.tensor_copy(identb[:, :], identf)
            nc.vector.memset(KB[:, :, :], 0.0)
            link(nc.vector.memset(BD[:, :, :, :], 0.0))
            nc.vector.memset(epsneg[:, :], -0.5).then_inc(setup_done, 1)
            dve.wait_ge(ld_ctx, 16)
            half = DC // 2
            cos = CO[:, C_COS:C_COS + DC]
            sin = CO[:, C_SIN:C_SIN + DC]

            def fold(i, u):
                p = i * 2 + u
                dve.wait_ge(ld_fb[u], i * 16 + 16)
                for h in range(2):
                    ins = nc.vector.tensor_copy(KB[64 * h:64 * h + 64, u, 64 * h:64 * h + 64],
                                                FB[64 * h:64 * h + 64, u, 704:768])
                ins.then_inc(fold_block, 1)
                dve.wait_ge(fold_a2, p + 1)
                nc.vector.tensor_copy(A2[:, u, :, :].rearrange("p h d -> p (h d)"),
                                      bank[2 + u][:, 0:128]).then_inc(fold_a2_out, 1)
                dve.wait_ge(fold_nv, p + 1)
                nc.vector.tensor_copy(N[:, :, p, :], bank[4 + u][:, 0:256].rearrange("p (c n) -> p c n", c=2)
                                      ).then_inc(fold_n_out, 1)

            for u in range(2):
                fold(0, u)
            with dve.Fori(1, NP0 // 2) as i:
                for u in range(2):
                    dve.wait_ge(fold_a1, i * 2 + u - 1)
                    fold(i, u)

            def ln_stats(b, u):
                nc.vector.bn_stats(st[:, u, :], X[:, b, :])
                return u

            def stats(b, u):
                link(nc.vector.bn_stats(st[:, u, :], X[:, b, :]))
                hold(dve)
                link(nc.vector.bn_aggr(mv[:, u, :], st[:, u, :]))
                nc.vector.tensor_scalar(veps[:, u, :], mv[:, u, 1:2], EPS, None, ALU.add).then_inc(var_ready, 1)

            def normed(b, u):
                dve.wait_ge(rstd_ready, b + 1)
                nc.vector.tensor_scalar(xn[:, u, :], X[:, b, :], mv[:, u, 0:1], rstd[:, u, :],
                                        ALU.subtract, ALU.mult).then_inc(xn_ready, 1)

            def blocks(b, u):
                dve.wait_ge(kdT_psum, b + 1)
                for h in range(2):
                    ins = nc.vector.tensor_copy(BD[64 * h:64 * h + 64, u, h, :],
                                                bank[7][64 * h:64 * h + 64, 256:384])
                ins.then_inc(bd_ready, 1)

            def finish(b, u):
                for g in range(4):
                    dve.wait_ge(pT_psum, b * 4 + g + 1)
                    nc.vector.tensor_copy(PT[:, g, :], bank[4 + g % 2][:, :]).then_inc(pT_ready, 1)
                dve.wait_ge(att_psum, b + 1)
                nc.vector.tensor_tensor(X[:, b, :], X[:, b, :], bank[7][:, 0:D], ALU.add).then_inc(x1_ready, 1)

            def normalise(b, u):
                for q in range(2):
                    dve.wait_ge(exp_ready, b * 2 + q + 1)
                    link(nc.vector.reciprocal(rden[:, u, q * 8:q * 8 + 8], den[:, u, q * 8:q * 8 + 8]))
                    nc.vector.tensor_tensor(P[:, u, q * 8:q * 8 + 8, :], P[:, u, q * 8:q * 8 + 8, :],
                                            rden[:, u, q * 8:q * 8 + 8].unsqueeze(2).to_broadcast([128, 8, 128]),
                                            ALU.mult).then_inc(prob_ready, 1)

            def maxima(b, u):
                for q in range(2):
                    dve.wait_ge(score_psum, b * 2 + q + 1)
                    for k in range(2):
                        ins = nc.vector.tensor_reduce(
                            nmx[:, u, q * 8 + k * 4:q * 8 + k * 4 + 4],
                            bank[q * 2 + k][:, :].rearrange("p (h l) -> p h l", h=4), AX.X, ALU.max, negate=True)
                    ins.then_inc(max_ready, 1)

            def body(b, u, nxt, cur, prv, more):
                if more:
                    stats(b + 2, u)
                if nxt:
                    normed(b + 1, 1 - u)
                    blocks(b + 1, 1 - u)
                if prv:
                    finish(b - 1, 1 - u)
                if cur:
                    normalise(b, u)
                if nxt:
                    maxima(b + 1, 1 - u)

            dve.wait_ge(ld_x, 16)
            stats(0, 0)
            dve.wait_ge(fold_n_out, NP0)
            body(-1, 1, True, False, False, True)
            body(0, 0, True, True, False, True)
            with dve.Fori(0, B // 2 - 2) as i:
                ch.enter(i, 8)
                for v in range(2):
                    body(i * 2 + v + 1, 1 - v, True, True, True, True)
                ch.leave(B // 2 - 2)
            body(B - 3, 1, True, True, True, True)
            body(B - 2, 0, True, True, True, False)
            body(B - 1, 1, False, True, True, False)
            body(B, 0, False, False, True, False)

            dve.wait_ge(x1_ready, B)

            def places(b, u):
                dve.wait_ge(logit_psum, b + 1)
                link(nc.vector.tensor_copy(LG[:, u, :], bank[u][:, 0:E]))
                hold(dve)
                link(nc.vector.max(top[:, u, :], LG[:, u, :]))
                hold(dve)
                nc.vector.match_replace(rest[:, u, :], top[:, u, :], LG[:, u, :], -3.0e38)
                link(nc.vector.tensor_scalar(ntop[:, u, :], top[:, u, 0:1], -1.0, None, ALU.mult))
                nc.vector.tensor_copy(lsum[:, u, 1:2], ntop[:, u, :]).then_inc(top_ready, 1)
                link(nc.vector.tensor_tensor(sel[:, u, :], rest[:, u, :], LG[:, u, :], ALU.not_equal))
                nc.vector.tensor_tensor(seen[:, 1 - u, :], seen[:, u, :], sel[:, u, :], ALU.add).then_inc(sel_ready, 1)
                dve.wait_ge(ex_ready, b + 1)
                link(nc.vector.scalar_tensor_tensor(ex[:, u, :], ex[:, u, :], 1.0, sel[:, u, :], ALU.mult, ALU.mult,
                                                    accum_out=lsum[:, u, 0:1]))
                link(nc.vector.reciprocal(lsum[:, u, 0:1], lsum[:, u, 0:1]))
                nc.vector.tensor_scalar(XR[:, u, D:XW], ex[:, u, :], lsum[:, u, 0:1], None,
                                        ALU.mult).then_inc(row_ready, 1)
                dve.wait_ge(place_psum, b + 1)
                nc.vector.scalar_tensor_tensor(fits[:, u, :], bank[2 + u][:, 0:E], float(CAP), sel[:, u, :],
                                               ALU.is_lt, ALU.mult)
                link(nc.vector.tensor_tensor(code[:, u, :], bank[2 + u][:, 0:E], CO[:, C_ECODE:C_ECODE + E], ALU.add))
                link(nc.vector.tensor_tensor(code[:, u, :], code[:, u, :], fits[:, u, :], ALU.mult))
                hold(dve)
                link(nc.vector.max(code8[:, u, :], code[:, u, :]))
                link(nc.vector.tensor_scalar(none8[:, u, :], code8[:, u, :], 0.0, float(E * CAP + 1),
                                             ALU.is_equal, ALU.mult))
                nc.vector.scalar_tensor_tensor(IDX[:, b, :], code8[:, u, :], -1.0, none8[:, u, :], ALU.add, ALU.add)
                link(nc.vector.tensor_tensor(SELT[:, bass.ds(b * S, S)], bank[4 + u][0:E, 0:128],
                                             REV[:, bass.ds(b * S, S)], ALU.mult))

            def route_normed(b, u, free):
                dve.wait_ge(rstd_ready, B + b + 1)
                if free:
                    dve.wait_ge(row_stored[u], b * 8 - (8 * u))
                nc.vector.tensor_scalar(XR[:, u, 0:D], X[:, b, :], mv[:, u, 0:1], rstd[:, u, :],
                                        ALU.subtract, ALU.mult).then_inc(xn_ready, 1)

            nc.vector.memset(seen[:, :, :], 0.0)
            nc.vector.tensor_copy(upb[:, :], CO[:, C_UP:C_UP + 128])
            nc.vector.memset(onesb[:, :], 1.0)
            link(nc.vector.memset(YS[:, :, :], 0.0))
            nc.vector.memset(none8[:, :, :], 0.0).then_inc(zero_ready, 1)
            stats(0, 0)
            stats(1, 1)
            route_normed(0, 0, False)
            stats(2, 0)
            route_normed(1, 1, False)
            dve.wait_ge(rev_ready, 1)
            places(0, 0)
            stats(3, 1)
            route_normed(2, 0, True)
            places(1, 1)
            with dve.Fori(1, B // 2 - 1) as i:
                ch.enter(i - 1, 26)
                for v in range(2):
                    b = i * 2 + v
                    stats(b + 2, v)
                    route_normed(b + 1, 1 - v, True)
                    places(b, v)
                ch.leave(B // 2 - 2)
            route_normed(B - 1, 1, True)
            places(B - 2, 0)
            places(B - 1, 1)
            for r in range(CAP // 8):
                link(nc.vector.max(TL[:, 0, r * 8:r * 8 + 8], SELT))
                link(nc.vector.match_replace(SELT, TL[:, 0, r * 8:r * 8 + 8], SELT, -1.0))
            nc.vector.tensor_scalar(TL[:, 1, :], TL[:, 0, :], -1.0, float(B * S), ALU.mult,
                                    ALU.add).then_inc(list_ready, 1)
            dve.wait_ge(slot_psum, 1)
            nc.vector.tensor_scalar(GI[:, :], bank[0][:, 0:NPE], float(B * S - 1), None, ALU.min).then_inc(gi_ready, 1)

            def hidden(i, v):
                j, u = i * RING + v, v % 2
                dve.wait_ge(gathered[u], i * (RING // 2 * 16) + v // 2 * 16 + 16)
                for e in range(2):
                    w = XG[64 * e:64 * e + 64, u, bass.ds(j * 2 + D + e, 1)]
                    nc.vector.tensor_scalar(wslot[64 * e:64 * e + 64, u, :], w, 0.5, None, ALU.mult)
                dve.wait_ge(tanh_ready, j + 1)
                link(nc.vector.scalar_tensor_tensor(TH[:, u, :], TH[:, u, :], 1.0, bank[2 + u][:, 0:FE],
                                                    ALU.add, ALU.mult))
                nc.vector.scalar_tensor_tensor(HH[:, u, :], TH[:, u, :], wslot[:, u, :], bank[2 + u][:, FE:2 * FE],
                                               ALU.mult, ALU.mult).then_inc(h_ready, 1)

            def slots_out(i, v):
                j, u = i * RING + v, v % 2
                dve.wait_ge(down_psum, j + 1)
                if not (isinstance(i, int) and j < 2):
                    dve.wait_ge(os_stored[u], i * (RING // 2 * 16) + v // 2 * 16)
                nc.vector.tensor_copy(OS[:, u, :], bank[6 + u][:, 0:D]).then_inc(os_ready, 1)

            def expert_body(i, v, nxt):
                n = (i, v + 1) if v + 1 < RING else (i + 1, 0)
                if nxt:
                    hidden(*n)
                slots_out(i, v)

            hidden(0, 0)
            for v in range(RING):
                expert_body(0, v, True)
            with dve.Fori(1, NPE // RING - 1) as i:
                ch.enter(i - 1, RING)
                for v in range(RING):
                    expert_body(i, v, True)
                ch.leave(NPE // RING - 2)
            for v in range(RING):
                expert_body(NPE // RING - 1, v, v + 1 < RING)

            nc.vector.memset(ones[:, :], 1.0)
            nc.vector.memset(magic[:, :], MAGIC)
            nc.vector.memset(W2F[:, (FT - 1) * D:FT * D], 0.0).then_inc(w2_cleared, 1)

            def combine(b, u, i):
                dve.wait_ge(yg_in[u], i * 128 + 128)
                link(nc.vector.tensor_reduce(YS[:, u, :], YG[:, u, :, :].rearrange("p k d -> p d k"), AX.X, ALU.add))
                ins = nc.vector.tensor_tensor(X[:, b, :], X[:, b, :], YS[:, u, :], ALU.add)
                ins.then_inc(x2_ready, 1)
                dve.wait_ge(x2_ready, b + 1)
                hold(dve)
                stats(b, u)

            def split_queries(b, u):
                dve.wait_ge(rstd_ready, 2 * B + b + 1)
                nc.vector.tensor_scalar(xq[:, 0, :], X[:, b, :], mv[:, u, 0:1], rstd[:, u, :],
                                        ALU.subtract, ALU.mult).then_inc(xq_ready, 1)
                dve.wait_ge(xq_ready, b + 1)
                link(nc.vector.tensor_copy(Q6[:, :, :, 0, :], heads(xq[:, 0, :])))
                nc.vector.tensor_tensor(heads(xq[:, 1, :]), heads(xq[:, 0, :]), Q6[:, :, :, 0, :],
                                        ALU.subtract).then_inc(xr_ready, 1)
                dve.wait_ge(xr_ready, b + 1)
                link(nc.vector.tensor_copy(Q6[:, :, :, 1, :], heads(xq[:, 1, :])))
                nc.vector.tensor_tensor(Q6[:, :, :, 5, :], heads(xq[:, 1, :]), Q6[:, :, :, 1, :],
                                        ALU.subtract).then_inc(q6_ready, 1)

            def maxima1(b):
                for g in range(G1):
                    dve.wait_ge(a_psum, b * 4 + g + 1)
                    ins = nc.vector.tensor_reduce(
                        nm[:, g * KV:g * KV + KV],
                        PS[:, g % 2 * 2:g % 2 * 2 + 2, :].rearrange("p a (k t) -> p (a k) t", t=128),
                        AX.X, ALU.max, negate=True)
                    ins.then_inc(a_read, 1)
                dve.wait_ge(a_read, b * 4 + 4)
                link(nc.vector.tensor_copy(M3[:, 0, :], nm[:, :]))
                link(nc.vector.tensor_tensor(nm[:, :], nm[:, :], M3[:, 0, :], ALU.subtract))
                link(nc.vector.tensor_copy(M3[:, 1, :], nm[:, :]))
                nc.vector.tensor_tensor(M3[:, 2, :], nm[:, :], M3[:, 1, :], ALU.subtract).then_inc(m3_ready, 1)

            def outputs(b, u):
                for half in range(2):
                    dve.wait_ge(o_psum, b * 2 + half + 1)
                    o = bank[6 + half].rearrange("p (g k c) -> p g k c", g=G1, k=4)
                    link(nc.vector.reciprocal(RD[:, half, :, :], o[:, :, :, DH]))
                    ins = nc.vector.tensor_tensor(
                        OA[:, half * 128:half * 128 + 128].rearrange("p (k g d) -> p g k d", k=4, g=G1),
                        o[:, :, :, 0:DH], RD[:, half, :, :].unsqueeze(3).to_broadcast([128, G1, 4, DH]), ALU.mult)
                link(ins)
                nc.vector.tensor_tensor(X[:, b, :], X[:, b, :], OA[:, :], ALU.add).then_inc(x3_ready, 1)

            def tile(b, u, i, nxt):
                maxima1(b)
                if nxt:
                    n = i if u == 0 else i + 1
                    combine(b + 1, 1 - u, n)
                    split_queries(b + 1, 1 - u)
                outputs(b, u)

            combine(0, 0, 0)
            dve.wait_ge(parts_ready, 1)
            split_queries(0, 0)
            with dve.Fori(0, B // 2 - 1) as i:
                ch.enter(i, 22)
                for u in range(2):
                    tile(i * 2 + u, u, i, True)
                ch.leave(B // 2 - 1)
            tile(B - 2, 0, B // 2 - 1, True)
            tile(B - 1, 1, B // 2 - 1, False)

            dve.wait_ge(wsum_psum, 1)
            link(nc.vector.tensor_reduce(wmean[:, :], bank[7][:, 0:6].rearrange("p (w c) -> p w c", c=2), AX.X, ALU.add))
            link(nc.vector.tensor_scalar(wmean[:, :], wmean[:, :], 1.0 / (F1 * D), EPS, ALU.mult, ALU.max))
            link(nc.vector.tensor_scalar(wdeq[:, 0:1], wmean[:, 0:1], 0.5 / 127.0, None, ALU.mult))
            nc.vector.tensor_scalar(wdeq[:, 1:2], wmean[:, 1:2], wdeq[:, 0:1], 1.0 / 127.0, ALU.mult, ALU.mult)
            nc.vector.tensor_scalar(wdeq[:, 2:3], wmean[:, 2:3], 1.0 / 127.0, None, ALU.mult)
            nc.vector.reciprocal(wscale[:, :], wmean[:, :]).then_inc(wscale_ready, 1)
            dve.wait_ge(wround_ready, 1)
            link(nc.vector.tensor_scalar(ring[:, 0:4 * F1 + FT * D], ring[:, 0:4 * F1 + FT * D], MAGIC, 1.0,
                                         ALU.subtract, ALU.min))
            nc.vector.tensor_scalar(W1[:, :, :, :].rearrange("p c w n -> p (c w n)"), W1F, -1.0, None, ALU.max)
            nc.vector.tensor_scalar(W2[:, :, :].rearrange("p t n -> p (t n)"), W2F, -1.0, None,
                                    ALU.max).then_inc(w_ready, 1)

            def feed(b):
                dve.wait_ge(x3_ready, b + 1)
                hold(dve)
                link(nc.vector.bn_stats(st[:, 0, :], X[:, b, :]))
                hold(dve)
                link(nc.vector.bn_aggr(mv[:, 0, :], st[:, 0, :]))
                nc.vector.tensor_scalar(veps[:, 0, :], mv[:, 0, 1:2], EPS, None, ALU.add).then_inc(var_ready, 1)
                dve.wait_ge(rstd_ready, 3 * B + b + 1)
                link(nc.vector.tensor_scalar(XF[:, :], X[:, b, :], mv[:, 0, 0:1], rstd[:, 0, :],
                                             ALU.subtract, ALU.mult))
                link(nc.vector.tensor_reduce(tok[:, 0:1], XF[:, :], AX.X, ALU.max, apply_absolute_value=True))
                link(nc.vector.tensor_scalar(tok[:, 0:1], tok[:, 0:1], EPS, None, ALU.max))
                nc.vector.tensor_scalar(tok[:, 2:3], tok[:, 0:1], wdeq[:, 0:1], None, ALU.mult).then_inc(gate_scale, 1)
                link(nc.vector.reciprocal(tok[:, 1:2], tok[:, 0:1]))
                link(nc.vector.tensor_scalar(tok[:, 1:2], tok[:, 1:2], 127.0, None, ALU.mult))
                link(nc.vector.tensor_scalar(XF[:, :], XF[:, :], tok[:, 1:2], MAGIC, ALU.mult, ALU.add))
                nc.vector.tensor_scalar(XQ[:, :], XF[:, :], MAGIC, None, ALU.subtract).then_inc(xqf_ready, 1)
                link(nc.vector.tensor_scalar(tok[:, 3:4], tok[:, 0:1], tok[:, 0:1], wdeq[:, 1:2], ALU.mult, ALU.mult))
                dve.wait_ge(tg_ready, b + 1)
                tg = TG[:, :].rearrange("p (a n) -> p a n", a=2)
                hg = HG[:, :].rearrange("p (a n) -> p a n", a=2)
                link(nc.vector.scalar_tensor_tensor(tg, tg, 1.0, PS[:, 0:2, 0:F1 // 2], ALU.add, ALU.mult))
                link(nc.vector.tensor_tensor(hg, tg, PS[:, 2:4, 0:F1 // 2], ALU.mult))
                link(nc.vector.tensor_reduce(tok[:, 4:5], HG[:, :], AX.X, ALU.max, apply_absolute_value=True))
                link(nc.vector.tensor_scalar(tok[:, 4:5], tok[:, 4:5], tok[:, 3:4], EPS, ALU.mult, ALU.max))
                nc.vector.tensor_scalar(tok[:, 6:7], tok[:, 4:5], wdeq[:, 2:3], None, ALU.mult)
                link(nc.vector.reciprocal(tok[:, 5:6], tok[:, 4:5]))
                link(nc.vector.tensor_scalar(tok[:, 5:6], tok[:, 5:6], tok[:, 3:4], 127.0, ALU.mult, ALU.mult))
                link(nc.vector.tensor_scalar(HG[:, :], HG[:, :], tok[:, 5:6], MAGIC, ALU.mult, ALU.add))
                nc.vector.tensor_scalar(HQ[:, :], HG[:, :], MAGIC, None, ALU.subtract).then_inc(hq_ready, 1)
                dve.wait_ge(down1_psum, b + 1)
                nc.vector.scalar_tensor_tensor(X[:, b, :], bank[5][:, 0:D], tok[:, 6:7], X[:, b, :],
                                               ALU.mult, ALU.add).then_inc(y_ready, 1)

            with dve.Fori(0, B) as b:
                ch.enter(b, 16)
                feed(b)
                ch.leave(B)

        @block.scalar
        def _(act):
            def fold(i, u):
                p = i * 2 + u
                act.wait_ge(fold_a1, p + 1)
                nc.scalar.copy(A1[:, u, :, :].rearrange("p c n -> p (c n)"),
                               bank[u][0:KC, 0:256]).then_inc(fold_a1_out, 1)
                act.wait_ge(fold_nv, p + 1)
                nc.scalar.copy(V[:, p, :], bank[6 + u][:, 0:D]).then_inc(fold_v_out, 1)

            with act.Fori(0, NP0 // 2) as i:
                for u in range(2):
                    fold(i, u)

            def queries(b, u):
                act.wait_ge(xnT_psum, b + 1)
                nc.scalar.copy(xnT[:, u, :, :].rearrange("p c s -> p (c s)"),
                               bank[6][:, 0:256]).then_inc(xnT_ready, 1)
                for q in range(2):
                    act.wait_ge(q_psum, b * 2 + q + 1)
                    nc.scalar.copy(qT[:, u, q * 4:q * 4 + 4, :].rearrange("p h s -> p (h s)"),
                                   bank[4 + q][:, :]).then_inc(qT_ready, 1)

            def exps(b, u):
                for q in range(2):
                    act.wait_ge(max_ready, b * 2 + q + 1)
                    for h in range(q * 8, q * 8 + 8):
                        ins = nc.scalar.activation(P[:, u, h, :], bank[h // 4][:, (h % 4) * 128:(h % 4) * 128 + 128],
                                                   ACT.Exp, bias=nmx[:, u, h:h + 1], accum_out=den[:, u, h:h + 1])
                    ins.then_inc(exp_ready, 1)

            def contexts(b, u):
                for q in range(2):
                    act.wait_ge(ctx_psum, b * 2 + q + 1)
                    nc.scalar.copy(cT[:, q, :], bank[6][:, :]).then_inc(ctxT_ready, 1)

            def body(b, u, nxt, cur, prv):
                if nxt:
                    queries(b + 1, 1 - u)
                if cur:
                    exps(b, u)
                if prv:
                    contexts(b - 1, 1 - u)

            body(-1, 1, True, False, False)
            body(0, 0, True, True, False)
            with act.Fori(0, B // 2 - 1) as i:
                for v in range(2):
                    body(i * 2 + v + 1, 1 - v, True, True, True)
            body(B - 1, 1, False, True, True)
            body(B, 0, False, False, True)

            def route(b, u):
                act.wait_ge(xnT_psum, B + b + 1)
                nc.scalar.copy(xnT[:, u, :, :].rearrange("p c s -> p (c s)"),
                               bank[6][:, 0:256]).then_inc(xnT_ready, 1)

            def route_exp(b, u):
                act.wait_ge(top_ready, b + 1)
                nc.scalar.activation(ex[:, u, :], LG[:, u, :], ACT.Exp, bias=ntop[:, u, :]).then_inc(ex_ready, 1)

            route(0, 0)
            with act.Fori(0, B // 2 - 1) as i:
                for v in range(2):
                    route(i * 2 + v + 1, 1 - v)
                    route_exp(i * 2 + v, v)
            route(B - 1, 1)
            route_exp(B - 2, 0)
            route_exp(B - 1, 1)

            def rows(j, u):
                act.wait_ge(xg_psum, j + 1)
                nc.scalar.copy(XGT[:, u, :, :].rearrange("p c s -> p (c s)"),
                               bank[u][:, 0:256]).then_inc(xg_ready, 1)

            def tanh(j, u):
                act.wait_ge(gu_psum, j + 1)
                nc.scalar.activation(TH[:, u, :], bank[2 + u][:, 0:FE], ACT.Tanh, scale=0.5).then_inc(tanh_ready, 1)

            def turned(j, u):
                act.wait_ge(hT_psum, j + 1)
                nc.scalar.copy(HT[:, u, :], bank[4 + u][0:FE, 0:128]).then_inc(hT_ready, 1)

            rows(0, 0)
            tanh(0, 0)
            rows(1, 1)
            turned(0, 0)
            tanh(1, 1)
            with act.Fori(0, NPE // 2 - 1) as i:
                for v in range(2):
                    rows(i * 2 + v + 2, v)
                    turned(i * 2 + v + 1, 1 - v)
                    tanh(i * 2 + v + 2, v)
            turned(NPE - 1, 1)

            def copy_queries(b):
                act.wait_ge(xq_ready, b + 1)
                nc.scalar.copy(Q6[:, :, :, 2, :], heads(xq[:, 0, :]))
                nc.scalar.copy(Q6[:, :, :, 4, :], heads(xq[:, 0, :]))
                act.wait_ge(xr_ready, b + 1)
                nc.scalar.copy(Q6[:, :, :, 3, :], heads(xq[:, 1, :])).then_inc(q6_copied, 1)

            def turned_queries(b):
                for q in range(2):
                    act.wait_ge(qt_psum, b * 2 + q + 1)
                    nc.scalar.copy(QT[:, q * 8:q * 8 + 8, :].rearrange("p a s -> p (a s)"),
                                   bank[4 + q].bitcast(bf16)[0:96, :]).then_inc(qt_ready, 1)
                act.wait_ge(kt_psum, b + 1)
                nc.scalar.copy(KT[:, :, :].rearrange("p k t -> p (k t)"),
                               bank[6].bitcast(bf16)[0:96, :]).then_inc(kt_ready, 1)

            def tile(b, nxt):
                act.wait_ge(mt_psum, b + 1)
                nc.scalar.copy(MT[:, :], bank[7].bitcast(bf16)[0:96, 0:128]).then_inc(mt_ready, 1)
                for kv in range(KV):
                    act.wait_ge(b_psum, b * 8 + kv + 1)
                    nc.scalar.activation(PE1[:, kv, :], bank[kv % 4], ACT.Exp, scale=SCALE1).then_inc(e_ready, 1)
                if nxt:
                    copy_queries(b + 1)
                    turned_queries(b + 1)
                for half in range(2):
                    act.wait_ge(pv_psum, b * 2 + half + 1)
                    nc.scalar.copy(OT[:, half, :], bank[4 + half]).then_inc(ot_ready, 1)

            copy_queries(0)
            turned_queries(0)
            with act.Fori(0, B - 1) as b:
                tile(b, True)
            tile(B - 1, False)

            act.wait_ge(ld_w12, 16 + 16 * FT)
            act.wait_ge(w2_cleared, 1)
            for c in range(2):
                for w in range(2):
                    nc.scalar.activation(TG[:, :], W1F[:, (c * 2 + w) * F1:(c * 2 + w) * F1 + F1], ACT.Abs,
                                         accum_out=wsum[:, w, c:c + 1]).then_inc(act_own, 1)
                    act.wait_ge(act_own, c * 2 + w + 1)
            for c in range(2):
                n = (FT * D) // 2
                ins = nc.scalar.activation(P[:, 0, 0:n // 128, :].rearrange("p h l -> p (h l)"),
                                           W2F[:, c * n:c * n + n], ACT.Abs, accum_out=wsum[:, 2, c:c + 1])
                ins.then_inc(act_own, 1)
                act.wait_ge(act_own, 5 + c)
            act.sem_inc(wsum_ready, 1)
            act.wait_ge(wscale_ready, 1)
            for c in range(2):
                for w in range(2):
                    piece = W1F[:, (c * 2 + w) * F1:(c * 2 + w) * F1 + F1]
                    nc.scalar.activation(piece, piece, ACT.Identity, scale=wscale[:, w:w + 1], bias=magic[:, :])
            nc.scalar.activation(W2F, W2F, ACT.Identity, scale=wscale[:, 2:3], bias=magic[:, :]).then_inc(wround_ready, 1)

            with act.Fori(0, B) as b:
                act.wait_ge(xqT_psum, b + 1)
                nc.scalar.copy(XQT[:, :, :].rearrange("p c s -> p (c s)"),
                               bank[6].bitcast(bf16)[:, 0:256]).then_inc(xqT_ready, 1)
                act.wait_ge(gate_scale, b + 1)
                act.wait_ge(gu1_psum, b + 1)
                nc.scalar.activation(TG[:, :].rearrange("p (a n) -> p a n", a=2), PS[:, 0:2, 0:F1 // 2], ACT.Tanh,
                                     scale=tok[:, 2:3]).then_inc(tg_ready, 1)
                act.wait_ge(hqT_psum, b + 1)
                nc.scalar.copy(HQT[:, 0:FT - 1, :].rearrange("p t s -> p (t s)"),
                               bank[4].bitcast(bf16)[:, 0:(FT - 1) * 128])
                nc.scalar.copy(HQT[0:F1 % 128, FT - 1, :],
                               bank[4].bitcast(bf16)[0:F1 % 128, (FT - 1) * 128:FT * 128]).then_inc(hqT_ready, 1)

        @block.gpsimd
        def _(pool):
            ch = Chain(pool, pool_own)
            half = DC // 2
            cos = CO[:, C_COS:C_COS + DC]
            sin = CO[:, C_SIN:C_SIN + DC]
            pool.wait_ge(ld_const, 16)
            pool.wait_ge(ld_ctx, 16)
            tmp = P[:, 0, 0:8, :].rearrange("p h l -> p (h l)").rearrange("p (b c) -> p b c", b=B)
            nc.gpsimd.tensor_tensor(KR[:, :, :], CT[:, :, :], cos.unsqueeze(1).to_broadcast([128, B, DC]), ALU.mult)
            nc.gpsimd.tensor_tensor(tmp[:, :, 0:half], CT[:, :, half:DC],
                                    sin[:, 0:half].unsqueeze(1).to_broadcast([128, B, half]), ALU.mult)
            ch.link(nc.gpsimd.tensor_tensor(tmp[:, :, half:DC], CT[:, :, 0:half],
                                            sin[:, half:DC].unsqueeze(1).to_broadcast([128, B, half]), ALU.mult))
            ch.link(nc.gpsimd.tensor_tensor(KR[:, :, :], KR[:, :, :], tmp, ALU.add))
            pool.wait_ge(setup_done, 1)

            def root(b, u):
                pool.wait_ge(var_ready, b + 1)
                nc.gpsimd.tensor_tensor(rstd[:, u, :], veps[:, u, :], epsneg[:, :], ALU.pow).then_inc(rstd_ready, 1)

            def keys(b, u):
                for k in range(2):
                    ins = nc.gpsimd.tensor_copy(KD[:, u, k, :], KR[:, b, :])
                ins.then_inc(kd_ready, 1)

            def body(b, u, nxt, more, free):
                if more:
                    root(b + 2, u)
                if nxt:
                    if free:
                        pool.wait_ge(kdT_psum, b)
                        hold(pool)
                    keys(b + 1, 1 - u)
                    if free:
                        pool.wait_ge(att_psum, b)
                        hold(pool)
                    nc.gpsimd.tensor_copy(VD[:, 1 - u, :], KR[:, b + 1, :]).then_inc(vd_ready, 1)

            root(0, 0)
            body(-1, 1, True, True, False)
            body(0, 0, True, True, False)
            with pool.Fori(0, B // 2 - 2) as i:
                for v in range(2):
                    body(i * 2 + v + 1, 1 - v, True, True, True)
            body(B - 3, 1, True, True, True)
            body(B - 2, 0, True, False, True)

            pool.wait_ge(x1_ready, B)
            nc.gpsimd.iota(REV, [[-1, B * S]], base=B * S, channel_multiplier=0,
                           allow_small_or_imprecise_dtypes=True).then_inc(rev_ready, 1)
            with pool.Fori(0, B // 2) as i:
                for u in range(2):
                    root(i * 2 + u + B, u)

            pool.wait_ge(gi_ready, 1)
            pool.wait_ge(row_stored[0], B // 2 * 16)
            pool.wait_ge(row_stored[1], B // 2 * 16)

            def gather(i, u, free):
                j = i * 2 + u
                if free:
                    pool.wait_ge(xg_psum, j - 1)
                    pool.wait_ge(h_ready, j - 1)
                    hold(pool)
                ch.link(nc.gpsimd.tensor_copy(gidx[:, u, :], GI[:, bass.ds(j, 1)]))
                hold(pool)
                nc.gpsimd.indirect_dma_start(
                    XG[:, u, :], None, routed, bass.IndirectOffsetOnAxis(ap=gidx[:, u, :], axis=0),
                    bounds_check=B * S - 1, oob_is_err=False).then_inc(gathered[u], 16)

            for u in range(2):
                gather(0, u, False)
            with pool.Fori(1, NPE // 2) as i:
                ch.enter(i - 1, 2)
                for u in range(2):
                    gather(i, u, True)
                ch.leave(NPE // 2 - 1)

            pool.wait_ge(setup_done, 1)
            nc.gpsimd.memset(V1[:, :, :, :], 1.0)
            nc.gpsimd.tensor_copy(I3b[:, :], CO[0:96, C_I3:C_I3 + H1])
            nc.gpsimd.memset(KZ[:, :, :, :, :, :].rearrange("p a j k t d -> p (a j k t d)"), 0.0)
            ch.link(nc.gpsimd.tensor_copy(CB[0][:, :, :], CT[:, :, :]))
            ch.link(nc.gpsimd.tensor_tensor(CRST[:, :, :], CT[:, :, :], CB[0][:, :, :], ALU.subtract))
            ch.link(nc.gpsimd.tensor_copy(CB[1][:, :, :], CRST[:, :, :]))
            ins = nc.gpsimd.tensor_tensor(CB[2][:, :, :], CRST[:, :, :], CB[1][:, :, :], ALU.subtract)
            ins.then_inc(parts_ready, 1)
            pool.wait_ge(parts_ready, 1)

            pool.wait_ge(os_stored[0], NPE // 2 * 16)
            pool.wait_ge(os_stored[1], NPE // 2 * 16)
            pool.wait_ge(zero_stored, 16)

            def collect(i, u, free):
                b = i * 2 + u
                if free:
                    pool.wait_ge(x2_ready, b - 1)
                    hold(pool)
                ch.link(nc.gpsimd.tensor_copy(cidx[:, u, :], IDX[:, b, :]))
                hold(pool)
                for k in range(TOPK):
                    nc.gpsimd.indirect_dma_start(
                        YG[:, u, k, :], None, moe, bass.IndirectOffsetOnAxis(ap=cidx[:, u, k:k + 1], axis=0),
                        bounds_check=E * CAP, oob_is_err=False).then_inc(yg_in[u], 16)

            def keys1(b, u, free):
                root(b + 2 * B, u)
                if free:
                    pool.wait_ge(kt_psum, b)
                    hold(pool)
                for k in range(2):
                    for part, slots in ((0, slice(0, 2)), (0, slice(5, 6)), (1, slice(2, 4)), (2, slice(4, 5))):
                        n = slots.stop - slots.start
                        ins = nc.gpsimd.tensor_copy(
                            KZ[:, k, :, k, slots, :],
                            CB[part][:, b, :].rearrange("p (j k d) -> p j k d", j=4, k=2)[:, :, k, :]
                            .unsqueeze(2).to_broadcast([128, 4, n, DH]))
                ins.then_inc(kz_ready, 1)
                if free:
                    pool.wait_ge(pv_psum, b * 2 - 2)
                    hold(pool)
                nc.gpsimd.tensor_copy(V1[:, u, :, 0:DH],
                                      CT[:, b, :].rearrange("p (k d) -> p k d", k=KV)).then_inc(v1_ready, 1)

            for u in range(2):
                collect(0, u, False)
            keys1(0, 0, False)
            keys1(1, 1, True)
            with pool.Fori(1, B // 2) as i:
                ch.enter(i - 1, 2)
                for u in range(2):
                    collect(i, u, True)
                    keys1(i * 2 + u, u, True)
                ch.leave(B // 2 - 1)

            with pool.Fori(0, B) as b:
                pool.wait_ge(var_ready, 3 * B + b + 1)
                nc.gpsimd.tensor_tensor(rstd[:, 0, :], veps[:, 0, :], epsneg[:, :], ALU.pow).then_inc(rstd_ready, 1)


def _constants():
    c = np.zeros((128, C_END), np.float32)
    r = np.arange(128)
    c[:, C_ID:C_ID + 128] = np.eye(128)
    c[:, C_UP:C_UP + 128] = r[:, None] < r[None, :]
    c[:, C_ECODE:C_ECODE + E] = np.arange(E) * CAP + 1
    inv = (1.0 / np.float32(10000.0) ** (np.arange(0, DC, 2, dtype=np.float32) / DC)).astype(np.float32)
    freqs = (np.arange(S, dtype=np.float32)[:, None] * inv[None, :]).astype(np.float32)
    sin, cos = np.repeat(np.sin(freqs), 2, -1), np.repeat(np.cos(freqs), 2, -1)
    sin[:, :DC // 2] *= -1
    c[:, C_COS:C_COS + DC] = cos
    c[:, C_SIN:C_SIN + DC] = sin
    for k in range(3):
        c[k * 32:k * 32 + 32, C_I3:C_I3 + 32] = np.eye(32)
    for par in range(2):
        for n in range(NPE):
            c[2 * n + par, C_PAR + par * NPE + n] = 1
    return c


def _layout(i):
    wq = i["L0_xattn_Wq"].reshape(NP0, 2, K0, D).transpose(0, 2, 1, 3).reshape(NP0, K0, 2 * D)
    kv = i["L0_xattn_w_kc_kv"].reshape(NP0, 2, K0, DC).transpose(0, 2, 1, 3).reshape(NP0, K0, 2 * DC)
    wo = i["L0_xattn_Wo"].T.reshape(NP0, 2, K0, D).transpose(0, 2, 1, 3).reshape(NP0, K0, 2 * D)
    fold_a = np.concatenate([wq, kv, wo], -1)
    kq = i["L0_xattn_w_kc_q"].transpose(0, 2, 1).reshape(NP0, 2, 2, KC, K0).transpose(0, 3, 2, 1, 4).reshape(NP0, KC, 512)
    qr = i["L0_xattn_W_qr"].transpose(0, 2, 1).reshape(NP0, 128, CQ)
    kr = i["L0_xattn_W_kr"].transpose(0, 2, 1).reshape(NP0, 128, DC)
    fold_b = np.zeros((NP0, 128, 768), np.float32)
    fold_b[:, :KC, :512] = kq
    fold_b[:, :, 512:704] = qr
    fold_b[:, :, 704:] = kr
    gate_t = i["L0_ffn_gate_w"].T.reshape(2, 128, E).transpose(1, 0, 2)
    wg = i["L0_ffn_wg"].reshape(NPE, 2, 2, 128, FE)
    wu = i["L0_ffn_wu"].reshape(NPE, 2, 2, 128, FE)
    wgu = np.concatenate([wg, wu], -1).transpose(0, 3, 1, 2, 4)
    wd = i["L0_ffn_wd"].reshape(NPE, 2, FE, D).transpose(0, 2, 1, 3)
    w1 = np.concatenate([i["L1_ffn_w_gate"].T, i["L1_ffn_w_up"].T], -1).reshape(2, 128, 2 * F1).transpose(1, 0, 2)
    w2 = i["L1_ffn_w_down"].T
    c = np.ascontiguousarray
    return {"x": c(i["x"]), "ctx": c(i["ctx_512"]), "fold_a": c(fold_a), "fold_b": fold_b, "gate_t": c(gate_t),
            "wgu": c(wgu), "wd": c(wd), "w1": c(w1), "w2": c(w2), "consts": _constants()}


def kernel(**inputs):
    import concourse.bacc as bacc
    from concourse.bass_utils import run_bass_kernel_spmd as run

    nc = bacc.Bacc("TRN2", target_bir_lowering=False, num_devices=1)
    arrays = _layout({k: np.asarray(v) for k, v in inputs.items()})
    args = [nc.dram_tensor(n, a.shape, mybir.dt.from_np(a.dtype), kind="ExternalInput").ap()
            for n, a in arrays.items()]
    out = nc.dram_tensor("out", (B, S, D), fp32, kind="ExternalOutput").ap()
    build(nc, *args, out, STAGE)
    return run(nc, [arrays], core_ids=[0]).results[0]["out"]


STAGE = 4
```

```python
import numpy as np
import concourse.bass as bass
from concourse import mybir
from contextlib import ExitStack

fp32 = mybir.dt.float32
bf16 = mybir.dt.bfloat16
i32 = mybir.dt.int32
ALU = mybir.AluOpType
ACT = mybir.ActivationFunctionType
AX = mybir.AxisListType

B, S, D, DC = 16, 128, 256, 64
H0, K0, CQ, R0 = 16, 128, 192, 64
NP0 = H0 // 2
E, TOPK, FE, CAP = 64, 8, 96, 64
NPE = E // 2
H1, KV, DH = 32, 8, 8
G1 = H1 // KV
KR1, KM1 = 12 * DH, 12 * DH + 3 * KV
F1 = 832
FT = 7
EPS = 1e-5
SCALE1 = DH ** -0.5
MAGIC = 1.5 * 2.0 ** 23
KC = CQ // 2
RING = 8
XW = D + E
C_ID, C_UP, C_ECODE, C_COS, C_SIN, C_KV, C_PAR, C_END = 0, 128, 256, 320, 384, 448, 456, 520


class Chain:

    def __init__(self, eng, sem):
        self.eng, self.sem, self.base, self.n = eng, sem, 0, 0

    def link(self, ins):
        ins.then_inc(self.sem, 1)
        self.n += 1
        self.eng.wait_ge(self.sem, self.base + self.n)

    def enter(self, i, per):
        self.before, self.per = self.base + self.n, per
        self.base, self.n = i * per + self.before, 0

    def leave(self, times):
        assert self.n == self.per, f"a turn of the loop links {self.n}, not {self.per}"
        self.base, self.n = self.before + times * self.per, 0


def build(nc, x, ctx, fold_a, fold_b, gate_t, wgu, wd, w1, w2, consts, out, stage):
    es = ExitStack()
    with es:
        def sb(name, shape, dt=fp32):
            return es.enter_context(nc.sbuf_tensor(name, shape, dt))

        def sem(name):
            return es.enter_context(nc.semaphore(name))

        X = sb("X", [128, B, D])
        CT = sb("CT", [128, B, DC])
        KR = sb("KR", [128, B, DC])
        CO = sb("CO", [128, C_END])
        identf = CO[:, C_ID:C_ID + 128]
        identb = sb("identb", [128, 128], bf16)
        epsneg = sb("epsneg", [128, 1])
        NV = sb("NV", [128, 2 * NP0 * (128 + 128)])
        N = NV[:, 0:2 * NP0 * 128].rearrange("p (c h n) -> p c h n", c=2, h=NP0)
        V = NV[:, 2 * NP0 * 128:].rearrange("p (h n) -> p h n", h=NP0)
        st = sb("st", [128, 2, 6])
        mv = sb("mv", [128, 2, 2])
        veps = sb("veps", [128, 2, 1])
        rstd = sb("rstd", [128, 2, 1])
        xn = sb("xn", [128, 2, D])
        xnT = sb("xnT", [128, 2, 2, 128])
        FA = sb("FA", [128, 2, 1152])
        FB = sb("FB", [128, 2, 768])
        KB = sb("KB", [128, 2, 128])
        A1 = sb("A1", [KC, 2, 2, 128])
        A2 = sb("A2", [128, 2, 2, 64])
        KD = sb("KD", [128, 2, 2, DC])
        VD = sb("VD", [128, 2, DC])
        BD = sb("BD", [128, 2, 2, 128])
        qT = sb("qT", [128, 2, NP0, 128])
        nmx = sb("nmx", [128, 2, H0])
        den = sb("den", [128, 2, H0])
        rden = sb("rden", [128, 2, H0])
        P = sb("P", [128, 2, H0, 128])
        PT = sb("PT", [128, 4, 512])
        cT = sb("cT", [128, 2, 512])

        GT = sb("GT", [128, 2, E])
        upb = sb("upb", [128, 128], bf16)
        onesb = sb("onesb", [128, 128], bf16)
        XR = sb("XR", [128, 2, XW])
        LG = sb("LG", [128, 2, E])
        top = sb("top", [128, 2, 8])
        rest = sb("rest", [128, 2, E])
        sel = sb("sel", [128, 2, E], bf16)
        seen = sb("seen", [128, 2, E], bf16)
        ex = sb("ex", [128, 2, E])
        lsum = sb("lsum", [128, 2, 2])
        ntop = sb("ntop", [128, 2, 1])
        fits = sb("fits", [128, 2, E])
        code = sb("code", [128, 2, E])
        code8 = sb("code8", [128, 2, 8])
        none8 = sb("none8", [128, 2, 8])
        IDX = sb("IDX", [128, B, 8], i32)
        wide = P[:, :, :, :].rearrange("p u h l -> p (u h l)")
        REV = wide[0:E, 0:B * S]
        SELT = wide[0:E, B * S:2 * B * S]
        TL = sb("TL", [E, 2, CAP])
        GI = sb("GI", [128, NPE], i32)
        gidx = sb("gidx", [128, 2, 1], i32)
        XG = sb("XG", [128, 2, XW])
        XGT = sb("XGT", [128, 2, 2, 128])
        WGU = sb("WGU", [128, RING, 2, 2, 2 * FE])
        WD = sb("WD", [FE, RING, 2, D])
        TH = sb("TH", [128, 2, FE])
        HH = sb("HH", [128, 2, FE])
        HT = sb("HT", [FE, 2, 128])
        wslot = sb("wslot", [128, 2, 1])
        OS = sb("OS", [128, 2, D])
        cidx = sb("cidx", [128, 2, 8], i32)
        YG = NV[:, :].rearrange("p (u k d) -> p u k d", u=2, k=TOPK)
        YS = sb("YS", [128, 2, D])
        routed = nc.dram_tensor("routed", (B * S, XW), fp32, kind="Internal").ap()
        moe = nc.dram_tensor("moe", (E * CAP + 1, D), fp32, kind="Internal").ap()

        CB = [sb(f"CB{k}", [128, B, DC], bf16) for k in range(3)]
        CRST = cT[:, :, :].rearrange("p q n -> p (q n)").rearrange("p (b c) -> p b c", b=B)
        KZ = sb("KZ", [128, 2, 4, 2, 6, DH], bf16)
        V1 = sb("V1", [128, 2, KV, 32])
        xq = sb("xq", [128, 2, D])
        ring = WGU[:, :, :, :, :].rearrange("p r e c n -> p (r e c n)").bitcast(bf16)
        n6, nq, nk = G1 * KV * 6 * DH, 16 * 128, KV * 128
        Q6 = ring[:, 0:2 * n6].rearrange("p (u g k t d) -> p u g k t d", u=2, g=G1, k=KV, t=6)
        QT = ring[:, 2 * n6:2 * n6 + 2 * nq].rearrange("p (u a s) -> p u a s", u=2, a=16)
        KT = ring[:, 2 * n6 + 2 * nq:2 * n6 + 2 * nq + 2 * nk].rearrange("p (u k t) -> p u k t", u=2, k=KV)
        nm = sb("nm", [128, H1])
        M3 = sb("M3", [128, G1, 3, KV], bf16)
        PE1 = P[:, :, :, :].rearrange("p u h l -> p (u h l)").rearrange("p (k n) -> p k n", k=KV)
        OT = PT[:, 0:2, :]
        RD = sb("RD", [128, 2, G1, 4])
        OA = sb("OA", [128, D])

        W1F = NV[:, 0:4 * F1]
        W2F = qT[:, :, :, :].rearrange("p u h s -> p (u h s)")[:, 0:FT * D]
        W1 = FA[:, :, :].rearrange("p u n -> p (u n)")[:, 0:2 * F1].bitcast(bf16).rearrange(
            "p (c w n) -> p c w n", c=2, w=2)
        W2 = FB[:, :, :].rearrange("p u n -> p (u n)")[:, 0:FT * D // 2].bitcast(bf16).rearrange(
            "p (t n) -> p t n", t=FT)
        scratch = PT[:, :, :].rearrange("p q n -> p (q n)")
        ones = sb("ones", [128, 128])
        magic = sb("magic", [128, 2])
        wsum = sb("wsum", [128, 3, 2])
        wmean = sb("wmean", [128, 3])
        wscale = sb("wscale", [128, 3])
        wdeq = sb("wdeq", [128, 3])
        XF = wide[:, 0:D]
        TG = wide[:, D:D + F1]
        HG = wide[:, D + F1:D + 3 * F1].rearrange("p (u n) -> p u n", u=2)
        XQ = sb("XQ", [128, 2, D], bf16)
        XQT = sb("XQT", [128, 2, 128], bf16)
        xscale = sb("xscale", [128, 2, 4])
        hscale = sb("hscale", [128, 2, 3])
        HQ = sb("HQ", [128, F1], bf16)
        HQT = sb("HQT", [128, FT, 128], bf16)

        PS = es.enter_context(nc.psum_tensor("PS", [128, 8, 512], fp32))
        bank = [PS[:, i, :] for i in range(8)]

        ld_const = sem("ld_const"); ld_x = sem("ld_x"); ld_ctx = sem("ld_ctx")
        ld_fa = [sem("ld_fa0"), sem("ld_fa1")]; ld_fb = [sem("ld_fb0"), sem("ld_fb1")]
        dve_own = sem("dve_own"); act_own = sem("act_own"); pool_own = sem("pool_own")
        held = sem("held")
        rope_done = sem("rope_done"); setup_done = sem("setup_done")
        fold_block = sem("fold_block"); fold_a1 = sem("fold_a1"); fold_a1_out = sem("fold_a1_out")
        fold_a2 = sem("fold_a2"); fold_a2_out = sem("fold_a2_out"); fold_nv = sem("fold_nv")
        fold_n_out = sem("fold_n_out"); fold_v_out = sem("fold_v_out")
        var_ready = sem("var_ready"); rstd_ready = sem("rstd_ready")
        xn_ready = sem("xn_ready"); xnT_psum = sem("xnT_psum"); xnT_ready = sem("xnT_ready")
        kd_ready = sem("kd_ready"); vd_ready = sem("vd_ready"); kdT_psum = sem("kdT_psum"); bd_ready = sem("bd_ready")
        q_psum = sem("q_psum"); qT_ready = sem("qT_ready")
        score_psum = sem("score_psum"); max_ready = sem("max_ready"); exp_ready = sem("exp_ready")
        prob_ready = sem("prob_ready"); pT_psum = sem("pT_psum"); pT_ready = sem("pT_ready")
        ctx_psum = sem("ctx_psum"); ctxT_ready = sem("ctxT_ready"); att_psum = sem("att_psum")
        x1_ready = sem("x1_ready")
        ld_gate = sem("ld_gate"); ld_w = [sem(f"ld_w{r}") for r in range(RING)]
        rt_psum = sem("rt_psum"); rt_ready = sem("rt_ready"); logit_psum = sem("logit_psum")
        top_ready = sem("top_ready"); ex_ready = sem("ex_ready"); sel_ready = sem("sel_ready")
        place_psum = sem("place_psum"); place_read = sem("place_read")
        row_ready = sem("row_ready"); row_stored = [sem("row_stored0"), sem("row_stored1")]
        rev_ready = sem("rev_ready"); list_ready = sem("list_ready"); slot_psum = sem("slot_psum")
        gi_ready = sem("gi_ready"); gathered = [sem("gathered0"), sem("gathered1")]
        xg_psum = sem("xg_psum"); xg_ready = sem("xg_ready"); gu_psum = sem("gu_psum")
        tanh_ready = sem("tanh_ready"); h_ready = sem("h_ready"); hT_psum = sem("hT_psum")
        hT_ready = sem("hT_ready"); down_psum = sem("down_psum"); os_ready = sem("os_ready")
        os_stored = [sem("os_stored0"), sem("os_stored1")]; zero_ready = sem("zero_ready")
        zero_stored = sem("zero_stored"); idx_ready = sem("idx_ready")
        parts_ready = sem("parts_ready"); select_ready = sem("select_ready"); kz_ready = sem("kz_ready"); v1_ready = sem("v1_ready")
        xq_ready = sem("xq_ready"); xr_ready = sem("xr_ready"); q6_copied = sem("q6_copied")
        ld_w12 = sem("ld_w12"); w2_cleared = sem("w2_cleared"); wsum_ready = sem("wsum_ready")
        wsum_psum = sem("wsum_psum"); wscale_ready = sem("wscale_ready"); wround_ready = sem("wround_ready")
        w_ready = sem("w_ready"); xqf_ready = sem("xqf_ready"); xqT_psum = sem("xqT_psum")
        xqT_ready = sem("xqT_ready"); gu1_psum = sem("gu1_psum"); gu1_read = sem("gu1_read")
        tg_ready = sem("tg_ready"); hscale_ready = sem("hscale_ready"); hround_ready = sem("hround_ready"); hq_ready = sem("hq_ready"); hqT_psum = sem("hqT_psum")
        hqT_ready = sem("hqT_ready"); down1_psum = sem("down1_psum"); y_ready = sem("y_ready")
        q6_ready = sem("q6_ready"); qt_psum = sem("qt_psum"); qt_ready = sem("qt_ready")
        kt_psum = sem("kt_psum"); kt_ready = sem("kt_ready"); a_psum = sem("a_psum"); a_read = sem("a_read")
        m3_ready = sem("m3_ready"); mt_psum = sem("mt_psum"); mt_ready = sem("mt_ready")
        b_psum = sem("b_psum"); e_ready = sem("e_ready"); pv_psum = sem("pv_psum"); ot_ready = sem("ot_ready")
        o_psum = sem("o_psum"); x3_ready = sem("x3_ready")
        yg_in = [sem("yg_in0"), sem("yg_in1")]; x2_ready = sem("x2_ready")
        stored = sem("stored")
        block = es.enter_context(nc.Block())

        def heads(row):
            return row.rearrange("p (k g d) -> p g k d", k=KV, g=G1)

        def hold(eng):
            eng.sem_inc(held, 1)

        def since(eng, signal, n):
            if not (isinstance(n, int) and n <= 0):
                eng.wait_ge(signal, n)

        def turn_has(b, *ahead):
            return [not isinstance(b, int) or 0 <= b + n < B for n in ahead]

        @block.sync
        def _(sp):
            sp.dma_start(CO[:, :], consts).then_inc(ld_const, 16)
            sp.dma_start(CT[:, :, :], ctx.rearrange("b s c -> s b c")).then_inc(ld_ctx, 16)
            sp.dma_start(GT[:, :, :], gate_t).then_inc(ld_gate, 16)
            for p in range(2):
                sp.dma_start(FA[:, p, :], fold_a[p]).then_inc(ld_fa[p], 16)
                sp.dma_start(FB[:, p, :], fold_b[p]).then_inc(ld_fb[p], 16)
            sp.dma_start(X[:, :, :], x.rearrange("b s d -> s b d")).then_inc(ld_x, 16)
            with sp.Fori(0, NP0 // 2 - 1) as i:
                for u in range(2):
                    sp.wait_ge(fold_nv, i * 2 + u + 1)
                    sp.dma_start(FA[:, u, :], fold_a[i * 2 + u + 2]).then_inc(ld_fa[u], 16)
                    sp.dma_start(FB[:, u, :], fold_b[i * 2 + u + 2]).then_inc(ld_fb[u], 16)
            for r in range(RING):
                sp.dma_start(WGU[:, r, :, :, :], wgu[r]).then_inc(ld_w[r], 16)
                sp.dma_start(WD[:, r, :, :], wd[r]).then_inc(ld_w[r], 16)
            sp.wait_ge(x1_ready, B)
            sp.wait_ge(w2_cleared, 1)
            sp.dma_start(W1F, w1.rearrange("p c n -> p (c n)")).then_inc(ld_w12, 16)
            for t in range(FT):
                rows = min(128, F1 - t * 128)
                sp.dma_start(W2F[0:rows, t * D:t * D + D], w2[t * 128:t * 128 + rows, :]).then_inc(ld_w12, 16)
            with sp.Fori(0, B // 2) as i:
                for u in range(2):
                    sp.wait_ge(row_ready, i * 2 + u + 1)
                    sp.dma_start(routed[bass.ds((i * 2 + u) * S, S), :], XR[:, u, :]).then_inc(row_stored[u], 16)
            sp.wait_ge(zero_ready, 1)
            sp.dma_start(moe[E * CAP:E * CAP + 1, :], YS[0:1, 0, :]).then_inc(zero_stored, 16)

            def store_slots(i, v):
                j = i * RING + v
                sp.wait_ge(os_ready, j + 1)
                sp.dma_start(moe[bass.ds(j * 128, 128), :], OS[:, v % 2, :]).then_inc(os_stored[v % 2], 16)

            with sp.Fori(0, NPE // RING - 1) as i:
                for v in range(RING):
                    store_slots(i, v)
                    sp.dma_start(WGU[:, v, :, :, :], wgu[(i + 1) * RING + v]).then_inc(ld_w[v], 16)
                    sp.dma_start(WD[:, v, :, :], wd[(i + 1) * RING + v]).then_inc(ld_w[v], 16)
            for v in range(RING):
                store_slots(NPE // RING - 1, v)
            with sp.Fori(0, B) as b:
                sp.wait_ge(y_ready, b + 1)
                sp.dma_start(out[b], X[:, b, :]).then_inc(stored, 16)
            sp.wait_ge(stored, 16 * B)

        @block.tensor
        def _(pe):
            mm = nc.tensor.matmul

            def fold(i, u):
                p = i * 2 + u
                pe.wait_ge(ld_fa[u], i * 16 + 16)
                pe.wait_ge(fold_block, p + 1)
                for c in range(2):
                    last = mm(bank[u][0:KC, c * 128:c * 128 + 128],
                              FB[:, u, 512 + c * KC:512 + c * KC + KC], KB[:, u, :], start=True, stop=True)
                last.then_inc(fold_a1, 1)
                pe.wait_ge(fold_a1_out, p + 1)
                for h in range(2):
                    for c in range(2):
                        last = mm(bank[2 + u][:, h * 64:h * 64 + 64],
                                  FB[0:KC, u, (c * 2 + h) * 128:(c * 2 + h) * 128 + 128],
                                  A1[:, u, c, h * 64:h * 64 + 64], start=(c == 0), stop=(c == 1))
                last.then_inc(fold_a2, 1)
                for h in range(2):
                    mm(bank[6 + u][64 * h:64 * h + 64, 0:D], FA[:, u, 512 + h * 64:512 + h * 64 + 64],
                       FA[:, u, 640 + h * 256:640 + h * 256 + 256], start=True, stop=True)
                pe.wait_ge(fold_a2_out, p + 1)
                for c in range(2):
                    for h in range(2):
                        last = mm(bank[4 + u][:, c * 128 + h * 64:c * 128 + h * 64 + 64],
                                  FA[:, u, h * 256 + c * 128:h * 256 + c * 128 + 128], A2[:, u, h, :],
                                  start=True, stop=True)
                last.then_inc(fold_nv, 1)

            pe.wait_ge(setup_done, 1)
            for u in range(2):
                fold(0, u)
            with pe.Fori(1, NP0 // 2) as i:
                for u in range(2):
                    pe.wait_ge(fold_n_out, i * 2 + u - 1)
                    pe.wait_ge(fold_v_out, i * 2 + u - 1)
                    fold(i, u)

            def turn_rows(b, u):
                pe.wait_ge(kd_ready, b + 1)
                nc.tensor.transpose(bank[7][:, 256:384], KD[:, u, :, :].rearrange("p a d -> p (a d)"),
                                    identf).then_inc(kdT_psum, 1)
                pe.wait_ge(xn_ready, b + 1)
                for c in range(2):
                    last = nc.tensor.transpose(bank[7][:, c * 128:c * 128 + 128], xn[:, u, c * 128:c * 128 + 128],
                                               identf)
                last.then_inc(xnT_psum, 1)

            def queries(b, u):
                pe.wait_ge(xnT_ready, b + 1)
                for q in range(2):
                    for p in range(4):
                        for c in range(2):
                            last = mm(bank[4 + q][:, p * 128:p * 128 + 128], N[:, c, q * 4 + p, :], xnT[:, u, c, :],
                                      start=(c == 0), stop=(c == 1))
                    last.then_inc(q_psum, 1)

            def scores(b, u, q):
                pe.wait_ge(qT_ready, b * 2 + q + 1)
                pe.wait_ge(bd_ready, b + 1)
                since(pe, exp_ready, b * 2 + q - 1)
                for p in range(4):
                    last = mm(bank[q * 2 + p // 2][:, (p % 2) * 256:(p % 2) * 256 + 256], qT[:, u, q * 4 + p, :],
                              BD[:, u, :, :].rearrange("p a l -> p (a l)"), start=True, stop=True)
                last.then_inc(score_psum, 1)

            def turn_probs(b, u, asked):
                for q in range(2):
                    pe.wait_ge(prob_ready, b * 2 + q + 1)
                    for par in range(2):
                        if q == 1:
                            pe.wait_ge(pT_ready, b * 4 + par + 1)
                        elif asked:
                            pe.wait_ge(qT_ready, b * 2 + par + 5)
                        for p in range(4):
                            last = nc.tensor.transpose(bank[4 + par][:, p * 128:p * 128 + 128],
                                                       P[:, u, (q * 4 + p) * 2 + par, :], identf)
                        last.then_inc(pT_psum, 1)

            def contexts(b, u):
                pe.wait_ge(vd_ready, b + 1)
                for q in range(2):
                    pe.wait_ge(pT_ready, b * 4 + q + 3)
                    for par in range(2):
                        last = mm(bank[4 + q][64 * par:64 * par + 64, :], VD[:, u, :], PT[:, q * 2 + par, :],
                                  start=True, stop=True)
                    last.then_inc(ctx_psum, 1)

            def project(b):
                since(pe, x1_ready, b)
                for q in range(2):
                    pe.wait_ge(ctxT_ready, b * 2 + q + 1)
                    for p in range(4):
                        last = mm(bank[6][:, 0:D], cT[:, q, p * 128:p * 128 + 128], V[:, q * 4 + p, :],
                                  start=(q + p == 0), stop=(q * 4 + p == NP0 - 1))
                last.then_inc(att_psum, 1)

            def attend(b, u):
                ask, back, rows = turn_has(b, 1, -1, 2)
                if ask:
                    queries(b + 1, 1 - u)
                if back:
                    turn_probs(b - 1, 1 - u, ask)
                if ask:
                    scores(b + 1, 1 - u, 0)
                if back:
                    contexts(b - 1, 1 - u)
                if ask:
                    scores(b + 1, 1 - u, 1)
                if rows:
                    turn_rows(b + 2, u)
                if back:
                    project(b - 1)

            pe.wait_ge(fold_n_out, NP0)
            pe.wait_ge(fold_v_out, NP0)
            for b in range(-2, 2):
                attend(b, b % 2)
            with pe.Fori(1, B // 2 - 1) as i:
                for u in range(2):
                    attend(i * 2 + u, u)
            for b in range(B - 2, B + 1):
                attend(b, b % 2)

            pe.wait_ge(ld_gate, 16)
            pe.wait_ge(x1_ready, B)

            def route_logits(b, u):
                pe.wait_ge(xn_ready, B + b + 1)
                for c in range(2):
                    last = nc.tensor.transpose(bank[6][:, c * 128:c * 128 + 128], XR[:, u, c * 128:c * 128 + 128],
                                               identf)
                last.then_inc(xnT_psum, 1)
                pe.wait_ge(xnT_ready, B + b + 1)
                for c in range(2):
                    last = mm(bank[u][:, 0:E], xnT[:, u, c, :], GT[:, c, :], start=(c == 0), stop=(c == 1))
                last.then_inc(logit_psum, 1)

            def route_places(b, u, first):
                pe.wait_ge(sel_ready, b + 1)
                mm(bank[2 + u][:, 0:E], upb[:, :], sel[:, u, :], start=True, stop=False)
                mm(bank[2 + u][:, 0:E], onesb[:, :], seen[:, u, :], start=False, stop=True)
                mm(bank[4 + u][0:E, 0:128], sel[:, u, :], identb[:, :], start=True, stop=True).then_inc(place_psum, 1)

            route_logits(0, 0)
            with pe.Fori(0, B // 2 - 1) as i:
                for v in range(2):
                    route_logits(i * 2 + v + 1, 1 - v)
                    route_places(i * 2 + v, v, False)
            route_logits(B - 1, 1)
            route_places(B - 2, 0, False)
            route_places(B - 1, 1, False)

            pe.wait_ge(wsum_ready, 1)
            mm(bank[7][:, 0:6], ones[:, :], wsum[:, :, :].rearrange("p w c -> p (w c)"),
               start=True, stop=True).then_inc(wsum_psum, 1)

            pe.wait_ge(list_ready, 1)
            for par in range(2):
                last = mm(bank[0][64 * par:64 * par + CAP, 0:NPE], TL[:, 1, :],
                          CO[0:E, C_PAR + par * NPE:C_PAR + par * NPE + NPE], start=True, stop=True)
            last.then_inc(slot_psum, 1)
            pe.wait_ge(gi_ready, 1)

            def expert_rows(i, v):
                j, u = i * RING + v, v % 2
                pe.wait_ge(gathered[u], i * (RING // 2 * 16) + v // 2 * 16 + 16)
                for c in range(2):
                    last = nc.tensor.transpose(bank[u][:, c * 128:c * 128 + 128], XG[:, u, c * 128:c * 128 + 128],
                                               identf)
                last.then_inc(xg_psum, 1)

            def expert_up(i, v):
                j, u = i * RING + v, v % 2
                pe.wait_ge(xg_ready, j + 1)
                pe.wait_ge(ld_w[v], i * 32 + 32)
                for c in range(2):
                    for e in range(2):
                        last = mm(bank[2 + u][64 * e:64 * e + 64, 0:2 * FE], XGT[:, u, c, 64 * e:64 * e + 64],
                                  WGU[:, v, e, c, :], start=(c == 0), stop=(c == 1))
                last.then_inc(gu_psum, 1)

            def expert_turn(i, v):
                j, u = i * RING + v, v % 2
                pe.wait_ge(h_ready, j + 1)
                nc.tensor.transpose(bank[4 + u][0:FE, 0:128], HH[:, u, :], identf).then_inc(hT_psum, 1)

            def expert_down(i, v):
                j, u = i * RING + v, v % 2
                pe.wait_ge(hT_ready, j + 1)
                if not (isinstance(i, int) and j < 2):
                    pe.wait_ge(os_ready, j - 1)
                elif j == 1:
                    pe.wait_ge(wscale_ready, 1)
                for e in range(2):
                    last = mm(bank[6 + u][64 * e:64 * e + 64, 0:D], HT[:, u, 64 * e:64 * e + 64], WD[:, v, e, :],
                              start=True, stop=True)
                last.then_inc(down_psum, 1)

            def expert_body(i, v, nxt):
                n = (i, v + 1) if v + 1 < RING else (i + 1, 0)
                if nxt:
                    expert_rows(*n)
                expert_turn(i, v)
                if nxt:
                    expert_up(*n)
                expert_down(i, v)

            expert_rows(0, 0)
            expert_up(0, 0)
            for v in range(RING):
                expert_body(0, v, True)
            with pe.Fori(1, NPE // RING - 1) as i:
                for v in range(RING):
                    expert_body(i, v, True)
            for v in range(RING):
                expert_body(NPE // RING - 1, v, v + 1 < RING)

            def turn(b, u):
                pe.wait_ge(q6_ready, b + 1)
                pe.wait_ge(q6_copied, b + 1)
                since(pe, x3_ready, b - 2)
                for g in range(G1):
                    for j in range(4):
                        at = (g % 2 * 4 + j) * 128
                        last = nc.tensor.transpose(bank[6 + g // 2].bitcast(bf16)[0:KR1, at:at + 128],
                                                   Q6[:, u, g, 2 * j:2 * j + 2, :, :].rearrange("p k t d -> p (k t d)"),
                                                   identb[:, :])
                    if g % 2:
                        last.then_inc(qt_psum, 1)
                pe.wait_ge(kz_ready, b + 1)
                since(pe, a_read, b * 4 - 1)
                for kv in range(KV):
                    last = nc.tensor.transpose(bank[0].bitcast(bf16)[0:KR1, kv * 128:kv * 128 + 128],
                                               KZ[:, kv % 2, kv // 2, :, :, :].rearrange("p k t d -> p (k t d)"),
                                               identb[:, :])
                last.then_inc(kt_psum, 1)

            def row_scores(b, u, g):
                if g == 0:
                    pe.wait_ge(qt_ready, b * 2 + 2)
                    pe.wait_ge(kt_ready, b + 1)
                    since(pe, mt_ready, b)
                since(pe, a_read, b * 4 + g - 1)
                for j in range(4):
                    last = mm(bank[g % 2 * 2 + j // 2][:, j % 2 * 256:j % 2 * 256 + 256], QT[0:KR1, u, g * 4 + j, :],
                              KT[0:KR1, u, 2 * j:2 * j + 2, :].rearrange("p k t -> p (k t)"), start=True, stop=True)
                last.then_inc(a_psum, 1)

            def turn_maxima(b):
                pe.wait_ge(m3_ready, b + 1)
                for g in range(G1):
                    last = nc.tensor.transpose(bank[1].bitcast(bf16)[0:3 * KV, g * 128:g * 128 + 128],
                                               M3[:, g, :, :].rearrange("p a k -> p (a k)"), identb[:, :])
                last.then_inc(mt_psum, 1)

            def column_scores(b, u, kv):
                if kv == 0:
                    pe.wait_ge(mt_ready, b + 1)
                since(pe, e_ready, b * 8 + kv - 1)
                mm(bank[4 + kv % 2], KT[0:KM1, u, kv, :],
                   QT[0:KM1, u, :, :].rearrange("p (g j) s -> p j g s", g=G1)[:, kv // 2, :, :],
                   start=True, stop=True).then_inc(b_psum, 1)

            def values(b, u, half, turned):
                if half == 0:
                    pe.wait_ge(v1_ready, b + 1)
                if turned:
                    pe.wait_ge(qt_ready, b * 2 + half + 5)
                else:
                    pe.wait_ge(x3_ready, b)
                for kv in range(4 * half, 4 * half + 4):
                    pe.wait_ge(e_ready, b * 8 + kv + 1)
                    last = mm(bank[6 + half][32 * (kv % 4):32 * (kv % 4) + 32, :], V1[:, u, kv, :],
                              PE1[:, kv, :], start=True, stop=True)
                last.then_inc(pv_psum, 1)

            def turn_back(b, half):
                pe.wait_ge(ot_ready, b * 2 + half + 1)
                for g in range(G1):
                    last = nc.tensor.transpose(bank[6 + half][:, g * 128:g * 128 + 128],
                                               OT[:, half, g * 128:g * 128 + 128], identf)
                last.then_inc(o_psum, 1)

            def attend1(b, u):
                rows, cols, back, new = turn_has(b, 1, 0, -1, 2)
                for g in range(G1):
                    if rows:
                        row_scores(b + 1, 1 - u, g)
                    if back and g in (1, 2):
                        turn_back(b - 1, g - 1)
                    if cols:
                        column_scores(b, u, 2 * g)
                        column_scores(b, u, 2 * g + 1)
                if new:
                    turn(b + 2, u)
                if rows:
                    turn_maxima(b + 1)
                if cols:
                    for half in range(2):
                        values(b, u, half, new)

            for b in range(-2, 4):
                attend1(b, b % 2)
            with pe.Fori(2, B // 2 - 2) as i:
                for u in range(2):
                    attend1(i * 2 + u, u)
            for b in range(B - 4, B + 1):
                attend1(b, b % 2)

            pe.wait_ge(w_ready, 1)
            pe.wait_ge(x3_ready, B)

            def turn_rows(b, u):
                pe.wait_ge(xqf_ready, b + 1)
                for c in range(2):
                    last = nc.tensor.transpose(bank[6].bitcast(bf16)[:, c * 128:c * 128 + 128],
                                               XQ[:, u, c * 128:c * 128 + 128], identb[:, :])
                last.then_inc(xqT_psum, 1)

            def gate_up(b, free):
                pe.wait_ge(xqT_ready, b + 1)
                if free:
                    pe.wait_ge(gu1_read, b)
                for half in range(4):
                    for c in range(2):
                        last = mm(bank[half][:, 0:F1 // 2], XQT[:, c, :],
                                  W1[:, c, half // 2, half % 2 * (F1 // 2):half % 2 * (F1 // 2) + F1 // 2],
                                  start=(c == 0), stop=(c == 1))
                last.then_inc(gu1_psum, 1)

            def turn_hidden(b):
                pe.wait_ge(hq_ready, b + 1)
                for t in range(FT):
                    rows = min(128, F1 - t * 128)
                    last = nc.tensor.transpose(bank[4].bitcast(bf16)[0:rows, t * 128:t * 128 + 128],
                                               HQ[:, t * 128:t * 128 + rows], identb[:, :])
                last.then_inc(hqT_psum, 1)

            def down(b, u):
                pe.wait_ge(hqT_ready, b + 1)
                for t in range(FT):
                    rows = min(128, F1 - t * 128)
                    last = mm(bank[5 + 2 * u][:, 0:D], HQT[0:rows, t, :], W2[0:rows, t, :],
                              start=(t == 0), stop=(t == FT - 1))
                last.then_inc(down1_psum, 1)

            def feed(b, u, nxt=True, cur=True, prv=True, free=True):
                if nxt:
                    turn_rows(b + 1, 1 - u)
                if prv:
                    down(b - 1, 1 - u)
                if nxt:
                    gate_up(b + 1, free)
                if cur:
                    turn_hidden(b)

            feed(-1, 1, cur=False, prv=False, free=False)
            feed(0, 0, prv=False)
            with pe.Fori(0, B // 2 - 1) as i:
                for v in range(2):
                    feed(i * 2 + v + 1, 1 - v)
            feed(B - 1, 1, nxt=False)
            feed(B, 0, nxt=False, cur=False)

        @block.vector
        def _(dve):
            ch = Chain(dve, dve_own)
            link = ch.link
            dve.wait_ge(ld_const, 16)
            nc.vector.tensor_copy(identb[:, :], identf)
            nc.vector.memset(KB[:, :, :], 0.0)
            link(nc.vector.memset(BD[:, :, :, :], 0.0))
            nc.vector.memset(epsneg[:, :], -0.5).then_inc(setup_done, 1)
            dve.wait_ge(ld_ctx, 16)
            half = DC // 2
            cos = CO[:, C_COS:C_COS + DC]
            sin = CO[:, C_SIN:C_SIN + DC]

            def fold(i, u):
                p = i * 2 + u
                dve.wait_ge(ld_fb[u], i * 16 + 16)
                for h in range(2):
                    ins = nc.vector.tensor_copy(KB[64 * h:64 * h + 64, u, 64 * h:64 * h + 64],
                                                FB[64 * h:64 * h + 64, u, 704:768])
                ins.then_inc(fold_block, 1)
                dve.wait_ge(fold_a2, p + 1)
                nc.vector.tensor_copy(A2[:, u, :, :].rearrange("p h d -> p (h d)"),
                                      bank[2 + u][:, 0:128]).then_inc(fold_a2_out, 1)
                dve.wait_ge(fold_nv, p + 1)
                nc.vector.tensor_copy(N[:, :, p, :], bank[4 + u][:, 0:256].rearrange("p (c n) -> p c n", c=2)
                                      ).then_inc(fold_n_out, 1)

            for u in range(2):
                fold(0, u)
            with dve.Fori(1, NP0 // 2) as i:
                for u in range(2):
                    dve.wait_ge(fold_a1, i * 2 + u - 1)
                    fold(i, u)

            def ln_stats(b, u):
                nc.vector.bn_stats(st[:, u, :], X[:, b, :])
                return u

            def stats(b, u):
                link(nc.vector.bn_stats(st[:, u, :], X[:, b, :]))
                hold(dve)
                link(nc.vector.bn_aggr(mv[:, u, :], st[:, u, :]))
                nc.vector.tensor_scalar(veps[:, u, :], mv[:, u, 1:2], EPS, None, ALU.add).then_inc(var_ready, 1)

            def normed(b, u):
                dve.wait_ge(rstd_ready, b + 1)
                nc.vector.tensor_scalar(xn[:, u, :], X[:, b, :], mv[:, u, 0:1], rstd[:, u, :],
                                        ALU.subtract, ALU.mult).then_inc(xn_ready, 1)

            def probs_turned(b):
                for g in range(4):
                    dve.wait_ge(pT_psum, b * 4 + g + 1)
                    nc.vector.tensor_copy(PT[:, g, :], bank[4 + g % 2][:, :]).then_inc(pT_ready, 1)

            def add_attention(b):
                dve.wait_ge(att_psum, b + 1)
                nc.vector.tensor_tensor(X[:, b, :], X[:, b, :], bank[6][:, 0:D], ALU.add).then_inc(x1_ready, 1)

            def normalise(b, u):
                for q in range(2):
                    dve.wait_ge(exp_ready, b * 2 + q + 1)
                    link(nc.vector.reciprocal(rden[:, u, q * 8:q * 8 + 8], den[:, u, q * 8:q * 8 + 8]))
                    nc.vector.tensor_tensor(P[:, u, q * 8:q * 8 + 8, :], P[:, u, q * 8:q * 8 + 8, :],
                                            rden[:, u, q * 8:q * 8 + 8].unsqueeze(2).to_broadcast([128, 8, 128]),
                                            ALU.mult).then_inc(prob_ready, 1)

            def maxima(b, u):
                for q in range(2):
                    dve.wait_ge(score_psum, b * 2 + q + 1)
                    for k in range(2):
                        ins = nc.vector.tensor_reduce(
                            nmx[:, u, q * 8 + k * 4:q * 8 + k * 4 + 4],
                            bank[q * 2 + k][:, :].rearrange("p (h l) -> p h l", h=4), AX.X, ALU.max, negate=True)
                    ins.then_inc(max_ready, 1)

            def attend(b, u):
                added, cur, first, rows, back, ask = turn_has(b, -2, 0, 3, 2, -1, 1)
                if cur:
                    normalise(b, u)
                if added:
                    add_attention(b - 2)
                if first:
                    stats(b + 3, 1 - u)
                if rows:
                    normed(b + 2, u)
                if back:
                    probs_turned(b - 1)
                if ask:
                    maxima(b + 1, 1 - u)

            dve.wait_ge(ld_x, 16)
            for b in range(-3, 2):
                attend(b, b % 2)
            with dve.Fori(1, B // 2 - 2) as i:
                ch.enter(i - 1, 8)
                for u in range(2):
                    attend(i * 2 + u, u)
                ch.leave(B // 2 - 3)
            for b in range(B - 4, B + 2):
                attend(b, b % 2)

            dve.wait_ge(x1_ready, B)

            def places(b, u):
                dve.wait_ge(logit_psum, b + 1)
                link(nc.vector.tensor_copy(LG[:, u, :], bank[u][:, 0:E]))
                hold(dve)
                link(nc.vector.max(top[:, u, :], LG[:, u, :]))
                hold(dve)
                nc.vector.match_replace(rest[:, u, :], top[:, u, :], LG[:, u, :], -3.0e38)
                link(nc.vector.tensor_scalar(ntop[:, u, :], top[:, u, 0:1], -1.0, None, ALU.mult))
                nc.vector.tensor_copy(lsum[:, u, 1:2], ntop[:, u, :]).then_inc(top_ready, 1)
                link(nc.vector.tensor_tensor(sel[:, u, :], rest[:, u, :], LG[:, u, :], ALU.not_equal))
                nc.vector.tensor_tensor(seen[:, 1 - u, :], seen[:, u, :], sel[:, u, :], ALU.add).then_inc(sel_ready, 1)
                dve.wait_ge(ex_ready, b + 1)
                link(nc.vector.scalar_tensor_tensor(ex[:, u, :], ex[:, u, :], 1.0, sel[:, u, :], ALU.mult, ALU.mult,
                                                    accum_out=lsum[:, u, 0:1]))
                link(nc.vector.reciprocal(lsum[:, u, 0:1], lsum[:, u, 0:1]))
                nc.vector.tensor_scalar(XR[:, u, D:XW], ex[:, u, :], lsum[:, u, 0:1], None,
                                        ALU.mult).then_inc(row_ready, 1)
                dve.wait_ge(place_psum, b + 1)
                nc.vector.scalar_tensor_tensor(fits[:, u, :], bank[2 + u][:, 0:E], float(CAP), sel[:, u, :],
                                               ALU.is_lt, ALU.mult)
                link(nc.vector.tensor_tensor(code[:, u, :], bank[2 + u][:, 0:E], CO[:, C_ECODE:C_ECODE + E], ALU.add))
                link(nc.vector.tensor_tensor(code[:, u, :], code[:, u, :], fits[:, u, :], ALU.mult))
                hold(dve)
                link(nc.vector.max(code8[:, u, :], code[:, u, :]))
                link(nc.vector.tensor_scalar(none8[:, u, :], code8[:, u, :], 0.0, float(E * CAP + 1),
                                             ALU.is_equal, ALU.mult))
                nc.vector.scalar_tensor_tensor(IDX[:, b, :], code8[:, u, :], -1.0, none8[:, u, :], ALU.add, ALU.add)
                link(nc.vector.tensor_tensor(SELT[:, bass.ds(b * S, S)], bank[4 + u][0:E, 0:128],
                                             REV[:, bass.ds(b * S, S)], ALU.mult))

            def route_normed(b, u, free):
                dve.wait_ge(rstd_ready, B + b + 1)
                if free:
                    dve.wait_ge(row_stored[u], b * 8 - (8 * u))
                nc.vector.tensor_scalar(XR[:, u, 0:D], X[:, b, :], mv[:, u, 0:1], rstd[:, u, :],
                                        ALU.subtract, ALU.mult).then_inc(xn_ready, 1)

            nc.vector.memset(W2F[:, (FT - 1) * D:FT * D], 0.0).then_inc(w2_cleared, 1)
            nc.vector.memset(ones[:, :], 1.0)
            nc.vector.memset(magic[:, 0:1], MAGIC)
            nc.vector.memset(magic[:, 1:2], -MAGIC)
            nc.vector.memset(seen[:, :, :], 0.0)
            nc.vector.tensor_copy(upb[:, :], CO[:, C_UP:C_UP + 128])
            nc.vector.memset(onesb[:, :], 1.0)
            link(nc.vector.memset(YS[:, :, :], 0.0))
            nc.vector.memset(none8[:, :, :], 0.0).then_inc(zero_ready, 1)
            stats(0, 0)
            stats(1, 1)
            route_normed(0, 0, False)
            stats(2, 0)
            route_normed(1, 1, False)
            dve.wait_ge(rev_ready, 1)
            places(0, 0)
            stats(3, 1)
            route_normed(2, 0, True)
            places(1, 1)
            with dve.Fori(1, B // 2 - 1) as i:
                ch.enter(i - 1, 26)
                for v in range(2):
                    b = i * 2 + v
                    stats(b + 2, v)
                    route_normed(b + 1, 1 - v, True)
                    places(b, v)
                ch.leave(B // 2 - 2)
            route_normed(B - 1, 1, True)
            places(B - 2, 0)
            places(B - 1, 1)
            for r in range(CAP // 8):
                link(nc.vector.max(TL[:, 0, r * 8:r * 8 + 8], SELT))
                link(nc.vector.match_replace(SELT, TL[:, 0, r * 8:r * 8 + 8], SELT, -1.0))
            nc.vector.tensor_scalar(TL[:, 1, :], TL[:, 0, :], -1.0, float(B * S), ALU.mult,
                                    ALU.add).then_inc(list_ready, 1)
            dve.wait_ge(slot_psum, 1)
            nc.vector.tensor_scalar(GI[:, :], bank[0][:, 0:NPE], float(B * S - 1), None, ALU.min).then_inc(gi_ready, 1)

            dve.wait_ge(wsum_psum, 1)
            link(nc.vector.tensor_reduce(wmean[:, :], bank[7][:, 0:6].rearrange("p (w c) -> p w c", c=2), AX.X, ALU.add))
            link(nc.vector.tensor_scalar(wmean[:, :], wmean[:, :], 1.0 / (F1 * D), EPS, ALU.mult, ALU.max))
            link(nc.vector.tensor_scalar(wdeq[:, 0:1], wmean[:, 0:1], 0.5 / 127.0, None, ALU.mult))
            nc.vector.tensor_scalar(wdeq[:, 1:2], wmean[:, 1:2], wdeq[:, 0:1], 1.0 / 127.0, ALU.mult, ALU.mult)
            nc.vector.tensor_scalar(wdeq[:, 2:3], wmean[:, 2:3], 1.0 / 127.0, None, ALU.mult)
            nc.vector.reciprocal(wscale[:, :], wmean[:, :]).then_inc(wscale_ready, 1)
            dve.wait_ge(wround_ready, 1)
            nc.vector.tensor_scalar(W1F, W1F, MAGIC, 1.0, ALU.subtract, ALU.min)
            link(nc.vector.tensor_scalar(W2F, W2F, MAGIC, 1.0, ALU.subtract, ALU.min))
            nc.vector.tensor_scalar(W1[:, :, :, :].rearrange("p c w n -> p (c w n)"), W1F, -1.0, None, ALU.max)
            nc.vector.tensor_scalar(W2[:, :, :].rearrange("p t n -> p (t n)"), W2F, -1.0, None,
                                    ALU.max).then_inc(w_ready, 1)

            def hidden(i, v):
                j, u = i * RING + v, v % 2
                dve.wait_ge(gathered[u], i * (RING // 2 * 16) + v // 2 * 16 + 16)
                for e in range(2):
                    w = XG[64 * e:64 * e + 64, u, bass.ds(j * 2 + D + e, 1)]
                    nc.vector.tensor_scalar(wslot[64 * e:64 * e + 64, u, :], w, 0.5, None, ALU.mult)
                dve.wait_ge(tanh_ready, j + 1)
                link(nc.vector.scalar_tensor_tensor(TH[:, u, :], TH[:, u, :], 1.0, bank[2 + u][:, 0:FE],
                                                    ALU.add, ALU.mult))
                nc.vector.scalar_tensor_tensor(HH[:, u, :], TH[:, u, :], wslot[:, u, :], bank[2 + u][:, FE:2 * FE],
                                               ALU.mult, ALU.mult).then_inc(h_ready, 1)

            def slots_out(i, v):
                j, u = i * RING + v, v % 2
                dve.wait_ge(down_psum, j + 1)
                if not (isinstance(i, int) and j < 2):
                    dve.wait_ge(os_stored[u], i * (RING // 2 * 16) + v // 2 * 16)
                nc.vector.tensor_copy(OS[:, u, :], bank[6 + u][:, 0:D]).then_inc(os_ready, 1)

            def expert_body(i, v, nxt):
                n = (i, v + 1) if v + 1 < RING else (i + 1, 0)
                if nxt:
                    hidden(*n)
                slots_out(i, v)

            hidden(0, 0)
            for v in range(RING):
                expert_body(0, v, True)
            with dve.Fori(1, NPE // RING - 1) as i:
                ch.enter(i - 1, RING)
                for v in range(RING):
                    expert_body(i, v, True)
                ch.leave(NPE // RING - 2)
            for v in range(RING):
                expert_body(NPE // RING - 1, v, v + 1 < RING)

            for u in range(2):
                ins = nc.vector.tensor_copy(KT[KR1:KM1, u, :, :],
                                            CO[KR1:KM1, C_KV:C_KV + KV].unsqueeze(2).to_broadcast([3 * KV, KV, 128]))
            ins.then_inc(select_ready, 1)

            def combine(b, u):
                dve.wait_ge(yg_in[u], b * 64 + (128 - 64 * u))
                link(nc.vector.tensor_reduce(YS[:, u, :], YG[:, u, :, :].rearrange("p k d -> p d k"), AX.X, ALU.add))
                ins = nc.vector.tensor_tensor(X[:, b, :], X[:, b, :], YS[:, u, :], ALU.add)
                ins.then_inc(x2_ready, 1)
                dve.wait_ge(x2_ready, b + 1)
                hold(dve)
                stats(b, u)

            def split_queries(b, u):
                q6 = Q6[:, u]
                since(dve, q6_copied, b)
                dve.wait_ge(rstd_ready, b + (2 * B + 1))
                nc.vector.tensor_scalar(xq[:, 0, :], X[:, b, :], mv[:, u, 0:1], rstd[:, u, :],
                                        ALU.subtract, ALU.mult).then_inc(xq_ready, 1)
                dve.wait_ge(xq_ready, b + 1)
                link(nc.vector.tensor_copy(q6[:, :, :, 0, :], heads(xq[:, 0, :])))
                nc.vector.tensor_tensor(heads(xq[:, 1, :]), heads(xq[:, 0, :]), q6[:, :, :, 0, :],
                                        ALU.subtract).then_inc(xr_ready, 1)
                dve.wait_ge(xr_ready, b + 1)
                link(nc.vector.tensor_copy(q6[:, :, :, 1, :], heads(xq[:, 1, :])))
                nc.vector.tensor_tensor(q6[:, :, :, 5, :], heads(xq[:, 1, :]), q6[:, :, :, 1, :],
                                        ALU.subtract).then_inc(q6_ready, 1)

            def maxima1(b, g):
                dve.wait_ge(a_psum, b * 4 + g + 1)
                nc.vector.tensor_reduce(nm[:, g * KV:g * KV + KV],
                                        PS[:, g % 2 * 2:g % 2 * 2 + 2, :].rearrange("p a (k t) -> p (a k) t", t=128),
                                        AX.X, ALU.max, negate=True).then_inc(a_read, 1)

            def split_maxima(b):
                dve.wait_ge(a_read, b * 4 + 4)
                n = nm[:, :].rearrange("p (g k) -> p g k", g=G1)
                link(nc.vector.tensor_copy(M3[:, :, 0, :], n))
                link(nc.vector.tensor_tensor(n, n, M3[:, :, 0, :], ALU.subtract))
                link(nc.vector.tensor_copy(M3[:, :, 1, :], n))
                nc.vector.tensor_tensor(M3[:, :, 2, :], n, M3[:, :, 1, :], ALU.subtract).then_inc(m3_ready, 1)

            def outputs(b):
                for half in range(2):
                    dve.wait_ge(o_psum, b * 2 + half + 1)
                    o = bank[6 + half].rearrange("p (g k c) -> p g k c", g=G1, k=4)
                    link(nc.vector.reciprocal(RD[:, half, :, :], o[:, :, :, DH]))
                    ins = nc.vector.tensor_tensor(
                        OA[:, half * 128:half * 128 + 128].rearrange("p (k g d) -> p g k d", k=4, g=G1),
                        o[:, :, :, 0:DH], RD[:, half, :, :].unsqueeze(3).to_broadcast([128, G1, 4, DH]), ALU.mult)
                link(ins)
                nc.vector.tensor_tensor(X[:, b, :], X[:, b, :], OA[:, :], ALU.add).then_inc(x3_ready, 1)

            def attend1(b, u):
                rows, back, query, new = turn_has(b, 1, -1, 3, 4)
                for g in range(G1):
                    if back and g == 3:
                        outputs(b - 1)
                    if rows:
                        maxima1(b + 1, g)
                if rows:
                    split_maxima(b + 1)
                if query:
                    split_queries(b + 3, 1 - u)
                if new:
                    combine(b + 4, u)

            for b in range(-4, 2):
                attend1(b, b % 2)
            with dve.Fori(1, B // 2 - 2) as i:
                ch.enter(i - 1, 22)
                for u in range(2):
                    attend1(i * 2 + u, u)
                ch.leave(B // 2 - 3)
            for b in range(B - 4, B + 1):
                attend1(b, b % 2)

            def quantise(b, u):
                xs = xscale[:, u, :]
                dve.wait_ge(rstd_ready, 3 * B + b + 1)
                link(nc.vector.tensor_scalar(XF[:, :], X[:, b, :], mv[:, u, 0:1], rstd[:, u, :],
                                             ALU.subtract, ALU.mult))
                link(nc.vector.tensor_reduce(xs[:, 0:1], XF[:, :], AX.X, ALU.max, apply_absolute_value=True))
                link(nc.vector.tensor_scalar(xs[:, 0:1], xs[:, 0:1], EPS, None, ALU.max))
                nc.vector.tensor_scalar(xs[:, 2:3], xs[:, 0:1], wdeq[:, 0:1], None, ALU.mult)
                nc.vector.tensor_scalar(xs[:, 3:4], xs[:, 0:1], xs[:, 0:1], wdeq[:, 1:2], ALU.mult, ALU.mult)
                link(nc.vector.reciprocal(xs[:, 1:2], xs[:, 0:1]))
                link(nc.vector.tensor_scalar(xs[:, 1:2], xs[:, 1:2], 127.0, None, ALU.mult))
                link(nc.vector.tensor_scalar(XF[:, :], XF[:, :], xs[:, 1:2], MAGIC, ALU.mult, ALU.add))
                nc.vector.tensor_scalar(XQ[:, u, :], XF[:, :], MAGIC, None, ALU.subtract).then_inc(xqf_ready, 1)

            def hidden1(b, u):
                xs, hs = xscale[:, u, :], hscale[:, u, :]
                dve.wait_ge(tg_ready, b + 1)
                tg = TG[:, :].rearrange("p (a n) -> p a n", a=2)
                link(nc.vector.scalar_tensor_tensor(tg, tg, 1.0, PS[:, 0:2, 0:F1 // 2], ALU.add, ALU.mult))
                nc.vector.tensor_tensor(HG[:, u, :].rearrange("p (a n) -> p a n", a=2), tg,
                                        PS[:, 2:4, 0:F1 // 2], ALU.mult).then_inc(gu1_read, 1)
                dve.wait_ge(gu1_read, b + 1)
                link(nc.vector.tensor_reduce(hs[:, 0:1], HG[:, u, :], AX.X, ALU.max, apply_absolute_value=True))
                link(nc.vector.tensor_scalar(hs[:, 0:1], hs[:, 0:1], xs[:, 3:4], EPS, ALU.mult, ALU.max))
                link(nc.vector.reciprocal(hs[:, 1:2], hs[:, 0:1]))
                nc.vector.tensor_scalar(hs[:, 1:2], hs[:, 1:2], xs[:, 3:4], 127.0, ALU.mult,
                                        ALU.mult).then_inc(hscale_ready, 1)
                link(nc.vector.tensor_scalar(hs[:, 2:3], hs[:, 0:1], wdeq[:, 2:3], None, ALU.mult))

            def add_down(b, u):
                dve.wait_ge(down1_psum, b + 1)
                nc.vector.scalar_tensor_tensor(X[:, b, :], bank[5 + 2 * u][:, 0:D], hscale[:, u, 2:3], X[:, b, :],
                                               ALU.mult, ALU.add).then_inc(y_ready, 1)

            def feed(b, u, more=True, nxt=True, cur=True, prv=True):
                if nxt:
                    quantise(b + 1, 1 - u)
                if more:
                    stats(b + 2, u)
                if cur:
                    hidden1(b, u)
                if prv:
                    add_down(b - 1, 1 - u)

            dve.wait_ge(x3_ready, B)
            hold(dve)
            stats(0, 0)
            feed(-1, 1, cur=False, prv=False)
            feed(0, 0, prv=False)
            with dve.Fori(0, B // 2 - 2) as i:
                ch.enter(i, 26)
                for v in range(2):
                    feed(i * 2 + v + 1, 1 - v)
                ch.leave(B // 2 - 2)
            feed(B - 3, 1)
            feed(B - 2, 0, more=False)
            feed(B - 1, 1, more=False, nxt=False)
            feed(B, 0, more=False, nxt=False, cur=False)

        @block.scalar
        def _(act):
            def fold(i, u):
                p = i * 2 + u
                act.wait_ge(fold_a1, p + 1)
                nc.scalar.copy(A1[:, u, :, :].rearrange("p c n -> p (c n)"),
                               bank[u][0:KC, 0:256]).then_inc(fold_a1_out, 1)
                act.wait_ge(fold_nv, p + 1)
                nc.scalar.copy(V[:, p, :], bank[6 + u][:, 0:D]).then_inc(fold_v_out, 1)

            with act.Fori(0, NP0 // 2) as i:
                for u in range(2):
                    fold(i, u)

            def rows_turned(b, u):
                act.wait_ge(xnT_psum, b + 1)
                nc.scalar.copy(xnT[:, u, :, :].rearrange("p c s -> p (c s)"),
                               bank[7][:, 0:256]).then_inc(xnT_ready, 1)
                for h in range(2):
                    ins = nc.scalar.copy(BD[64 * h:64 * h + 64, u, h, :], bank[7][64 * h:64 * h + 64, 256:384])
                ins.then_inc(bd_ready, 1)

            def queries(b, u):
                for q in range(2):
                    act.wait_ge(q_psum, b * 2 + q + 1)
                    nc.scalar.copy(qT[:, u, q * 4:q * 4 + 4, :].rearrange("p h s -> p (h s)"),
                                   bank[4 + q][:, :]).then_inc(qT_ready, 1)

            def exps(b, u, q):
                act.wait_ge(max_ready, b * 2 + q + 1)
                for h in range(q * 8, q * 8 + 8):
                    ins = nc.scalar.activation(P[:, u, h, :], bank[h // 4][:, (h % 4) * 128:(h % 4) * 128 + 128],
                                               ACT.Exp, bias=nmx[:, u, h:h + 1], accum_out=den[:, u, h:h + 1])
                ins.then_inc(exp_ready, 1)

            def contexts(b):
                for q in range(2):
                    act.wait_ge(ctx_psum, b * 2 + q + 1)
                    nc.scalar.copy(cT[:, q, :], bank[4 + q][:, :]).then_inc(ctxT_ready, 1)

            def attend(b, u):
                ask, back, rows = turn_has(b, 1, -1, 2)
                if ask:
                    queries(b + 1, 1 - u)
                if back:
                    contexts(b - 1)
                if ask:
                    exps(b + 1, 1 - u, 0)
                if rows:
                    rows_turned(b + 2, u)
                if ask:
                    exps(b + 1, 1 - u, 1)

            for b in range(-2, 2):
                attend(b, b % 2)
            with act.Fori(1, B // 2 - 1) as i:
                for u in range(2):
                    attend(i * 2 + u, u)
            for b in range(B - 2, B + 1):
                attend(b, b % 2)

            def route(b, u):
                act.wait_ge(xnT_psum, B + b + 1)
                nc.scalar.copy(xnT[:, u, :, :].rearrange("p c s -> p (c s)"),
                               bank[6][:, 0:256]).then_inc(xnT_ready, 1)

            def route_exp(b, u):
                act.wait_ge(top_ready, b + 1)
                nc.scalar.activation(ex[:, u, :], LG[:, u, :], ACT.Exp, bias=ntop[:, u, :]).then_inc(ex_ready, 1)

            route(0, 0)
            with act.Fori(0, B // 2 - 1) as i:
                for v in range(2):
                    route(i * 2 + v + 1, 1 - v)
                    route_exp(i * 2 + v, v)
            route(B - 1, 1)
            route_exp(B - 2, 0)
            route_exp(B - 1, 1)

            act.wait_ge(ld_w12, 16 + 16 * FT)
            pieces = [(w, c, W1F[:, (c * 2 + w) * F1:(c * 2 + w) * F1 + F1]) for c in range(2) for w in range(2)]
            pieces += [(2, c, W2F[:, c * FT * D // 2:(c + 1) * FT * D // 2]) for c in range(2)]
            for n, (w, c, piece) in enumerate(pieces):
                nc.scalar.activation(scratch[:, 0:piece.shape[-1]], piece, ACT.Abs,
                                     accum_out=wsum[:, w, c:c + 1]).then_inc(act_own, 1)
                act.wait_ge(act_own, n + 1)
            act.sem_inc(wsum_ready, 1)
            act.wait_ge(wscale_ready, 1)
            for w, c, piece in pieces:
                ins = nc.scalar.activation(piece, piece, ACT.Identity, scale=wscale[:, w:w + 1], bias=magic[:, 0:1])
            ins.then_inc(wround_ready, 1)

            def rows(j, u):
                act.wait_ge(xg_psum, j + 1)
                nc.scalar.copy(XGT[:, u, :, :].rearrange("p c s -> p (c s)"),
                               bank[u][:, 0:256]).then_inc(xg_ready, 1)

            def tanh(j, u):
                act.wait_ge(gu_psum, j + 1)
                nc.scalar.activation(TH[:, u, :], bank[2 + u][:, 0:FE], ACT.Tanh, scale=0.5).then_inc(tanh_ready, 1)

            def turned(j, u):
                act.wait_ge(hT_psum, j + 1)
                nc.scalar.copy(HT[:, u, :], bank[4 + u][0:FE, 0:128]).then_inc(hT_ready, 1)

            rows(0, 0)
            tanh(0, 0)
            rows(1, 1)
            turned(0, 0)
            tanh(1, 1)
            with act.Fori(0, NPE // 2 - 1) as i:
                for v in range(2):
                    rows(i * 2 + v + 2, v)
                    turned(i * 2 + v + 1, 1 - v)
                    tanh(i * 2 + v + 2, v)
            turned(NPE - 1, 1)

            def copy_queries(b, u):
                act.wait_ge(xq_ready, b + 1)
                nc.scalar.copy(Q6[:, u, :, :, 2, :], heads(xq[:, 0, :]))
                nc.scalar.copy(Q6[:, u, :, :, 4, :], heads(xq[:, 0, :]))
                act.wait_ge(xr_ready, b + 1)
                nc.scalar.copy(Q6[:, u, :, :, 3, :], heads(xq[:, 1, :])).then_inc(q6_copied, 1)

            def turned(b, u):
                for q in range(2):
                    act.wait_ge(qt_psum, b * 2 + q + 1)
                    nc.scalar.copy(QT[0:KR1, u, q * 8:q * 8 + 8, :].rearrange("p a s -> p (a s)"),
                                   bank[6 + q].bitcast(bf16)[0:KR1, :]).then_inc(qt_ready, 1)
                act.wait_ge(kt_psum, b + 1)
                nc.scalar.copy(KT[0:KR1, u, :, :].rearrange("p k t -> p (k t)"),
                               bank[0].bitcast(bf16)[0:KR1, :]).then_inc(kt_ready, 1)

            def turned_maxima(b, u):
                act.wait_ge(mt_psum, b + 1)
                m = bank[1].bitcast(bf16)[0:3 * KV, 0:G1 * 128].rearrange("p (g s) -> p g s", g=G1)
                nc.scalar.copy(QT[KR1:KM1, u, :, :].rearrange("p (g j) s -> p g j s", g=G1),
                               m.unsqueeze(2).to_broadcast([3 * KV, G1, 4, 128])).then_inc(mt_ready, 1)

            def attend1(b, u):
                cols, new, rows, copied = turn_has(b, 0, 2, 1, 3)
                if cols:
                    for kv in range(KV):
                        act.wait_ge(b_psum, b * 8 + kv + 1)
                        nc.scalar.activation(PE1[:, kv, :], bank[4 + kv % 2], ACT.Exp,
                                             scale=SCALE1).then_inc(e_ready, 1)
                if new:
                    turned(b + 2, u)
                if rows:
                    turned_maxima(b + 1, 1 - u)
                if cols:
                    for half in range(2):
                        act.wait_ge(pv_psum, b * 2 + half + 1)
                        nc.scalar.copy(OT[:, half, :], bank[6 + half]).then_inc(ot_ready, 1)
                if copied:
                    copy_queries(b + 3, 1 - u)

            for b in range(-3, 2):
                attend1(b, b % 2)
            with act.Fori(1, B // 2 - 2) as i:
                for u in range(2):
                    attend1(i * 2 + u, u)
            for b in range(B - 4, B):
                attend1(b, b % 2)

            def rows_turned(b):
                act.wait_ge(xqT_psum, b + 1)
                nc.scalar.copy(XQT[:, :, :].rearrange("p c s -> p (c s)"),
                               bank[6].bitcast(bf16)[:, 0:256]).then_inc(xqT_ready, 1)

            def hidden_turned(b):
                act.wait_ge(hqT_psum, b + 1)
                nc.scalar.copy(HQT[:, 0:FT - 1, :].rearrange("p t s -> p (t s)"),
                               bank[4].bitcast(bf16)[:, 0:(FT - 1) * 128])
                nc.scalar.copy(HQT[0:F1 % 128, FT - 1, :],
                               bank[4].bitcast(bf16)[0:F1 % 128, (FT - 1) * 128:FT * 128]).then_inc(hqT_ready, 1)

            def gate_tanh(b, u):
                act.wait_ge(gu1_psum, b + 1)
                nc.scalar.activation(TG[:, :].rearrange("p (a n) -> p a n", a=2), PS[:, 0:2, 0:F1 // 2], ACT.Tanh,
                                     scale=xscale[:, u, 2:3]).then_inc(tg_ready, 1)

            def round_hidden(b, u):
                act.wait_ge(hscale_ready, b + 1)
                nc.scalar.activation(HG[:, u, :], HG[:, u, :], ACT.Identity, scale=hscale[:, u, 1:2],
                                     bias=magic[:, 0:1]).then_inc(hround_ready, 1)
                act.wait_ge(hround_ready, b + 1)
                nc.scalar.activation(HQ[:, :], HG[:, u, :], ACT.Identity, bias=magic[:, 1:2]).then_inc(hq_ready, 1)

            def feed(b, u, nxt=True, cur=True, prv=True):
                if nxt:
                    rows_turned(b + 1)
                if prv:
                    hidden_turned(b - 1)
                if nxt:
                    gate_tanh(b + 1, 1 - u)
                if cur:
                    round_hidden(b, u)

            feed(-1, 1, cur=False, prv=False)
            feed(0, 0, prv=False)
            with act.Fori(0, B // 2 - 1) as i:
                for v in range(2):
                    feed(i * 2 + v + 1, 1 - v)
            feed(B - 1, 1, nxt=False)
            feed(B, 0, nxt=False, cur=False)

        @block.gpsimd
        def _(pool):
            ch = Chain(pool, pool_own)
            half = DC // 2
            cos = CO[:, C_COS:C_COS + DC]
            sin = CO[:, C_SIN:C_SIN + DC]
            pool.wait_ge(ld_const, 16)
            pool.wait_ge(ld_ctx, 16)
            tmp = P[:, 0, 0:8, :].rearrange("p h l -> p (h l)").rearrange("p (b c) -> p b c", b=B)
            nc.gpsimd.tensor_tensor(KR[:, :, :], CT[:, :, :], cos.unsqueeze(1).to_broadcast([128, B, DC]), ALU.mult)
            nc.gpsimd.tensor_tensor(tmp[:, :, 0:half], CT[:, :, half:DC],
                                    sin[:, 0:half].unsqueeze(1).to_broadcast([128, B, half]), ALU.mult)
            ch.link(nc.gpsimd.tensor_tensor(tmp[:, :, half:DC], CT[:, :, 0:half],
                                            sin[:, half:DC].unsqueeze(1).to_broadcast([128, B, half]), ALU.mult))
            ch.link(nc.gpsimd.tensor_tensor(KR[:, :, :], KR[:, :, :], tmp, ALU.add))
            pool.wait_ge(setup_done, 1)

            def root(b, u):
                pool.wait_ge(var_ready, b + 1)
                nc.gpsimd.tensor_tensor(rstd[:, u, :], veps[:, u, :], epsneg[:, :], ALU.pow).then_inc(rstd_ready, 1)

            def keys(b, u):
                for k in range(2):
                    ins = nc.gpsimd.tensor_copy(KD[:, u, k, :], KR[:, b, :])
                ins.then_inc(kd_ready, 1)

            def attend(b, u):
                first, cur = turn_has(b, 3, 0)
                if first:
                    root(b + 3, 1 - u)
                    since(pool, kdT_psum, b + 2)
                    hold(pool)
                    keys(b + 3, 1 - u)
                if cur:
                    since(pool, att_psum, b - 1)
                    hold(pool)
                    nc.gpsimd.tensor_copy(VD[:, u, :], KR[:, b, :]).then_inc(vd_ready, 1)

            for b in range(-3, 2):
                attend(b, b % 2)
            with pool.Fori(1, B // 2 - 2) as i:
                for u in range(2):
                    attend(i * 2 + u, u)
            for b in range(B - 4, B):
                attend(b, b % 2)

            pool.wait_ge(x1_ready, B)
            nc.gpsimd.iota(REV, [[-1, B * S]], base=B * S, channel_multiplier=0,
                           allow_small_or_imprecise_dtypes=True).then_inc(rev_ready, 1)
            with pool.Fori(0, B // 2) as i:
                for u in range(2):
                    root(i * 2 + u + B, u)

            nc.gpsimd.memset(V1[:, :, :, :], 1.0)
            nc.gpsimd.memset(KZ[:, :, :, :, :, :].rearrange("p a j k t d -> p (a j k t d)"), 0.0)
            ch.link(nc.gpsimd.tensor_copy(CB[0][:, :, :], CT[:, :, :]))
            ch.link(nc.gpsimd.tensor_tensor(CRST[:, :, :], CT[:, :, :], CB[0][:, :, :], ALU.subtract))
            ch.link(nc.gpsimd.tensor_copy(CB[1][:, :, :], CRST[:, :, :]))
            ins = nc.gpsimd.tensor_tensor(CB[2][:, :, :], CRST[:, :, :], CB[1][:, :, :], ALU.subtract)
            ins.then_inc(parts_ready, 1)
            pool.wait_ge(parts_ready, 1)

            pool.wait_ge(gi_ready, 1)
            pool.wait_ge(row_stored[0], B // 2 * 16)
            pool.wait_ge(row_stored[1], B // 2 * 16)

            def gather(i, u, free):
                j = i * 2 + u
                if free:
                    pool.wait_ge(xg_psum, j - 1)
                    pool.wait_ge(h_ready, j - 1)
                    hold(pool)
                ch.link(nc.gpsimd.tensor_copy(gidx[:, u, :], GI[:, bass.ds(j, 1)]))
                hold(pool)
                nc.gpsimd.indirect_dma_start(
                    XG[:, u, :], None, routed, bass.IndirectOffsetOnAxis(ap=gidx[:, u, :], axis=0),
                    bounds_check=B * S - 1, oob_is_err=False).then_inc(gathered[u], 16)

            for u in range(2):
                gather(0, u, False)
            with pool.Fori(1, NPE // 2) as i:
                ch.enter(i - 1, 2)
                for u in range(2):
                    gather(i, u, True)
                ch.leave(NPE // 2 - 1)

            pool.wait_ge(os_stored[0], NPE // 2 * 16)
            pool.wait_ge(os_stored[1], NPE // 2 * 16)
            pool.wait_ge(zero_stored, 16)

            def collect(b, u):
                since(pool, x2_ready, b - 1)
                hold(pool)
                ch.link(nc.gpsimd.tensor_copy(cidx[:, u, :], IDX[:, b, :]))
                hold(pool)
                for k in range(TOPK):
                    nc.gpsimd.indirect_dma_start(
                        YG[:, u, k, :], None, moe, bass.IndirectOffsetOnAxis(ap=cidx[:, u, k:k + 1], axis=0),
                        bounds_check=E * CAP, oob_is_err=False).then_inc(yg_in[u], 16)

            def keys1(b):
                since(pool, kt_psum, b)
                hold(pool)
                for k in range(2):
                    for part, slots in ((0, slice(0, 2)), (0, slice(5, 6)), (1, slice(2, 4)), (2, slice(4, 5))):
                        n = slots.stop - slots.start
                        ins = nc.gpsimd.tensor_copy(
                            KZ[:, k, :, k, slots, :],
                            CB[part][:, b, :].rearrange("p (j k d) -> p j k d", j=4, k=2)[:, :, k, :]
                            .unsqueeze(2).to_broadcast([128, 4, n, DH]))
                ins.then_inc(kz_ready, 1)

            def values1(b, u):
                since(pool, pv_psum, b * 2 - 2)
                hold(pool)
                nc.gpsimd.tensor_copy(V1[:, u, :, 0:DH],
                                      CT[:, b, :].rearrange("p (k d) -> p k d", k=KV)).then_inc(v1_ready, 1)

            def attend1(b, u):
                norm, rows, key, value = turn_has(b, 4, 6, 3, 1)
                if norm:
                    root(b + (2 * B + 4), u)
                if rows:
                    collect(b + 6, u)
                if key:
                    keys1(b + 3)
                if value:
                    values1(b + 1, 1 - u)

            for b in range(-6, 2):
                attend1(b, b % 2)
            with pool.Fori(1, B // 2 - 3) as i:
                ch.enter(i - 1, 2)
                for u in range(2):
                    attend1(i * 2 + u, u)
                ch.leave(B // 2 - 4)
            for b in range(B - 6, B):
                attend1(b, b % 2)

            with pool.Fori(0, B // 2) as i:
                for u in range(2):
                    root(i * 2 + u + 3 * B, u)


def _constants():
    c = np.zeros((128, C_END), np.float32)
    r = np.arange(128)
    c[:, C_ID:C_ID + 128] = np.eye(128)
    c[:, C_UP:C_UP + 128] = r[:, None] < r[None, :]
    c[:, C_ECODE:C_ECODE + E] = np.arange(E) * CAP + 1
    inv = (1.0 / np.float32(10000.0) ** (np.arange(0, DC, 2, dtype=np.float32) / DC)).astype(np.float32)
    freqs = (np.arange(S, dtype=np.float32)[:, None] * inv[None, :]).astype(np.float32)
    sin, cos = np.repeat(np.sin(freqs), 2, -1), np.repeat(np.cos(freqs), 2, -1)
    sin[:, :DC // 2] *= -1
    c[:, C_COS:C_COS + DC] = cos
    c[:, C_SIN:C_SIN + DC] = sin
    for k in range(3):
        c[96 + k * KV:96 + k * KV + KV, C_KV:C_KV + KV] = np.eye(KV)
    for par in range(2):
        for n in range(NPE):
            c[2 * n + par, C_PAR + par * NPE + n] = 1
    return c


def _layout(i):
    wq = i["L0_xattn_Wq"].reshape(NP0, 2, K0, D).transpose(0, 2, 1, 3).reshape(NP0, K0, 2 * D)
    kv = i["L0_xattn_w_kc_kv"].reshape(NP0, 2, K0, DC).transpose(0, 2, 1, 3).reshape(NP0, K0, 2 * DC)
    wo = i["L0_xattn_Wo"].T.reshape(NP0, 2, K0, D).transpose(0, 2, 1, 3).reshape(NP0, K0, 2 * D)
    fold_a = np.concatenate([wq, kv, wo], -1)
    kq = i["L0_xattn_w_kc_q"].transpose(0, 2, 1).reshape(NP0, 2, 2, KC, K0).transpose(0, 3, 2, 1, 4).reshape(NP0, KC, 512)
    qr = i["L0_xattn_W_qr"].transpose(0, 2, 1).reshape(NP0, 128, CQ)
    kr = i["L0_xattn_W_kr"].transpose(0, 2, 1).reshape(NP0, 128, DC)
    fold_b = np.zeros((NP0, 128, 768), np.float32)
    fold_b[:, :KC, :512] = kq
    fold_b[:, :, 512:704] = qr
    fold_b[:, :, 704:] = kr
    gate_t = i["L0_ffn_gate_w"].T.reshape(2, 128, E).transpose(1, 0, 2)
    wg = i["L0_ffn_wg"].reshape(NPE, 2, 2, 128, FE)
    wu = i["L0_ffn_wu"].reshape(NPE, 2, 2, 128, FE)
    wgu = np.concatenate([wg, wu], -1).transpose(0, 3, 1, 2, 4)
    wd = i["L0_ffn_wd"].reshape(NPE, 2, FE, D).transpose(0, 2, 1, 3)
    w1 = np.concatenate([i["L1_ffn_w_gate"].T, i["L1_ffn_w_up"].T], -1).reshape(2, 128, 2 * F1).transpose(1, 0, 2)
    w2 = i["L1_ffn_w_down"].T
    c = np.ascontiguousarray
    return {"x": c(i["x"]), "ctx": c(i["ctx_512"]), "fold_a": c(fold_a), "fold_b": fold_b, "gate_t": c(gate_t),
            "wgu": c(wgu), "wd": c(wd), "w1": c(w1), "w2": c(w2), "consts": _constants()}


def kernel(**inputs):
    import concourse.bacc as bacc
    from concourse.bass_utils import run_bass_kernel_spmd as run

    nc = bacc.Bacc("TRN2", target_bir_lowering=False, num_devices=1)
    arrays = _layout({k: np.asarray(v) for k, v in inputs.items()})
    args = [nc.dram_tensor(n, a.shape, mybir.dt.from_np(a.dtype), kind="ExternalInput").ap()
            for n, a in arrays.items()]
    out = nc.dram_tensor("out", (B, S, D), fp32, kind="ExternalOutput").ap()
    build(nc, *args, out, STAGE)
    return run(nc, [arrays], core_ids=[0]).results[0]["out"]


STAGE = 4
```

```python
import numpy as np
import concourse.bass as bass
from concourse import mybir
from contextlib import ExitStack

fp32 = mybir.dt.float32
bf16 = mybir.dt.bfloat16
i32 = mybir.dt.int32
ALU = mybir.AluOpType
ACT = mybir.ActivationFunctionType
AX = mybir.AxisListType

B, S, D, DC = 16, 128, 256, 64
H0, K0, CQ = 16, 128, 192
NP0 = H0 // 2
E, TOPK, FE, CAP = 64, 8, 96, 64
NPE = E // 2
H1, KV, DH = 32, 8, 8
G1 = H1 // KV
KR1, KM1 = 12 * DH, 12 * DH + 3 * KV
F1 = 832
FT = 7
EPS = 1e-5
SCALE1 = DH ** -0.5
MAGIC = 1.5 * 2.0 ** 23
KC = CQ // 2
RING = 4
XW = D + E
C_ID, C_UP, C_ECODE, C_COS, C_SIN, C_KV, C_END = 0, 128, 256, 320, 384, 448, 456


class Chain:

    def __init__(self, eng, sem):
        self.eng, self.sem, self.base, self.n = eng, sem, 0, 0

    def link(self, ins):
        ins.then_inc(self.sem, 1)
        self.n += 1
        self.eng.wait_ge(self.sem, self.base + self.n)

    def mark(self, ins):
        ins.then_inc(self.sem, 1)
        self.n += 1
        return self.n

    def reach(self, n):
        self.eng.wait_ge(self.sem, self.base + n)

    def enter(self, i, per):
        self.before, self.per = self.base + self.n, per
        self.base, self.n = i * per + self.before, 0

    def leave(self, times):
        assert self.n == self.per, f"a turn of the loop links {self.n}, not {self.per}"
        self.base, self.n = self.before + times * self.per, 0


def build(nc, x, ctx, fold_a, fold_b, gate_t, wgu, wd, w1, w2, consts, out):
    es = ExitStack()
    with es:
        def sb(name, shape, dt=fp32):
            return es.enter_context(nc.sbuf_tensor(name, shape, dt))

        def sem(name):
            return es.enter_context(nc.semaphore(name))

        X = sb("X", [128, B, D])
        CT = sb("CT", [128, B, DC])
        KR = sb("KR", [128, B, DC])
        CO = sb("CO", [128, C_END])
        identf = CO[:, C_ID:C_ID + 128]
        identb = sb("identb", [128, 128], bf16)
        negroot = sb("negroot", [128, 1])
        NV = sb("NV", [128, 2 * NP0 * (128 + 128)])
        N = NV[:, 0:2 * NP0 * 128].rearrange("p (c h n) -> p c h n", c=2, h=NP0)
        V = NV[:, 2 * NP0 * 128:].rearrange("p (h n) -> p h n", h=NP0)
        st = sb("st", [128, 3, 6])
        mv = sb("mv", [128, 3, 2])
        veps = sb("veps", [128, 3, 1])
        rstd = sb("rstd", [128, 3, 1])
        xn = sb("xn", [128, 2, D])
        xnT = sb("xnT", [128, 2, 2, 128])
        FA = sb("FA", [128, 2, 1152])
        FB = sb("FB", [128, 2, 768])
        KB = sb("KB", [128, 2, 128])
        A1 = sb("A1", [KC, 2, 2, 128])
        A2 = sb("A2", [128, 2, 2, 64])
        KD = sb("KD", [128, 2, 2, DC])
        VD = sb("VD", [128, 2, DC])
        BD = sb("BD", [128, 2, 2, 128])
        MID = sb("MID", [128, 2 * NP0 * 128 + 2 * 512 + 4 * 512])
        qT = MID[:, 0:2048].rearrange("p (u h s) -> p u h s", u=2, h=NP0)
        nmx = sb("nmx", [128, 2, H0])
        den = sb("den", [128, 2, H0])
        rden = sb("rden", [128, 2, H0])
        P = sb("P", [128, 2, H0, 128])
        cT = MID[:, 2048:3072].rearrange("p (q n) -> p q n", q=2)
        PT = MID[:, 3072:5120].rearrange("p (q n) -> p q n", q=4)

        GT = sb("GT", [128, 2, E])
        upb = sb("upb", [128, 128], bf16)
        onesb = sb("onesb", [128, 128], bf16)
        XR = sb("XR", [128, 2, XW])
        LG = sb("LG", [128, 2, E])
        top = sb("top", [128, 2, 8])
        rest = sb("rest", [128, 2, E])
        sel = sb("sel", [128, 2, E], bf16)
        seen = sb("seen", [128, 2, E], bf16)
        ex = sb("ex", [128, 2, E])
        lsum = sb("lsum", [128, 2, 1])
        ntop = sb("ntop", [128, 2, 1])
        fits = sb("fits", [128, 2, E])
        code = sb("code", [128, 2, E])
        code8 = sb("code8", [128, 2, 8])
        none8 = sb("none8", [128, 2, 8])
        IDX = sb("IDX", [128, B, 8], i32)
        wide = P[:, :, :, :].rearrange("p u h l -> p (u h l)")
        xrT = sb("xrT", [128, 2, 128])
        TOK = sb("TOK", [128, B], i32)
        tok = sb("tok", [128, 2, 1], i32)
        where = sb("where", [128, 2, 8], i32)
        none = sb("none", [128, NPE], i32)
        GI = sb("GI", [128, NPE], i32)
        gidx = sb("gidx", [128, RING, 1], i32)
        XG = sb("XG", [128, RING, XW])
        XGT = sb("XGT", [128, 2, 2, 128])
        WGU = sb("WGU", [128, RING, 2, 2, 2 * FE])
        WD = sb("WD", [FE, RING, 2, D])
        TH = sb("TH", [128, 2, FE])
        HH = sb("HH", [128, 2, FE])
        HT = sb("HT", [FE, 2, 128])
        wslot = sb("wslot", [128, 2, 1])
        OS = sb("OS", [128, 2, D])
        cidx = sb("cidx", [128, 2, 8], i32)
        YG = NV[:, :].rearrange("p (u k d) -> p u k d", u=2, k=TOPK)
        YS = sb("YS", [128, 2, D])
        slots = nc.dram_tensor("slots", (128 * NPE, 1), i32, kind="Internal").ap()
        routed = nc.dram_tensor("routed", (B * S, XW), fp32, kind="Internal").ap()
        moe = nc.dram_tensor("moe", (E * CAP + 1, D), fp32, kind="Internal").ap()

        CB = [sb(f"CB{k}", [128, B, DC], bf16) for k in range(3)]
        CRST = cT[:, :, :].rearrange("p q n -> p (q n)").rearrange("p (b c) -> p b c", b=B)
        KZ = MID[:, 0:B * 4 * 3 * 6 * DH // 2].bitcast(bf16).rearrange(
            "p (b j z t d) -> p b j z t d", b=B, j=4, z=3, t=6)
        V1 = sb("V1", [128, 2, KV, 32])
        xq = sb("xq", [128, 2, D])
        ring = WGU[:, :, :, :, :].rearrange("p r e c n -> p (r e c n)").bitcast(bf16)
        folds = FB[:, :, :].rearrange("p u n -> p (u n)").bitcast(bf16)
        n6, nq, nk = G1 * KV * 6 * DH, 16 * 128, KV * 128
        Q6 = folds[:, 0:2 * n6].rearrange("p (u g k t d) -> p u g k t d", u=2, g=G1, k=KV, t=6)
        QT = ring[:, 0:2 * nq].rearrange("p (u a s) -> p u a s", u=2, a=16)
        KT = ring[:, 2 * nq:2 * nq + 2 * nk].rearrange("p (u k t) -> p u k t", u=2, k=KV)
        nm = sb("nm", [128, H1])
        M3 = sb("M3", [128, G1, 3, KV], bf16)
        PE1 = P[:, :, :, :].rearrange("p u h l -> p (u h l)").rearrange("p (k n) -> p k n", k=KV)
        OT = FA[:, :, :].rearrange("p u n -> p (u n)")[:, 0:1024].rearrange("p (h n) -> p h n", h=2)
        RD = sb("RD", [128, 2, G1, 4])
        OA = sb("OA", [128, D])

        W1F = wide[:, 0:4 * F1]
        W2F = PT[:, :, :].rearrange("p q n -> p (q n)")[:, 0:FT * D]
        W1 = sb("W1", [128, 2, 2, F1], bf16)
        W2 = sb("W2", [128, FT, D], bf16)
        scratch = qT[:, :, :, :].rearrange("p u h s -> p (u h s)")
        ones = sb("ones", [128, 128])
        magic = sb("magic", [128, 2])
        wsum = sb("wsum", [128, 3, 2])
        wmean = sb("wmean", [128, 3])
        wscale = sb("wscale", [128, 3])
        wdeq = sb("wdeq", [128, 3])
        XF = YS[:, 0, :]
        TG = wide[:, D:D + F1]
        HG = wide[:, D + F1:D + 3 * F1].rearrange("p (u n) -> p u n", u=2)
        XQ = sb("XQ", [128, 2, D], bf16)
        XQT = sb("XQT", [128, 2, 2, 128], bf16)
        xscale = sb("xscale", [128, 2, 4])
        hscale = sb("hscale", [128, 2, 3])
        HQ = sb("HQ", [128, F1], bf16)
        HQT = sb("HQT", [128, FT, 128], bf16)

        PS = es.enter_context(nc.psum_tensor("PS", [128, 8, 512], fp32))
        bank = [PS[:, i, :] for i in range(8)]

        ld_const = sem("ld_const"); ld_x = sem("ld_x"); ld_x2 = sem("ld_x2"); ld_ctx = sem("ld_ctx")
        ld_fa = [sem("ld_fa0"), sem("ld_fa1")]; ld_fb = [sem("ld_fb0"), sem("ld_fb1")]
        dve_own = sem("dve_own"); act_own = sem("act_own"); pool_own = sem("pool_own")
        held = sem("held")
        setup_done = sem("setup_done")
        fold_block = sem("fold_block"); fold_a1 = sem("fold_a1"); fold_a1_out = sem("fold_a1_out")
        fold_a2 = sem("fold_a2"); fold_a2_out = sem("fold_a2_out"); fold_n = sem("fold_n"); fold_v = sem("fold_v")
        fold_n_out = sem("fold_n_out"); fold_v_out = sem("fold_v_out")
        var_ready = sem("var_ready"); rstd_ready = sem("rstd_ready")
        xn_ready = sem("xn_ready"); xnT_psum = sem("xnT_psum"); xnT_ready = sem("xnT_ready")
        kd_ready = sem("kd_ready"); vd_ready = sem("vd_ready"); kdT_psum = sem("kdT_psum"); bd_ready = sem("bd_ready")
        q_psum = sem("q_psum"); qT_ready = sem("qT_ready")
        score_psum = sem("score_psum"); max_ready = sem("max_ready"); exp_ready = sem("exp_ready")
        prob_ready = sem("prob_ready"); pT_psum = sem("pT_psum"); pT_ready = sem("pT_ready")
        ctx_psum = sem("ctx_psum"); ctxT_ready = sem("ctxT_ready"); att_psum = sem("att_psum")
        x1_ready = sem("x1_ready")
        ld_gate = sem("ld_gate"); ld_w = [sem(f"ld_w{r}") for r in range(RING)]
        rT_psum = sem("rT_psum"); rT_ready = sem("rT_ready"); logit_psum = sem("logit_psum")
        var2_ready = sem("var2_ready"); rstd2_ready = sem("rstd2_ready"); rn_ready = sem("rn_ready")
        logit_read = sem("logit_read"); scattered = [sem("scattered0"), sem("scattered1")]
        none_ready = sem("none_ready"); cleared = sem("cleared")
        top_ready = sem("top_ready"); ex_ready = sem("ex_ready"); sel_ready = sem("sel_ready")
        place_psum = sem("place_psum"); place_read = sem("place_read")
        row_ready = sem("row_ready"); row_stored = [sem("row_stored0"), sem("row_stored1")]
        gi_ready = sem("gi_ready"); gathered = [sem(f"gathered{r}") for r in range(RING)]
        xg_psum = sem("xg_psum"); xg_ready = sem("xg_ready"); gu_psum = sem("gu_psum")
        tanh_ready = sem("tanh_ready"); h_ready = sem("h_ready"); hT_psum = sem("hT_psum")
        hT_ready = sem("hT_ready"); down_psum = sem("down_psum"); os_ready = sem("os_ready")
        os_stored = [sem("os_stored0"), sem("os_stored1")]; zero_ready = sem("zero_ready")
        zero_stored = sem("zero_stored"); idx_ready = sem("idx_ready")
        parts_ready = sem("parts_ready"); kz_ready = sem("kz_ready"); select_ready = sem("select_ready")
        v1_ready = sem("v1_ready")
        xq_ready = sem("xq_ready"); xr_ready = sem("xr_ready"); q6_copied = sem("q6_copied")
        ld_w12 = sem("ld_w12"); w2_cleared = sem("w2_cleared"); wsum_ready = sem("wsum_ready")
        wsum_psum = sem("wsum_psum"); wscale_ready = sem("wscale_ready"); wround_ready = sem("wround_ready")
        w_ready = sem("w_ready"); xqf_ready = sem("xqf_ready"); xqT_psum = sem("xqT_psum")
        xqT_ready = sem("xqT_ready"); gu1_psum = sem("gu1_psum"); gu1_read = sem("gu1_read")
        tg_ready = sem("tg_ready"); hscale_ready = sem("hscale_ready"); hround_ready = sem("hround_ready")
        hq_ready = sem("hq_ready"); hqT_psum = sem("hqT_psum")
        xmax_ready = sem("xmax_ready"); xfactor_ready = sem("xfactor_ready"); hfactor_ready = sem("hfactor_ready")
        hqT_ready = sem("hqT_ready"); down1_psum = sem("down1_psum"); y_ready = sem("y_ready")
        q6_ready = sem("q6_ready"); qt_psum = sem("qt_psum"); qt_ready = sem("qt_ready")
        kt_psum = sem("kt_psum"); kt_ready = sem("kt_ready"); a_psum = sem("a_psum"); a_read = sem("a_read")
        m3_ready = sem("m3_ready"); mt_psum = sem("mt_psum"); mt_ready = sem("mt_ready")
        b_psum = sem("b_psum"); e_ready = sem("e_ready"); pv_psum = sem("pv_psum"); ot_ready = sem("ot_ready")
        o_psum = sem("o_psum"); x3_ready = sem("x3_ready")
        yg_in = [sem("yg_in0"), sem("yg_in1")]; x2_ready = sem("x2_ready")
        stored = sem("stored")
        block = es.enter_context(nc.Block())

        def heads(row):
            return row.rearrange("p (k g d) -> p g k d", k=KV, g=G1)

        def hold(eng):
            eng.sem_inc(held, 1)

        def since(eng, signal, n):
            if not (isinstance(n, int) and n <= 0):
                eng.wait_ge(signal, n)

        def turn_has(b, *ahead):
            return [not isinstance(b, int) or 0 <= b + n < B for n in ahead]

        @block.sync
        def _(sp):
            sp.dma_start(CO[:, :], consts).then_inc(ld_const, 16)
            sp.dma_start(CT[:, :, :], ctx.rearrange("b s c -> s b c")).then_inc(ld_ctx, 16)
            for p in range(2):
                sp.dma_start(FA[:, p, :], fold_a[p]).then_inc(ld_fa[p], 16)
                sp.dma_start(FB[:, p, :], fold_b[p]).then_inc(ld_fb[p], 16)
            sp.wait_ge(w2_cleared, 1)
            sp.dma_start(W1F, w1.rearrange("p c n -> p (c n)")).then_inc(ld_w12, 16)
            for t in range(FT):
                rows = min(128, F1 - t * 128)
                sp.dma_start(W2F[0:rows, t * D:t * D + D], w2[t * 128:t * 128 + rows, :]).then_inc(ld_w12, 16)
            sp.wait_ge(none_ready, 1)
            sp.dma_start(slots.rearrange("(s n) o -> s (n o)", s=128), none[:, :]).then_inc(cleared, 16)
            with sp.Fori(0, NP0 // 2 - 1) as i:
                for u in range(2):
                    sp.wait_ge(fold_a2, i * 2 + u + 1)
                    sp.dma_start(FB[:, u, :], fold_b[i * 2 + u + 2]).then_inc(ld_fb[u], 16)
                    sp.wait_ge(fold_n, i * 2 + u + 1)
                    sp.dma_start(FA[:, u, :], fold_a[i * 2 + u + 2]).then_inc(ld_fa[u], 16)
            sp.dma_start(X[:, 0:4, :], x[0:4].rearrange("b s d -> s b d")).then_inc(ld_x, 16)
            sp.dma_start(X[:, 4:B, :], x[4:B].rearrange("b s d -> s b d")).then_inc(ld_x2, 16)
            sp.dma_start(GT[:, :, :], gate_t).then_inc(ld_gate, 16)
            for r in range(RING):
                sp.dma_start(WGU[:, r, :, :, :], wgu[r]).then_inc(ld_w[r], 16)
                sp.dma_start(WD[:, r, :, :], wd[r]).then_inc(ld_w[r], 16)
            with sp.Fori(0, B // 2) as i:
                for u in range(2):
                    sp.wait_ge(row_ready, i * 2 + u + 1)
                    sp.dma_start(routed[bass.ds((i * 2 + u) * S, S), :], XR[:, u, :]).then_inc(row_stored[u], 16)
            sp.wait_ge(scattered[0], B // 2 * 8 * 16)
            sp.wait_ge(scattered[1], B // 2 * 8 * 16)
            sp.dma_start(GI[:, :], slots.rearrange("(s n) o -> s (n o)", s=128)).then_inc(gi_ready, 16)
            sp.wait_ge(zero_ready, 1)
            sp.dma_start(moe[E * CAP:E * CAP + 1, :], YS[0:1, 0, :]).then_inc(zero_stored, 16)

            rows_out = moe[0:E * CAP, :].rearrange("(s n) d -> s n d", s=128)

            def store_slots(i, v):
                j = i * RING + v
                sp.wait_ge(os_ready, j + 1)
                sp.dma_start(rows_out[:, bass.ds(j, 1), :], OS[:, v % 2, :].unsqueeze(1)).then_inc(os_stored[v % 2], 16)

            with sp.Fori(0, NPE // RING - 1) as i:
                for v in range(RING):
                    store_slots(i, v)
                    sp.dma_start(WGU[:, v, :, :, :], wgu[(i + 1) * RING + v]).then_inc(ld_w[v], 16)
                    sp.dma_start(WD[:, v, :, :], wd[(i + 1) * RING + v]).then_inc(ld_w[v], 16)
            for v in range(RING):
                store_slots(NPE // RING - 1, v)
            with sp.Fori(0, B) as b:
                sp.wait_ge(y_ready, b + 1)
                sp.dma_start(out[b], X[:, b, :]).then_inc(stored, 16)
            sp.wait_ge(stored, 16 * B)

        @block.tensor
        def _(pe):
            mm = nc.tensor.matmul


            def fold_a1_of(p, u):
                pe.wait_ge(fold_block, p + 1)
                if p == 6:
                    pe.wait_ge(wscale_ready, 1)
                for c in range(2):
                    last = mm(bank[u][0:KC, c * 128:c * 128 + 128],
                              FB[:, u, 512 + c * KC:512 + c * KC + KC], KB[:, u, :], start=True, stop=True)
                last.then_inc(fold_a1, 1)

            def fold_a2_of(p, u):
                pe.wait_ge(fold_a1_out, p + 1)
                for h in range(2):
                    for c in range(2):
                        last = mm(bank[2 + u][:, h * 64:h * 64 + 64],
                                  FB[0:KC, u, (c * 2 + h) * 128:(c * 2 + h) * 128 + 128],
                                  A1[:, u, c, h * 64:h * 64 + 64], start=(c == 0), stop=(c == 1))
                last.then_inc(fold_a2, 1)

            def fold_v_of(p, u):
                pe.wait_ge(ld_fa[u], p * 8 + (16 - 8 * u))
                since(pe, fold_v_out, p - 1)
                for h in range(2):
                    last = mm(bank[6 + u][64 * h:64 * h + 64, 0:D], FA[:, u, 512 + h * 64:512 + h * 64 + 64],
                              FA[:, u, 640 + h * 256:640 + h * 256 + 256], start=True, stop=True)
                last.then_inc(fold_v, 1)

            def fold_n_of(p, u):
                pe.wait_ge(fold_a2_out, p + 1)
                since(pe, fold_n_out, p - 1)
                for c in range(2):
                    for h in range(2):
                        last = mm(bank[4 + u][:, c * 128 + h * 64:c * 128 + h * 64 + 64],
                                  FA[:, u, h * 256 + c * 128:h * 256 + c * 128 + 128], A2[:, u, h, :],
                                  start=True, stop=True)
                last.then_inc(fold_n, 1)

            def fold(p, u):
                if p > 0:
                    fold_n_of(p - 1, 1 - u)
                if p < NP0:
                    fold_v_of(p, u)
                    fold_a2_of(p, u)
                if p < NP0 - 1:
                    fold_a1_of(p + 1, 1 - u)

            pe.wait_ge(setup_done, 1)
            fold_a1_of(0, 0)
            for p in range(5):
                fold(p, p % 2)
            pe.wait_ge(wsum_ready, 1)
            pe.wait_ge(fold_a1_out, 5)
            mm(bank[0][:, 256:262], ones[:, :], wsum[:, :, :].rearrange("p w c -> p (w c)"),
               start=True, stop=True).then_inc(wsum_psum, 1)
            for p in range(5, NP0 + 1):
                fold(p, p % 2)

            def turn_rows(b, u):
                since(pe, logit_read, b - 3)
                pe.wait_ge(kd_ready, b + 1)
                nc.tensor.transpose(bank[7][:, 256:384], KD[:, u, :, :].rearrange("p a d -> p (a d)"),
                                    identf).then_inc(kdT_psum, 1)
                pe.wait_ge(xn_ready, b + 1)
                for c in range(2):
                    last = nc.tensor.transpose(bank[7][:, c * 128:c * 128 + 128], xn[:, u, c * 128:c * 128 + 128],
                                               identf)
                last.then_inc(xnT_psum, 1)

            def queries(b, u):
                pe.wait_ge(xnT_ready, b + 1)
                pe.wait_ge(bd_ready, b + 1)
                for q in range(2):
                    for p in range(4):
                        for c in range(2):
                            last = mm(bank[4 + q][:, p * 128:p * 128 + 128], N[:, c, q * 4 + p, :], xnT[:, u, c, :],
                                      start=(c == 0), stop=(c == 1))
                    last.then_inc(q_psum, 1)

            def scores(b, u, q):
                pe.wait_ge(qT_ready, b * 2 + q + 1)
                pe.wait_ge(bd_ready, b + 1)
                since(pe, exp_ready, b * 2 + q - 1)
                for p in range(4):
                    last = mm(bank[q * 2 + p // 2][:, (p % 2) * 256:(p % 2) * 256 + 256], qT[:, u, q * 4 + p, :],
                              BD[:, u, :, :].rearrange("p a l -> p (a l)"), start=True, stop=True)
                last.then_inc(score_psum, 1)

            def turn_probs(b, u, q, asked):
                pe.wait_ge(prob_ready, b * 2 + q + 1)
                for par in range(2):
                    if q == 1:
                        pe.wait_ge(pT_ready, b * 4 + par + 1)
                    elif asked:
                        pe.wait_ge(qT_ready, b * 2 + par + 5)
                    for p in range(4):
                        last = nc.tensor.transpose(bank[4 + par][:, p * 128:p * 128 + 128],
                                                   P[:, u, (q * 4 + p) * 2 + par, :], identf)
                    last.then_inc(pT_psum, 1)

            def contexts(b, u):
                pe.wait_ge(vd_ready, b + 1)
                for q in range(2):
                    pe.wait_ge(pT_ready, b * 4 + q + 3)
                    for par in range(2):
                        last = mm(bank[4 + q][64 * par:64 * par + 64, :], VD[:, u, :], PT[:, q * 2 + par, :],
                                  start=True, stop=True)
                    last.then_inc(ctx_psum, 1)

            def project(b):
                since(pe, x1_ready, b)
                since(pe, place_read, b - 1)
                for q in range(2):
                    pe.wait_ge(ctxT_ready, b * 2 + q + 1)
                    for p in range(4):
                        last = mm(bank[6][:, 0:D], cT[:, q, p * 128:p * 128 + 128], V[:, q * 4 + p, :],
                                  start=(q + p == 0), stop=(q * 4 + p == NP0 - 1))
                last.then_inc(att_psum, 1)

            def route_rows(b, u):
                pe.wait_ge(rn_ready, b + 1)
                for c in range(2):
                    last = nc.tensor.transpose(bank[7][:, c * 128:c * 128 + 128], XR[:, u, c * 128:c * 128 + 128],
                                               identf)
                last.then_inc(rT_psum, 1)

            def route_logits(b):
                pe.wait_ge(rT_ready, b + 1)
                for c in range(2):
                    last = mm(bank[7][:, 384:384 + E], xrT[:, c, :], GT[:, c, :], start=(c == 0), stop=(c == 1))
                last.then_inc(logit_psum, 1)

            def route_places(b, u):
                pe.wait_ge(sel_ready, b + 1)
                pe.wait_ge(x1_ready, min(b + 2, B) if isinstance(b, int) else b + 2)
                mm(bank[6][:, D:D + E], upb[:, :], sel[:, u, :], start=True, stop=False)
                mm(bank[6][:, D:D + E], onesb[:, :], seen[:, u, :], start=False, stop=True).then_inc(place_psum, 1)

            def attend(b, u):
                ask, back, rows, route, place = turn_has(b, 1, -1, 2, -2, -3)
                if ask:
                    queries(b + 1, 1 - u)
                if back:
                    turn_probs(b - 1, 1 - u, 0, ask)
                if ask:
                    scores(b + 1, 1 - u, 0)
                if back:
                    turn_probs(b - 1, 1 - u, 1, ask)
                if route:
                    route_rows(b - 2, u)
                if ask:
                    scores(b + 1, 1 - u, 1)
                if back:
                    contexts(b - 1, 1 - u)
                if place:
                    route_places(b - 3, 1 - u)
                if route:
                    route_logits(b - 2)
                if rows:
                    turn_rows(b + 2, u)
                if back:
                    project(b - 1)

            pe.wait_ge(ld_gate, 16)
            pe.wait_ge(fold_n_out, NP0)
            pe.wait_ge(fold_v_out, NP0)
            for b in range(-2, 4):
                attend(b, b % 2)
            with pe.Fori(2, B // 2 - 1) as i:
                for u in range(2):
                    attend(i * 2 + u, u)
            for b in range(B - 2, B + 3):
                attend(b, b % 2)

            pe.wait_ge(place_read, B)
            pe.wait_ge(logit_read, B)

            def expert_rows(i, v):
                u = v % 2
                pe.wait_ge(gathered[v], i * 16 + 16)
                for c in range(2):
                    last = nc.tensor.transpose(bank[u][:, c * 128:c * 128 + 128], XG[:, v, c * 128:c * 128 + 128],
                                               identf)
                last.then_inc(xg_psum, 1)

            def expert_up(i, v):
                j, u = i * RING + v, v % 2
                pe.wait_ge(xg_ready, j + 1)
                pe.wait_ge(ld_w[v], i * 32 + 32)
                for c in range(2):
                    for e in range(2):
                        last = mm(bank[2 + u][64 * e:64 * e + 64, 0:2 * FE], XGT[:, u, c, 64 * e:64 * e + 64],
                                  WGU[:, v, e, c, :], start=(c == 0), stop=(c == 1))
                last.then_inc(gu_psum, 1)

            def expert_turn(i, v):
                j, u = i * RING + v, v % 2
                pe.wait_ge(h_ready, j + 1)
                nc.tensor.transpose(bank[4 + u][0:FE, 0:128], HH[:, u, :], identf).then_inc(hT_psum, 1)

            def expert_down(i, v):
                j, u = i * RING + v, v % 2
                pe.wait_ge(hT_ready, j + 1)
                if not (isinstance(i, int) and j < 2):
                    pe.wait_ge(os_ready, j - 1)
                for e in range(2):
                    last = mm(bank[6 + u][64 * e:64 * e + 64, 0:D], HT[:, u, 64 * e:64 * e + 64], WD[:, v, e, :],
                              start=True, stop=True)
                last.then_inc(down_psum, 1)

            def expert_body(i, v):
                last = NPE - 1 - (i * RING + v) if isinstance(i, int) else NPE
                n1 = (i, v + 1) if v + 1 < RING else (i + 1, v + 1 - RING)
                n2 = (i, v + 2) if v + 2 < RING else (i + 1, v + 2 - RING)
                if last >= 1:
                    expert_up(*n1)
                expert_turn(i, v)
                if last >= 2:
                    expert_rows(*n2)
                expert_down(i, v)

            expert_rows(0, 0)
            expert_rows(0, 1)
            expert_up(0, 0)
            for v in range(RING):
                expert_body(0, v)
            with pe.Fori(1, NPE // RING - 1) as i:
                for v in range(RING):
                    expert_body(i, v)
            for v in range(RING):
                expert_body(NPE // RING - 1, v)

            def turn(b, u):
                pe.wait_ge(q6_ready, b + 1)
                pe.wait_ge(q6_copied, b + 1)
                since(pe, x3_ready, b - 2)
                for g in range(G1):
                    for j in range(4):
                        at = (g % 2 * 4 + j) * 128
                        last = nc.tensor.transpose(bank[6 + g // 2].bitcast(bf16)[0:KR1, at:at + 128],
                                                   Q6[:, u, g, 2 * j:2 * j + 2, :, :].rearrange("p k t d -> p (k t d)"),
                                                   identb[:, :])
                    if g % 2:
                        last.then_inc(qt_psum, 1)
                since(pe, a_read, b * 4 - 1)
                for kv in range(KV):
                    last = nc.tensor.transpose(bank[0].bitcast(bf16)[0:KR1, kv * 128:kv * 128 + 128],
                                               KZ[:, b, kv // 2, kv % 2:kv % 2 + 2, :, :]
                                               .rearrange("p z t d -> p (z t d)"),
                                               identb[:, :])
                last.then_inc(kt_psum, 1)

            def row_scores(b, u, g):
                if g == 0:
                    pe.wait_ge(qt_ready, b * 2 + 2)
                    pe.wait_ge(kt_ready, b + 1)
                if g == 1:
                    since(pe, mt_ready, b)
                since(pe, a_read, b * 4 + g - 1)
                for j in range(4):
                    last = mm(bank[g % 2 * 2 + j // 2][:, j % 2 * 256:j % 2 * 256 + 256], QT[0:KR1, u, g * 4 + j, :],
                              KT[0:KR1, u, 2 * j:2 * j + 2, :].rearrange("p k t -> p (k t)"), start=True, stop=True)
                last.then_inc(a_psum, 1)

            def turn_maxima(b):
                pe.wait_ge(m3_ready, b + 1)
                for g in range(G1):
                    last = nc.tensor.transpose(bank[3].bitcast(bf16)[0:3 * KV, g * 128:g * 128 + 128],
                                               M3[:, g, :, :].rearrange("p a k -> p (a k)"), identb[:, :])
                last.then_inc(mt_psum, 1)

            def column_scores(b, u, kv):
                since(pe, e_ready, b * 8 + kv - 1)
                mm(bank[4 + kv % 2], KT[0:KR1, u, kv, :],
                   QT[0:KR1, u, :, :].rearrange("p (g j) s -> p j g s", g=G1)[:, kv // 2, :, :],
                   start=True, stop=False)
                if kv == 0:
                    pe.wait_ge(mt_ready, b + 1)
                mm(bank[4 + kv % 2], KT[KR1:KM1, u, kv, :], QT[KR1:KM1, u, 0:4, :].rearrange("p g s -> p (g s)"),
                   start=False, stop=True).then_inc(b_psum, 1)

            def values(b, u, half, turned):
                if half == 0:
                    pe.wait_ge(v1_ready, b + 1)
                if turned:
                    pe.wait_ge(qt_ready, b * 2 + half + 5)
                else:
                    pe.wait_ge(x3_ready, b)
                for kv in range(4 * half, 4 * half + 4):
                    pe.wait_ge(e_ready, b * 8 + kv + 1)
                    last = mm(bank[6 + half][32 * (kv % 4):32 * (kv % 4) + 32, :], V1[:, u, kv, :],
                              PE1[:, kv, :], start=True, stop=True)
                last.then_inc(pv_psum, 1)

            def turn_back(b, half):
                pe.wait_ge(ot_ready, b * 2 + half + 1)
                for g in range(G1):
                    last = nc.tensor.transpose(bank[6 + half][:, g * 128:g * 128 + 128],
                                               OT[:, half, g * 128:g * 128 + 128], identf)
                last.then_inc(o_psum, 1)

            def attend1(b, u):
                rows, cols, back, new = turn_has(b, 1, 0, -1, 2)
                for step, k in [(row_scores, 0), (column_scores, 0), (column_scores, 1), (row_scores, 1),
                                (turn_back, 0), (column_scores, 2), (column_scores, 3), (turn_back, 1),
                                (column_scores, 4), (row_scores, 2), (column_scores, 5), (column_scores, 6),
                                (row_scores, 3), (column_scores, 7)]:
                    if step is row_scores and rows:
                        row_scores(b + 1, 1 - u, k)
                    if step is column_scores and cols:
                        column_scores(b, u, k)
                    if step is turn_back and back:
                        turn_back(b - 1, k)
                if new:
                    turn(b + 2, u)
                if cols:
                    values(b, u, 0, new)
                if rows:
                    turn_maxima(b + 1)
                if cols:
                    values(b, u, 1, new)

            pe.wait_ge(kz_ready, B)
            pe.wait_ge(select_ready, 1)
            for b in range(-2, 4):
                attend1(b, b % 2)
            with pe.Fori(2, B // 2 - 2) as i:
                for u in range(2):
                    attend1(i * 2 + u, u)
            for b in range(B - 4, B + 1):
                attend1(b, b % 2)

            pe.wait_ge(w_ready, 1)
            pe.wait_ge(x3_ready, B)

            def turn_rows(b, u):
                pe.wait_ge(xqf_ready, b + 1)
                for c in range(2):
                    last = nc.tensor.transpose(bank[6].bitcast(bf16)[:, c * 128:c * 128 + 128],
                                               XQ[:, u, c * 128:c * 128 + 128], identb[:, :])
                last.then_inc(xqT_psum, 1)

            def gate_up(b, u):
                pe.wait_ge(xqT_ready, b + 1)
                since(pe, gu1_read, b)
                for half in range(4):
                    for c in range(2):
                        last = mm(bank[half][:, 0:F1 // 2], XQT[:, u, c, :],
                                  W1[:, c, half // 2, half % 2 * (F1 // 2):half % 2 * (F1 // 2) + F1 // 2],
                                  start=(c == 0), stop=(c == 1))
                    if half % 2:
                        last.then_inc(gu1_psum, 1)

            def turn_hidden(b):
                pe.wait_ge(hq_ready, b + 1)
                for t in range(FT):
                    rows = min(128, F1 - t * 128)
                    last = nc.tensor.transpose(bank[4].bitcast(bf16)[0:rows, t * 128:t * 128 + 128],
                                               HQ[:, t * 128:t * 128 + rows], identb[:, :])
                last.then_inc(hqT_psum, 1)

            def down(b, u):
                pe.wait_ge(hqT_ready, b + 1)
                for t in range(FT):
                    rows = min(128, F1 - t * 128)
                    last = mm(bank[5 + 2 * u][:, 0:D], HQT[0:rows, t, :], W2[0:rows, t, :],
                              start=(t == 0), stop=(t == FT - 1))
                last.then_inc(down1_psum, 1)

            def feed(b, u):
                ask, back, rows, cur = turn_has(b, 1, -1, 2, 0)
                if ask:
                    gate_up(b + 1, 1 - u)
                if back:
                    down(b - 1, 1 - u)
                if rows:
                    turn_rows(b + 2, u)
                if cur:
                    turn_hidden(b)

            for b in range(-2, 2):
                feed(b, b % 2)
            with pe.Fori(1, B // 2 - 1) as i:
                for u in range(2):
                    feed(i * 2 + u, u)
            for b in range(B - 2, B + 1):
                feed(b, b % 2)

        @block.vector
        def _(dve):
            ch = Chain(dve, dve_own)
            link = ch.link
            dve.wait_ge(ld_const, 16)
            nc.vector.tensor_copy(identb[:, :], identf)
            nc.vector.memset(KB[:, :, :], 0.0)
            link(nc.vector.memset(BD[:, :, :, :], 0.0))
            nc.vector.memset(W2F[:, (FT - 1) * D:FT * D], 0.0).then_inc(w2_cleared, 1)
            nc.vector.memset(none[:, :], 0).then_inc(none_ready, 1)
            nc.vector.memset(ones[:, :], 1.0)
            nc.vector.memset(magic[:, 0:1], MAGIC)
            nc.vector.memset(magic[:, 1:2], -MAGIC)
            nc.vector.memset(seen[:, :, :], 0.0)
            nc.vector.tensor_copy(upb[:, :], CO[:, C_UP:C_UP + 128])
            nc.vector.memset(onesb[:, :], 1.0)
            nc.vector.memset(YS[:, :, :], 0.0).then_inc(zero_ready, 1)
            nc.vector.memset(negroot[:, :], -0.5).then_inc(setup_done, 1)

            def block_of(p, u):
                dve.wait_ge(ld_fb[u], p * 8 + (16 - 8 * u))
                since(dve, fold_a1, p - 1)
                for h in range(2):
                    ins = nc.vector.tensor_copy(KB[64 * h:64 * h + 64, u, 64 * h:64 * h + 64],
                                                FB[64 * h:64 * h + 64, u, 704:768])
                ins.then_inc(fold_block, 1)

            def n_of(p, u):
                dve.wait_ge(fold_n, p + 1)
                nc.vector.tensor_copy(N[:, :, p, :], bank[4 + u][:, 0:256].rearrange("p (c n) -> p c n", c=2)
                                      ).then_inc(fold_n_out, 1)

            def fold(p, u):
                if p > 0:
                    n_of(p - 1, 1 - u)
                if p < NP0 - 1:
                    block_of(p + 1, 1 - u)
                if p < NP0:
                    dve.wait_ge(fold_a2, p + 1)
                    nc.vector.tensor_copy(A2[:, u, :, :].rearrange("p h d -> p (h d)"),
                                          bank[2 + u][:, 0:128]).then_inc(fold_a2_out, 1)

            block_of(0, 0)
            for p in range(5):
                fold(p, p % 2)
            dve.wait_ge(wsum_psum, 1)
            link(nc.vector.tensor_reduce(wmean[:, :], bank[0][:, 256:262].rearrange("p (w c) -> p w c", c=2),
                                         AX.X, ALU.add))
            link(nc.vector.tensor_scalar(wmean[:, :], wmean[:, :], 1.0 / (F1 * D), EPS, ALU.mult, ALU.max))
            link(nc.vector.tensor_scalar(wdeq[:, 0:1], wmean[:, 0:1], 0.5 / 127.0, None, ALU.mult))
            nc.vector.tensor_scalar(wdeq[:, 1:2], wmean[:, 1:2], wdeq[:, 0:1], 1.0 / 127.0, ALU.mult, ALU.mult)
            nc.vector.tensor_scalar(wdeq[:, 2:3], wmean[:, 2:3], 1.0 / 127.0, None, ALU.mult)
            nc.vector.reciprocal(wscale[:, :], wmean[:, :]).then_inc(wscale_ready, 1)
            for p in range(5, NP0 + 1):
                fold(p, p % 2)

            def stats(b, u, signal=var_ready):
                link(nc.vector.bn_stats(st[:, u, :], X[:, b, :]))
                hold(dve)
                link(nc.vector.bn_aggr(mv[:, u, :], st[:, u, :]))
                nc.vector.tensor_scalar(veps[:, u, :], mv[:, u, 1:2], EPS, None, ALU.add).then_inc(signal, 1)

            def normed(b, u):
                dve.wait_ge(rstd_ready, b + 1)
                nc.vector.tensor_scalar(xn[:, u, :], X[:, b, :], mv[:, u, 0:1], rstd[:, u, :],
                                        ALU.subtract, ALU.mult).then_inc(xn_ready, 1)

            def probs_turned(b, q):
                for g in range(2 * q, 2 * q + 2):
                    dve.wait_ge(pT_psum, b * 4 + g + 1)
                    nc.vector.tensor_copy(PT[:, g, :], bank[4 + g % 2][:, :]).then_inc(pT_ready, 1)

            def add_attention(b):
                dve.wait_ge(att_psum, b + 1)
                nc.vector.tensor_tensor(X[:, b, :], X[:, b, :], bank[6][:, 0:D], ALU.add).then_inc(x1_ready, 1)

            def normalise(b, u, q):
                dve.wait_ge(exp_ready, b * 2 + q + 1)
                link(nc.vector.reciprocal(rden[:, u, q * 8:q * 8 + 8], den[:, u, q * 8:q * 8 + 8]))
                nc.vector.tensor_tensor(P[:, u, q * 8:q * 8 + 8, :], P[:, u, q * 8:q * 8 + 8, :],
                                        rden[:, u, q * 8:q * 8 + 8].unsqueeze(2).to_broadcast([128, 8, 128]),
                                        ALU.mult).then_inc(prob_ready, 1)

            def maxima(b, u, q):
                dve.wait_ge(score_psum, b * 2 + q + 1)
                for k in range(2):
                    ins = nc.vector.tensor_reduce(
                        nmx[:, u, q * 8 + k * 4:q * 8 + k * 4 + 4],
                        bank[q * 2 + k][:, :].rearrange("p (h l) -> p h l", h=4), AX.X, ALU.max, negate=True)
                ins.then_inc(max_ready, 1)

            def route_normed(b, u):
                dve.wait_ge(rstd2_ready, b + 1)
                since(dve, row_stored[u], b * 8 - 8 * u)
                nc.vector.tensor_scalar(XR[:, u, 0:D], X[:, b, :], mv[:, 2, 0:1], rstd[:, 2, :],
                                        ALU.subtract, ALU.mult).then_inc(rn_ready, 1)

            def read_logits(b, u):
                dve.wait_ge(logit_psum, b + 1)
                nc.vector.tensor_copy(LG[:, u, :], bank[7][:, 384:384 + E]).then_inc(logit_read, 1)

            def choose(b, u):
                dve.wait_ge(logit_read, b + 1)
                hold(dve)
                link(nc.vector.max(top[:, u, :], LG[:, u, :]))
                hold(dve)
                nc.vector.match_replace(rest[:, u, :], top[:, u, :], LG[:, u, :], -3.0e38)
                link(nc.vector.tensor_scalar(ntop[:, u, :], top[:, u, 0:1], -1.0, None, ALU.mult))
                dve.sem_inc(top_ready, 1)
                link(nc.vector.tensor_tensor(sel[:, u, :], rest[:, u, :], LG[:, u, :], ALU.not_equal))
                nc.vector.tensor_tensor(seen[:, 1 - u, :], seen[:, u, :], sel[:, u, :], ALU.add).then_inc(sel_ready, 1)

            def weigh(b, u):
                dve.wait_ge(ex_ready, b + 1)
                link(nc.vector.scalar_tensor_tensor(ex[:, u, :], ex[:, u, :], 1.0, sel[:, u, :], ALU.mult, ALU.mult,
                                                    accum_out=lsum[:, u, :]))
                link(nc.vector.reciprocal(lsum[:, u, :], lsum[:, u, :]))
                nc.vector.tensor_scalar(XR[:, u, D:XW], ex[:, u, :], lsum[:, u, :], None,
                                        ALU.mult).then_inc(row_ready, 1)

            def read_places(b, u):
                dve.wait_ge(place_psum, b + 1)
                nc.vector.scalar_tensor_tensor(fits[:, u, :], bank[6][:, D:D + E], float(CAP), sel[:, u, :],
                                               ALU.is_lt, ALU.mult)
                nc.vector.scalar_tensor_tensor(code[:, u, :], bank[6][:, D:D + E], float(NPE),
                                               CO[:, C_ECODE:C_ECODE + E], ALU.mult, ALU.add).then_inc(place_read, 1)

            def places(b, u):
                dve.wait_ge(place_read, b + 1)
                link(nc.vector.tensor_tensor(code[:, u, :], code[:, u, :], fits[:, u, :], ALU.mult))
                hold(dve)
                link(nc.vector.max(code8[:, u, :], code[:, u, :]))
                link(nc.vector.tensor_scalar(none8[:, u, :], code8[:, u, :], 0.0, float(E * CAP + 1),
                                             ALU.is_equal, ALU.mult))
                nc.vector.scalar_tensor_tensor(IDX[:, b, :], code8[:, u, :], -1.0, none8[:, u, :], ALU.add,
                                               ALU.add).then_inc(idx_ready, 1)

            def attend(b, u):
                added, cur, first, rows, back, ask, place = turn_has(b, -2, 0, 3, 2, -1, 1, -3)
                if added:
                    add_attention(b - 2)
                    dve.wait_ge(x1_ready, b - 1)
                    hold(dve)
                    stats(b - 2, 2, var2_ready)
                if cur:
                    normalise(b, u, 0)
                if back:
                    probs_turned(b - 1, 0)
                if first:
                    stats(b + 3, 1 - u)
                if added:
                    route_normed(b - 2, u)
                if cur:
                    normalise(b, u, 1)
                if rows:
                    normed(b + 2, u)
                if back:
                    probs_turned(b - 1, 1)
                if ask:
                    maxima(b + 1, 1 - u, 0)
                if place:
                    read_places(b - 3, 1 - u)
                if added:
                    read_logits(b - 2, u)
                if ask:
                    maxima(b + 1, 1 - u, 1)
                if place:
                    weigh(b - 3, 1 - u)
                    places(b - 3, 1 - u)
                if added:
                    choose(b - 2, u)

            dve.wait_ge(ld_x, 16)
            for b in (-3, -2):
                attend(b, b % 2)
            dve.wait_ge(wround_ready, 1)
            nc.vector.tensor_scalar(W1F, W1F, MAGIC, 1.0, ALU.subtract, ALU.min)
            link(nc.vector.tensor_scalar(W2F, W2F, MAGIC, 1.0, ALU.subtract, ALU.min))
            nc.vector.tensor_scalar(W1[:, :, :, :].rearrange("p c w n -> p (c w n)"), W1F, -1.0, None, ALU.max)
            link(nc.vector.tensor_scalar(W2[:, :, :].rearrange("p t n -> p (t n)"), W2F, -1.0, None, ALU.max))
            dve.sem_inc(w_ready, 1)
            dve.wait_ge(ld_x2, 16)
            for b in range(-1, 4):
                attend(b, b % 2)
            with dve.Fori(2, B // 2 - 2) as i:
                ch.enter(i - 2, 28)
                for u in range(2):
                    attend(i * 2 + u, u)
                ch.leave(B // 2 - 4)
            for b in range(B - 4, B + 3):
                attend(b, b % 2)

            def hidden(i, v):
                j, u = i * RING + v, v % 2
                dve.wait_ge(gathered[v], i * 16 + 16)
                for e in range(2):
                    w = XG[64 * e:64 * e + 64, v, bass.ds(j * 2 + D + e, 1)]
                    nc.vector.tensor_scalar(wslot[64 * e:64 * e + 64, u, :], w, 0.5, None, ALU.mult)
                dve.wait_ge(tanh_ready, j + 1)
                link(nc.vector.scalar_tensor_tensor(TH[:, u, :], TH[:, u, :], 1.0, bank[2 + u][:, 0:FE],
                                                    ALU.add, ALU.mult))
                nc.vector.scalar_tensor_tensor(HH[:, u, :], TH[:, u, :], wslot[:, u, :], bank[2 + u][:, FE:2 * FE],
                                               ALU.mult, ALU.mult).then_inc(h_ready, 1)

            def slots_out(i, v):
                j, u = i * RING + v, v % 2
                dve.wait_ge(down_psum, j + 1)
                if not (isinstance(i, int) and j < 2):
                    dve.wait_ge(os_stored[u], i * (RING // 2 * 16) + v // 2 * 16)
                nc.vector.tensor_copy(OS[:, u, :], bank[6 + u][:, 0:D]).then_inc(os_ready, 1)

            def expert_body(i, v, nxt):
                n = (i, v + 1) if v + 1 < RING else (i + 1, 0)
                if nxt:
                    hidden(*n)
                slots_out(i, v)

            hidden(0, 0)
            for v in range(RING):
                expert_body(0, v, True)
            with dve.Fori(1, NPE // RING - 1) as i:
                ch.enter(i - 1, RING)
                for v in range(RING):
                    expert_body(i, v, True)
                ch.leave(NPE // RING - 2)
            for v in range(RING):
                expert_body(NPE // RING - 1, v, v + 1 < RING)

            for u in range(2):
                ins = nc.vector.tensor_copy(KT[KR1:KM1, u, :, :],
                                            CO[KR1:KM1, C_KV:C_KV + KV].unsqueeze(2).to_broadcast([3 * KV, KV, 128]))
            ins.then_inc(select_ready, 1)

            def maxima1(b, g):
                dve.wait_ge(a_psum, b * 4 + g + 1)
                nc.vector.tensor_reduce(nm[:, g * KV:g * KV + KV],
                                        PS[:, g % 2 * 2:g % 2 * 2 + 2, :].rearrange("p a (k t) -> p (a k) t", t=128),
                                        AX.X, ALU.max, negate=True).then_inc(a_read, 1)

            def denominators(b):
                for half in range(2):
                    dve.wait_ge(o_psum, b * 2 + half + 1)
                    o = bank[6 + half].rearrange("p (g k c) -> p g k c", g=G1, k=4)
                    ins = nc.vector.reciprocal(RD[:, half, :, :], o[:, :, :, DH])
                return ch.mark(ins)

            def outputs():
                for half in range(2):
                    o = bank[6 + half].rearrange("p (g k c) -> p g k c", g=G1, k=4)
                    ins = nc.vector.tensor_tensor(
                        OA[:, half * 128:half * 128 + 128].rearrange("p (k g d) -> p g k d", k=4, g=G1),
                        o[:, :, :, 0:DH], RD[:, half, :, :].unsqueeze(3).to_broadcast([128, G1, 4, DH]), ALU.mult)
                return ch.mark(ins)

            def third_part(v):
                nc.vector.tensor_tensor(Q6[:, v, :, :, 2, :], heads(xq[:, 1, :]), Q6[:, v, :, :, 1, :],
                                        ALU.subtract).then_inc(q6_ready, 1)

            def attend1(b, u):
                rows, back, query, new = turn_has(b, 1, -1, 3, 4)
                mark, reach = ch.mark, ch.reach
                v = 1 - u
                if rows:
                    maxima1(b + 1, 0)
                if query:
                    dve.wait_ge(x2_ready, b + 4)
                    hold(dve)
                    var = mark(nc.vector.bn_stats(st[:, v, :], X[:, b + 3, :]))
                if rows:
                    maxima1(b + 1, 1)
                if query:
                    reach(var)
                    hold(dve)
                    var = mark(nc.vector.bn_aggr(mv[:, v, :], st[:, v, :]))
                if back:
                    shares = denominators(b - 1)
                if query:
                    reach(var)
                    nc.vector.tensor_scalar(veps[:, v, :], mv[:, v, 1:2], EPS, None, ALU.add).then_inc(var_ready, 1)
                if back:
                    reach(shares)
                    shares = outputs()
                if rows:
                    maxima1(b + 1, 2)
                if back:
                    reach(shares)
                    nc.vector.tensor_tensor(X[:, b - 1, :], X[:, b - 1, :], OA[:, :], ALU.add).then_inc(x3_ready, 1)
                if rows:
                    maxima1(b + 1, 3)
                q6 = Q6[:, v]
                n = nm[:, :].rearrange("p (g k) -> p g k", g=G1)
                if rows:
                    dve.wait_ge(a_read, b * 4 + 8)
                    m1 = mark(nc.vector.tensor_copy(M3[:, :, 0, :], n))
                if query:
                    since(dve, q6_copied, b + 3)
                    dve.wait_ge(rstd_ready, b + (B + 4))
                    nc.vector.tensor_scalar(xq[:, 0, :], X[:, b + 3, :], mv[:, 1 - u, 0:1], rstd[:, 1 - u, :],
                                            ALU.subtract, ALU.mult).then_inc(xq_ready, 1)
                if rows:
                    reach(m1)
                    m1 = mark(nc.vector.tensor_tensor(n, n, M3[:, :, 0, :], ALU.subtract))
                if query:
                    dve.wait_ge(xq_ready, b + 4)
                    q1 = mark(nc.vector.tensor_copy(q6[:, :, :, 0, :], heads(xq[:, 0, :])))
                if rows:
                    reach(m1)
                    m1 = mark(nc.vector.tensor_copy(M3[:, :, 1, :], n))
                if query:
                    reach(q1)
                    nc.vector.tensor_tensor(heads(xq[:, 1, :]), heads(xq[:, 0, :]), q6[:, :, :, 0, :],
                                            ALU.subtract).then_inc(xr_ready, 1)
                if rows:
                    reach(m1)
                    nc.vector.tensor_tensor(M3[:, :, 2, :], n, M3[:, :, 1, :], ALU.subtract).then_inc(m3_ready, 1)
                if query:
                    dve.wait_ge(xr_ready, b + 4)
                    q1 = mark(nc.vector.tensor_copy(q6[:, :, :, 1, :], heads(xq[:, 1, :])))
                early = isinstance(b, int) and b < 0
                if query and early:
                    reach(q1)
                    third_part(v)
                if new:
                    dve.wait_ge(yg_in[u], b * 64 + (384 - 64 * u))
                    total = mark(nc.vector.tensor_reduce(YS[:, u, :], YG[:, u, :, :].rearrange("p k d -> p d k"),
                                                         AX.X, ALU.add))
                if query and not early:
                    reach(q1)
                    third_part(v)
                if new:
                    reach(total)
                    nc.vector.tensor_tensor(X[:, b + 4, :], X[:, b + 4, :], YS[:, u, :], ALU.add).then_inc(x2_ready, 1)

            for b in range(-4, 2):
                attend1(b, b % 2)
            with dve.Fori(1, B // 2 - 2) as i:
                ch.enter(i - 1, 20)
                for u in range(2):
                    attend1(i * 2 + u, u)
                ch.leave(B // 2 - 3)
            for b in range(B - 4, B):
                attend1(b, b % 2)

            halves = TG[:, :].rearrange("p (a n) -> p a n", a=2)

            def tanh_up(b):
                dve.wait_ge(tg_ready, b + 1)
                return ch.mark(nc.vector.scalar_tensor_tensor(halves, halves, 1.0, PS[:, 0:2, 0:F1 // 2],
                                                              ALU.add, ALU.mult))

            def products(b, u):
                dve.wait_ge(gu1_psum, b * 2 + 2)
                nc.vector.tensor_tensor(HG[:, u, :].rearrange("p (a n) -> p a n", a=2), halves,
                                        PS[:, 2:4, 0:F1 // 2], ALU.mult).then_inc(gu1_read, 1)

            def add_down(b, u):
                dve.wait_ge(down1_psum, b + 1)
                dve.wait_ge(hfactor_ready, b + 1)
                nc.vector.scalar_tensor_tensor(X[:, b, :], bank[5 + 2 * u][:, 0:D], hscale[:, u, 2:3], X[:, b, :],
                                               ALU.mult, ALU.add).then_inc(y_ready, 1)

            def feed(b, u):
                cur, back, rows, more, ask = turn_has(b, 0, -2, 2, 3, 1)
                xs, hs = xscale[:, u, :], hscale[:, u, :]
                mark, reach = ch.mark, ch.reach
                if back:
                    add_down(b - 2, u)
                if cur:
                    dve.wait_ge(gu1_read, b + 1)
                    top1 = mark(nc.vector.tensor_reduce(hs[:, 0:1], HG[:, u, :], AX.X, ALU.max,
                                                        apply_absolute_value=True))
                if rows:
                    dve.wait_ge(rstd_ready, 2 * B + 3 + b)
                    norm = mark(nc.vector.tensor_scalar(XF[:, :], X[:, b + 2, :], mv[:, u, 0:1], rstd[:, u, :],
                                                        ALU.subtract, ALU.mult))
                if cur:
                    reach(top1)
                    dve.wait_ge(xfactor_ready, b + 1)
                    top1 = mark(nc.vector.tensor_scalar(hs[:, 0:1], hs[:, 0:1], xs[:, 3:4], EPS, ALU.mult, ALU.max))
                if rows:
                    reach(norm)
                    top0 = mark(nc.vector.tensor_reduce(xs[:, 0:1], XF[:, :], AX.X, ALU.max,
                                                        apply_absolute_value=True))
                if cur:
                    reach(top1)
                    inv1 = mark(nc.vector.reciprocal(hs[:, 1:2], hs[:, 0:1]))
                if rows:
                    reach(top0)
                    top0 = mark(nc.vector.tensor_scalar(xs[:, 0:1], xs[:, 0:1], EPS, None, ALU.max))
                if cur:
                    reach(inv1)
                    nc.vector.tensor_scalar(hs[:, 1:2], hs[:, 1:2], xs[:, 3:4], 127.0, ALU.mult,
                                            ALU.mult).then_inc(hscale_ready, 1)
                if rows:
                    reach(top0)
                    nc.vector.reciprocal(xs[:, 1:2], xs[:, 0:1]).then_inc(xmax_ready, 1)
                if more:
                    var = mark(nc.vector.bn_stats(st[:, 1 - u, :], X[:, b + 3, :]))
                if rows:
                    dve.wait_ge(xmax_ready, b + 3)
                    inv0 = mark(nc.vector.tensor_scalar(xs[:, 1:2], xs[:, 1:2], 127.0, None, ALU.mult))
                if more:
                    reach(var)
                    hold(dve)
                    var = mark(nc.vector.bn_aggr(mv[:, 1 - u, :], st[:, 1 - u, :]))
                if rows:
                    reach(inv0)
                    norm = mark(nc.vector.tensor_scalar(XF[:, :], XF[:, :], xs[:, 1:2], MAGIC, ALU.mult, ALU.add))
                if more:
                    reach(var)
                    nc.vector.tensor_scalar(veps[:, 1 - u, :], mv[:, 1 - u, 1:2], EPS, None,
                                            ALU.add).then_inc(var_ready, 1)
                if ask:
                    summed = tanh_up(b + 1)
                if rows:
                    reach(norm)
                    nc.vector.tensor_scalar(XQ[:, u, :], XF[:, :], MAGIC, None, ALU.subtract).then_inc(xqf_ready, 1)
                if ask:
                    reach(summed)
                    products(b + 1, 1 - u)

            dve.wait_ge(x3_ready, B - 1)
            hold(dve)
            for b in (-3, -2):
                feed(b, b % 2)
            attend1(B, 0)
            dve.wait_ge(x3_ready, B)
            hold(dve)
            for b in range(-1, 2):
                feed(b, b % 2)
            with dve.Fori(1, B // 2 - 2) as i:
                ch.enter(i - 1, 22)
                for u in range(2):
                    feed(i * 2 + u, u)
                ch.leave(B // 2 - 3)
            for b in range(B - 4, B + 2):
                feed(b, b % 2)

        @block.scalar
        def _(act):
            def fold(p):
                if p < NP0:
                    act.wait_ge(fold_v, p + 1)
                    nc.scalar.copy(V[:, p, :], bank[6 + p % 2][:, 0:D]).then_inc(fold_v_out, 1)
                if p < NP0 - 1:
                    a1_of(p + 1)

            def a1_of(p):
                act.wait_ge(fold_a1, p + 1)
                nc.scalar.copy(A1[:, p % 2, :, :].rearrange("p c n -> p (c n)"),
                               bank[p % 2][0:KC, 0:256]).then_inc(fold_a1_out, 1)

            pieces = [(w, c, W1F[:, (c * 2 + w) * F1:(c * 2 + w) * F1 + F1]) for c in range(2) for w in range(2)]
            pieces += [(2, c, W2F[:, c * FT * D // 2:(c + 1) * FT * D // 2]) for c in range(2)]
            a1_of(0)
            for p in range(NP0):
                fold(p)
                for n in range(6):
                    w, c, piece = pieces[n]
                    if n // 2 == p - 1:
                        if n == 0:
                            act.wait_ge(ld_w12, 16 + 16 * FT)
                        nc.scalar.activation(scratch[:, 0:piece.shape[-1]], piece, ACT.Abs,
                                             accum_out=wsum[:, w, c:c + 1]).then_inc(act_own, 1)
                        act.wait_ge(act_own, n + 1)
                        if n == 5:
                            act.sem_inc(wsum_ready, 1)
                    if n // 2 == p - 5:
                        if n == 0:
                            act.wait_ge(wscale_ready, 1)
                        ins = nc.scalar.activation(piece, piece, ACT.Identity, scale=wscale[:, w:w + 1],
                                                   bias=magic[:, 0:1])
            ins.then_inc(wround_ready, 1)

            def rows_turned(b, u):
                act.wait_ge(xnT_psum, b + 1)
                nc.scalar.copy(xnT[:, u, :, :].rearrange("p c s -> p (c s)"),
                               bank[7][:, 0:256]).then_inc(xnT_ready, 1)
                for h in range(2):
                    ins = nc.scalar.copy(BD[64 * h:64 * h + 64, u, h, :], bank[7][64 * h:64 * h + 64, 256:384])
                ins.then_inc(bd_ready, 1)

            def queries(b, u):
                for q in range(2):
                    act.wait_ge(q_psum, b * 2 + q + 1)
                    nc.scalar.copy(qT[:, u, q * 4:q * 4 + 4, :].rearrange("p h s -> p (h s)"),
                                   bank[4 + q][:, :]).then_inc(qT_ready, 1)

            def exps(b, u, q):
                if isinstance(b, int) and b == 0:
                    act.wait_ge(w_ready, 1)
                act.wait_ge(max_ready, b * 2 + q + 1)
                for h in range(q * 8, q * 8 + 8):
                    ins = nc.scalar.activation(P[:, u, h, :], bank[h // 4][:, (h % 4) * 128:(h % 4) * 128 + 128],
                                               ACT.Exp, bias=nmx[:, u, h:h + 1], accum_out=den[:, u, h:h + 1])
                ins.then_inc(exp_ready, 1)

            def contexts(b):
                for q in range(2):
                    act.wait_ge(ctx_psum, b * 2 + q + 1)
                    nc.scalar.copy(cT[:, q, :], bank[4 + q][:, :]).then_inc(ctxT_ready, 1)

            def route_turned(b):
                act.wait_ge(rT_psum, b + 1)
                nc.scalar.copy(xrT[:, :, :].rearrange("p c s -> p (c s)"), bank[7][:, 0:256]).then_inc(rT_ready, 1)

            def route_exp(b, u):
                act.wait_ge(top_ready, b + 1)
                nc.scalar.activation(ex[:, u, :], LG[:, u, :], ACT.Exp, bias=ntop[:, u, :]).then_inc(ex_ready, 1)

            def attend(b, u):
                ask, back, rows, routed = turn_has(b, 1, -1, 2, -2)
                if ask:
                    queries(b + 1, 1 - u)
                if routed:
                    route_turned(b - 2)
                if back:
                    contexts(b - 1)
                if ask:
                    exps(b + 1, 1 - u, 0)
                if rows:
                    rows_turned(b + 2, u)
                if ask:
                    exps(b + 1, 1 - u, 1)
                if routed:
                    route_exp(b - 2, u)

            for b in range(-2, 2):
                attend(b, b % 2)
            with act.Fori(1, B // 2 - 1) as i:
                for u in range(2):
                    attend(i * 2 + u, u)
            for b in range(B - 2, B + 2):
                attend(b, b % 2)

            def rows(j, u):
                act.wait_ge(xg_psum, j + 1)
                nc.scalar.copy(XGT[:, u, :, :].rearrange("p c s -> p (c s)"),
                               bank[u][:, 0:256]).then_inc(xg_ready, 1)

            def tanh(j, u):
                act.wait_ge(gu_psum, j + 1)
                nc.scalar.activation(TH[:, u, :], bank[2 + u][:, 0:FE], ACT.Tanh, scale=0.5).then_inc(tanh_ready, 1)

            def turned(j, u):
                act.wait_ge(hT_psum, j + 1)
                nc.scalar.copy(HT[:, u, :], bank[4 + u][0:FE, 0:128]).then_inc(hT_ready, 1)

            rows(0, 0)
            rows(1, 1)
            tanh(0, 0)
            with act.Fori(0, NPE // 2 - 1) as i:
                for v in range(2):
                    tanh(i * 2 + v + 1, 1 - v)
                    turned(i * 2 + v, v)
                    rows(i * 2 + v + 2, v)
            tanh(NPE - 1, 1)
            turned(NPE - 2, 0)
            turned(NPE - 1, 1)

            def copy_queries(b, u):
                act.wait_ge(xq_ready, b + 1)
                for g in range(G1):
                    nc.scalar.copy(Q6[:, u, g, :, 3:6:2, :],
                                   heads(xq[:, 0, :])[:, g].unsqueeze(2).to_broadcast([128, KV, 2, DH]))
                act.wait_ge(xr_ready, b + 1)
                nc.scalar.copy(Q6[:, u, :, :, 4, :], heads(xq[:, 1, :])).then_inc(q6_copied, 1)

            def turned(b, u):
                for q in range(2):
                    act.wait_ge(qt_psum, b * 2 + q + 1)
                    nc.scalar.copy(QT[0:KR1, u, q * 8:q * 8 + 8, :].rearrange("p a s -> p (a s)"),
                                   bank[6 + q].bitcast(bf16)[0:KR1, :]).then_inc(qt_ready, 1)
                act.wait_ge(kt_psum, b + 1)
                nc.scalar.copy(KT[0:KR1, u, :, :].rearrange("p k t -> p (k t)"),
                               bank[0].bitcast(bf16)[0:KR1, :]).then_inc(kt_ready, 1)

            def turned_maxima(b, u):
                act.wait_ge(mt_psum, b + 1)
                nc.scalar.copy(QT[KR1:KM1, u, 0:G1, :].rearrange("p g s -> p (g s)"),
                               bank[3].bitcast(bf16)[0:3 * KV, 0:G1 * 128]).then_inc(mt_ready, 1)

            def attend1(b, u):
                cols, new, rows, copied = turn_has(b, 0, 2, 1, 3)
                if cols:
                    for kv in range(KV):
                        act.wait_ge(b_psum, b * 8 + kv + 1)
                        nc.scalar.activation(PE1[:, kv, :], bank[4 + kv % 2], ACT.Exp,
                                             scale=SCALE1).then_inc(e_ready, 1)
                if new:
                    turned(b + 2, u)
                if rows:
                    turned_maxima(b + 1, 1 - u)
                if copied:
                    copy_queries(b + 3, 1 - u)
                if cols:
                    for half in range(2):
                        act.wait_ge(pv_psum, b * 2 + half + 1)
                        nc.scalar.copy(OT[:, half, :], bank[6 + half]).then_inc(ot_ready, 1)

            for b in range(-3, 2):
                attend1(b, b % 2)
            with act.Fori(1, B // 2 - 2) as i:
                for u in range(2):
                    attend1(i * 2 + u, u)
            for b in range(B - 4, B):
                attend1(b, b % 2)

            def rows_turned(b, u):
                act.wait_ge(xqT_psum, b + 1)
                nc.scalar.copy(XQT[:, u, :, :].rearrange("p c s -> p (c s)"),
                               bank[6].bitcast(bf16)[:, 0:256]).then_inc(xqT_ready, 1)

            def hidden_turned(b):
                act.wait_ge(hqT_psum, b + 1)
                nc.scalar.copy(HQT[:, 0:FT - 1, :].rearrange("p t s -> p (t s)"),
                               bank[4].bitcast(bf16)[:, 0:(FT - 1) * 128])
                nc.scalar.copy(HQT[0:F1 % 128, FT - 1, :],
                               bank[4].bitcast(bf16)[0:F1 % 128, (FT - 1) * 128:FT * 128]).then_inc(hqT_ready, 1)

            def gate_tanh(b, u):
                act.wait_ge(gu1_psum, b * 2 + 1)
                act.wait_ge(xfactor_ready, b + 1)
                nc.scalar.activation(TG[:, :].rearrange("p (a n) -> p a n", a=2), PS[:, 0:2, 0:F1 // 2], ACT.Tanh,
                                     scale=xscale[:, u, 2:3]).then_inc(tg_ready, 1)

            def feed(b, u):
                back, cur, ask, rows = turn_has(b, -1, 0, 1, 2)
                if back:
                    hidden_turned(b - 1)
                if ask:
                    gate_tanh(b + 1, 1 - u)
                if cur:
                    act.wait_ge(hscale_ready, b + 1)
                    nc.scalar.activation(HG[:, u, :], HG[:, u, :], ACT.Identity, scale=hscale[:, u, 1:2],
                                         bias=magic[:, 0:1]).then_inc(hround_ready, 1)
                    act.wait_ge(hround_ready, b + 1)
                    nc.scalar.activation(HQ[:, :], HG[:, u, :], ACT.Identity,
                                         bias=magic[:, 1:2]).then_inc(hq_ready, 1)
                if rows:
                    rows_turned(b + 2, u)

            for b in range(-2, 2):
                feed(b, b % 2)
            with act.Fori(1, B // 2 - 1) as i:
                for u in range(2):
                    feed(i * 2 + u, u)
            for b in range(B - 2, B + 1):
                feed(b, b % 2)

        @block.gpsimd
        def _(pool):
            ch = Chain(pool, pool_own)
            half = DC // 2
            cos = CO[:, C_COS:C_COS + DC]
            sin = CO[:, C_SIN:C_SIN + DC]
            pool.wait_ge(ld_const, 16)
            pool.wait_ge(ld_ctx, 16)
            tmp = cT[:, :, :].rearrange("p q n -> p (q n)").rearrange("p (b c) -> p b c", b=B)
            nc.gpsimd.tensor_tensor(KR[:, :, :], CT[:, :, :], cos.unsqueeze(1).to_broadcast([128, B, DC]), ALU.mult)
            nc.gpsimd.tensor_tensor(tmp[:, :, 0:half], CT[:, :, half:DC],
                                    sin[:, 0:half].unsqueeze(1).to_broadcast([128, B, half]), ALU.mult)
            ch.link(nc.gpsimd.tensor_tensor(tmp[:, :, half:DC], CT[:, :, 0:half],
                                            sin[:, half:DC].unsqueeze(1).to_broadcast([128, B, half]), ALU.mult))
            ch.link(nc.gpsimd.tensor_tensor(KR[:, :, :], KR[:, :, :], tmp, ALU.add))
            pool.wait_ge(setup_done, 1)

            nc.gpsimd.memset(V1[:, :, :, :], 1.0)
            ch.link(nc.gpsimd.tensor_copy(CB[0][:, :, :], CT[:, :, :]))
            ch.link(nc.gpsimd.tensor_tensor(CRST[:, :, :], CT[:, :, :], CB[0][:, :, :], ALU.subtract))
            ch.link(nc.gpsimd.tensor_copy(CB[1][:, :, :], CRST[:, :, :]))
            ins = nc.gpsimd.tensor_tensor(CB[2][:, :, :], CRST[:, :, :], CB[1][:, :, :], ALU.subtract)
            ins.then_inc(parts_ready, 1)
            pool.wait_ge(parts_ready, 1)

            def root(b, u):
                pool.wait_ge(var_ready, b + 1)
                nc.gpsimd.tensor_tensor(rstd[:, u, :], veps[:, u, :], negroot[:, :], ALU.pow).then_inc(rstd_ready, 1)

            def keys(b, u):
                for k in range(2):
                    ins = nc.gpsimd.tensor_copy(KD[:, u, k, :], KR[:, b, :])
                ins.then_inc(kd_ready, 1)

            def scatter(b, u, half):
                if half == 0:
                    pool.wait_ge(idx_ready, b + 1)
                    since(pool, scattered[u], b * 64 - 64 * u)
                    hold(pool)
                    nc.gpsimd.tensor_copy(tok[:, u, :], TOK[:, bass.ds(b, 1)])
                    ch.link(nc.gpsimd.tensor_copy(where[:, u, :], IDX[:, b, :]))
                    hold(pool)
                for k in range(TOPK // 2 * half, TOPK // 2 * (half + 1)):
                    nc.gpsimd.indirect_dma_start(
                        slots, bass.IndirectOffsetOnAxis(ap=where[:, u, k:k + 1], axis=0), tok[:, u, :], None,
                        bounds_check=E * CAP - 1, oob_is_err=False).then_inc(scattered[u], 16)

            def attend(b, u):
                added, first, cur, placing, placed = turn_has(b, -2, 3, 0, -3, -4)
                if added:
                    pool.wait_ge(var2_ready, b - 1)
                    nc.gpsimd.tensor_tensor(rstd[:, 2, :], veps[:, 2, :], negroot[:, :],
                                            ALU.pow).then_inc(rstd2_ready, 1)
                if first:
                    root(b + 3, 1 - u)
                    since(pool, kdT_psum, b + 2)
                    hold(pool)
                    keys(b + 3, 1 - u)
                if cur:
                    since(pool, att_psum, b - 1)
                    hold(pool)
                    nc.gpsimd.tensor_copy(VD[:, u, :], KR[:, b, :]).then_inc(vd_ready, 1)
                if placed:
                    scatter(b - 4, u, 1)
                if placing:
                    scatter(b - 3, 1 - u, 0)

            nc.gpsimd.iota(TOK[:, :], [[S, B]], base=0, channel_multiplier=1)
            for b in range(-3, 2):
                attend(b, b % 2)
            pool.wait_ge(cleared, 16)
            for b in range(2, 4):
                attend(b, b % 2)
            with pool.Fori(2, B // 2 - 2) as i:
                ch.enter(i - 2, 2)
                for u in range(2):
                    attend(i * 2 + u, u)
                ch.leave(B // 2 - 4)
            for b in range(B - 4, B + 4):
                attend(b, b % 2)

            pool.wait_ge(gi_ready, 16)
            pool.wait_ge(row_stored[0], B // 2 * 16)
            pool.wait_ge(row_stored[1], B // 2 * 16)

            def gather(i, v):
                j = i * RING + v
                if not isinstance(i, int):
                    pool.wait_ge(xg_psum, j + 1 - RING)
                    pool.wait_ge(h_ready, j + 1 - RING)
                    hold(pool)
                ch.link(nc.gpsimd.tensor_copy(gidx[:, v, :], GI[:, bass.ds(j, 1)]))
                hold(pool)
                nc.gpsimd.indirect_dma_start(
                    XG[:, v, :], None, routed, bass.IndirectOffsetOnAxis(ap=gidx[:, v, :], axis=0),
                    bounds_check=B * S - 1, oob_is_err=False).then_inc(gathered[v], 16)

            def keys1(b):
                for part, slots in ((0, slice(0, 3)), (1, slice(3, 5)), (2, slice(5, 6))):
                    for k in range(2):
                        n = slots.stop - slots.start
                        ins = nc.gpsimd.tensor_copy(
                            KZ[:, b, :, 2 * k, slots, :],
                            CB[part][:, b, :].rearrange("p (j k d) -> p j k d", j=4, k=2)[:, :, k, :]
                            .unsqueeze(2).to_broadcast([128, 4, n, DH]))
                ins.then_inc(kz_ready, 1)

            for v in range(RING):
                gather(0, v)
            pool.wait_ge(att_psum, B)
            nc.gpsimd.memset(KZ[:, :, :, 1, :, :].rearrange("p b j t d -> p (b j) (t d)"), 0.0)
            keys1(0)
            keys1(1)
            with pool.Fori(1, NPE // RING) as i:
                ch.enter(i - 1, RING)
                for v in range(RING):
                    gather(i, v)
                    if v % 2:
                        keys1(i * 2 + v // 2)
                ch.leave(NPE // RING - 1)

            pool.wait_ge(os_stored[0], NPE // 2 * 16)
            pool.wait_ge(os_stored[1], NPE // 2 * 16)
            pool.wait_ge(zero_stored, 16)

            def collect(b, u, choices=range(TOPK)):
                if 0 in choices:
                    since(pool, x2_ready, b - 1)
                    hold(pool)
                    ch.link(nc.gpsimd.tensor_copy(cidx[:, u, :], IDX[:, b, :]))
                    hold(pool)
                for k in choices:
                    nc.gpsimd.indirect_dma_start(
                        YG[:, u, k, :], None, moe, bass.IndirectOffsetOnAxis(ap=cidx[:, u, k:k + 1], axis=0),
                        bounds_check=E * CAP, oob_is_err=False).then_inc(yg_in[u], 16)

            def values1(b, u):
                since(pool, pv_psum, b * 2 - 2)
                hold(pool)
                nc.gpsimd.tensor_copy(V1[:, u, :, 0:DH],
                                      CT[:, b, :].rearrange("p (k d) -> p k d", k=KV)).then_inc(v1_ready, 1)

            def attend1(b, u):
                norm, rows, value = turn_has(b, 3, 5, 1)
                if norm:
                    root(b + (B + 3), 1 - u)
                if rows:
                    collect(b + 5, 1 - u)
                if value:
                    values1(b + 1, 1 - u)

            values1(0, 0)
            collect(0, 0)
            for b, before in ((0, 5), (1, 5), (2, 7)):
                collect(b + 1, (b + 1) % 2, range(before))
                root(b + B, b % 2)
                collect(b + 1, (b + 1) % 2, range(before, TOPK))
            collect(4, 0)
            for b in range(2):
                attend1(b, b % 2)
            with pool.Fori(1, B // 2 - 3) as i:
                ch.enter(i - 1, 2)
                for u in range(2):
                    attend1(i * 2 + u, u)
                ch.leave(B // 2 - 4)
            for b in range(B - 6, B):
                attend1(b, b % 2)

            def feed(b, u):
                cur, rows, more = turn_has(b, 0, 2, 3)
                xs, hs = xscale[:, u, :], hscale[:, u, :]
                if cur:
                    pool.wait_ge(hscale_ready, b + 1)
                    nc.gpsimd.tensor_tensor(hs[:, 2:3], hs[:, 0:1], wdeq[:, 2:3], ALU.mult).then_inc(hfactor_ready, 1)
                if rows:
                    pool.wait_ge(xmax_ready, b + 3)
                    nc.gpsimd.tensor_tensor(xs[:, 2:3], xs[:, 0:1], wdeq[:, 0:1], ALU.mult)
                    ch.link(nc.gpsimd.tensor_tensor(xs[:, 3:4], xs[:, 0:1], xs[:, 0:1], ALU.mult))
                    nc.gpsimd.tensor_tensor(xs[:, 3:4], xs[:, 3:4], wdeq[:, 1:2],
                                            ALU.mult).then_inc(xfactor_ready, 1)
                if more:
                    root(b + (2 * B + 3), 1 - u)

            for b in range(-3, 2):
                feed(b, b % 2)
            with pool.Fori(1, B // 2 - 2) as i:
                ch.enter(i - 1, 2)
                for u in range(2):
                    feed(i * 2 + u, u)
                ch.leave(B // 2 - 3)
            for b in range(B - 4, B):
                feed(b, b % 2)


def _constants():
    c = np.zeros((128, C_END), np.float32)
    r = np.arange(128)
    c[:, C_ID:C_ID + 128] = np.eye(128)
    c[:, C_UP:C_UP + 128] = r[:, None] < r[None, :]
    e = np.arange(E)
    c[:, C_ECODE:C_ECODE + E] = (e % 2) * CAP * NPE + e // 2 + 1
    inv = (1.0 / np.float32(10000.0) ** (np.arange(0, DC, 2, dtype=np.float32) / DC)).astype(np.float32)
    freqs = (np.arange(S, dtype=np.float32)[:, None] * inv[None, :]).astype(np.float32)
    sin, cos = np.repeat(np.sin(freqs), 2, -1), np.repeat(np.cos(freqs), 2, -1)
    sin[:, :DC // 2] *= -1
    c[:, C_COS:C_COS + DC] = cos
    c[:, C_SIN:C_SIN + DC] = sin
    for k in range(3):
        c[96 + k * KV:96 + k * KV + KV, C_KV:C_KV + KV] = np.eye(KV)
    return c


def _layout(i):
    wq = i["L0_xattn_Wq"].reshape(NP0, 2, K0, D).transpose(0, 2, 1, 3).reshape(NP0, K0, 2 * D)
    kv = i["L0_xattn_w_kc_kv"].reshape(NP0, 2, K0, DC).transpose(0, 2, 1, 3).reshape(NP0, K0, 2 * DC)
    wo = i["L0_xattn_Wo"].T.reshape(NP0, 2, K0, D).transpose(0, 2, 1, 3).reshape(NP0, K0, 2 * D)
    fold_a = np.concatenate([wq, kv, wo], -1)
    kq = i["L0_xattn_w_kc_q"].transpose(0, 2, 1).reshape(NP0, 2, 2, KC, K0)
    kq = kq.transpose(0, 3, 2, 1, 4).reshape(NP0, KC, 512)
    qr = i["L0_xattn_W_qr"].transpose(0, 2, 1).reshape(NP0, 128, CQ)
    kr = i["L0_xattn_W_kr"].transpose(0, 2, 1).reshape(NP0, 128, DC)
    fold_b = np.zeros((NP0, 128, 768), np.float32)
    fold_b[:, :KC, :512] = kq
    fold_b[:, :, 512:704] = qr
    fold_b[:, :, 704:] = kr
    gate_t = i["L0_ffn_gate_w"].T.reshape(2, 128, E).transpose(1, 0, 2)
    wg = i["L0_ffn_wg"].reshape(NPE, 2, 2, 128, FE)
    wu = i["L0_ffn_wu"].reshape(NPE, 2, 2, 128, FE)
    wgu = np.concatenate([wg, wu], -1).transpose(0, 3, 1, 2, 4)
    wd = i["L0_ffn_wd"].reshape(NPE, 2, FE, D).transpose(0, 2, 1, 3)
    w1 = np.concatenate([i["L1_ffn_w_gate"].T, i["L1_ffn_w_up"].T], -1).reshape(2, 128, 2 * F1).transpose(1, 0, 2)
    w2 = i["L1_ffn_w_down"].T
    c = np.ascontiguousarray
    return {"x": c(i["x"]), "ctx": c(i["ctx_512"]), "fold_a": c(fold_a), "fold_b": fold_b, "gate_t": c(gate_t),
            "wgu": c(wgu), "wd": c(wd), "w1": c(w1), "w2": c(w2), "consts": _constants()}


def kernel(**inputs):
    import concourse.bacc as bacc
    from concourse.bass_utils import run_bass_kernel_spmd as run

    nc = bacc.Bacc("TRN2", target_bir_lowering=False, num_devices=1)
    arrays = _layout({k: np.asarray(v) for k, v in inputs.items()})
    args = [nc.dram_tensor(n, a.shape, mybir.dt.from_np(a.dtype), kind="ExternalInput").ap()
            for n, a in arrays.items()]
    out = nc.dram_tensor("out", (B, S, D), fp32, kind="ExternalOutput").ap()
    build(nc, *args, out)
    return run(nc, [arrays], core_ids=[0]).results[0]["out"]
```
